# Optimizing a Trainium2 kernel written in Bass

```python
import numpy as np
import jax
import jax.numpy as jnp

def _softmax(x, axis=-1):
    return jax.nn.softmax(x, axis=axis)

def _gelu(x):
    return jax.nn.gelu(x, approximate=True)

def _silu(x):
    return jax.nn.silu(x)

def _sigmoid(x):
    return jax.nn.sigmoid(x)

def _layernorm(x, axis=-1, eps=1e-05):
    m = jnp.mean(x, axis=axis, keepdims=True)
    v = jnp.var(x, axis=axis, keepdims=True)
    return (x - m) / jnp.sqrt(v + eps)

def _scatter_add(tgt, idx, src, axis=0):
    return tgt.at[idx].add(src)

def _segment_sum(src, seg, n):
    return jax.ops.segment_sum(src, seg, n)
kernel_name = 'mk_adaln_d1_jaxref_r8_0d9c51'

def setup_inputs(seed: int=0):
    np.random.seed(seed)
    _w = jnp.asarray

    def _L0_attn_setup():
        import jax, jax.numpy as jnp
        import numpy as np
        B, S, D, H = (2, 256, 256, 16)
        HD = D // H

        def _alibi_slopes(num_heads):
            ratio = 2.0 ** (-8.0 / num_heads)
            return ratio ** jnp.arange(1, num_heads + 1, dtype=jnp.float32)
        key = jax.random.key(seed)
        ks = jax.random.split(key, 9)
        sd = 1.0 / np.sqrt(D)
        inp = {'x': jax.random.normal(ks[0], (B, S, D), dtype=jnp.float32)}
        for i, name in enumerate(['Wq', 'Wk', 'Wv', 'Wo']):
            inp[name] = jax.random.normal(ks[1 + i], (D, D), dtype=jnp.float32) * sd
        for i, name in enumerate(['bq', 'bk', 'bv', 'bo']):
            inp[name] = jax.random.normal(ks[5 + i], (D,), dtype=jnp.float32) * 0.02
        return inp
    _L0_attn_in = _L0_attn_setup()

    def _L0_ffn_setup():
        import jax, jax.numpy as jnp
        import numpy as np
        from jax import lax
        DIM = 256
        INTER = 176
        N_EXPERTS = 32
        TOP_K = 6
        N_SHARED = 2
        CAPACITY = 256
        ROUTE_SCALE = 1.0

        def _gate(xf, gate_w):
            logits = xf @ gate_w.T
            scores = jax.nn.softmax(logits.astype(jnp.float32), axis=-1)
            top_w, top_i = lax.top_k(scores, TOP_K)
            return ((top_w * ROUTE_SCALE).astype(xf.dtype), top_i)

        def _moe(xf, gate_w, w1, w2, w3):
            T, D = xf.shape
            E, CAP = (N_EXPERTS, CAPACITY)
            top_w, top_i = _gate(xf, gate_w)
            e_flat = top_i.reshape(-1)
            t_flat = jnp.repeat(jnp.arange(T), TOP_K)
            w_flat = top_w.reshape(-1)
            order = jnp.argsort(e_flat)
            e_s, t_s, w_s = (e_flat[order], t_flat[order], w_flat[order])
            counts = jnp.zeros((E,), jnp.int32).at[e_s].add(1)
            starts = jnp.concatenate([jnp.zeros((1,), jnp.int32), jnp.cumsum(counts)[:-1]])
            pos = jnp.arange(T * TOP_K, dtype=jnp.int32) - starts[e_s]
            valid = pos < CAP
            buf_idx = jnp.where(valid, e_s * CAP + pos, E * CAP)
            xbuf = jnp.zeros((E * CAP + 1, D), xf.dtype).at[buf_idx].set(xf[t_s])
            xb = xbuf[:E * CAP].reshape(E, CAP, D)
            h = jax.nn.silu(jnp.einsum('ecd,edi->eci', xb, w1)) * jnp.einsum('ecd,edi->eci', xb, w3)
            ob = jnp.einsum('eci,eid->ecd', h, w2).reshape(E * CAP, D)
            ob = jnp.concatenate([ob, jnp.zeros((1, D), ob.dtype)], axis=0)
            y_pairs = ob[buf_idx] * w_s[:, None]
            y = jnp.zeros((T, D), xf.dtype).at[t_s].add(y_pairs)
            return y
        key = jax.random.key(seed)
        ks = jax.random.split(key, 9)
        B, S = (4, 256)
        si = INTER * N_SHARED
        inputs = {'x': jax.random.normal(ks[0], (B, S, DIM), jnp.float32), 'gate_w': jax.random.normal(ks[1], (N_EXPERTS, DIM), jnp.float32), 'w1': jax.random.normal(ks[2], (N_EXPERTS, DIM, INTER), jnp.float32) * DIM ** (-0.5), 'w2': jax.random.normal(ks[3], (N_EXPERTS, INTER, DIM), jnp.float32) * INTER ** (-0.5), 'w3': jax.random.normal(ks[4], (N_EXPERTS, DIM, INTER), jnp.float32) * DIM ** (-0.5), 'sw1': jax.random.normal(ks[5], (DIM, si), jnp.float32) * DIM ** (-0.5), 'sw2': jax.random.normal(ks[6], (si, DIM), jnp.float32) * si ** (-0.5), 'sw3': jax.random.normal(ks[7], (DIM, si), jnp.float32) * DIM ** (-0.5)}
        return inputs
    _L0_ffn_in = _L0_ffn_setup()
    _L0_c = _w((lambda *s: np.random.randn(*s).astype(np.float32) * 0.05)(2, 256))
    _L0_wmod = _w((lambda *s: np.random.randn(*s).astype(np.float32) * 0.05)(256, 6 * 256) * 256 ** (-0.5))
    _d = {'L0_attn_x': _L0_attn_in['x'], 'L0_attn_Wq': _L0_attn_in['Wq'], 'L0_attn_bq': _L0_attn_in['bq'], 'L0_attn_Wk': _L0_attn_in['Wk'], 'L0_attn_bk': _L0_attn_in['bk'], 'L0_attn_Wv': _L0_attn_in['Wv'], 'L0_attn_bv': _L0_attn_in['bv'], 'L0_attn_Wo': _L0_attn_in['Wo'], 'L0_attn_bo': _L0_attn_in['bo'], 'L0_ffn_gate_w': _L0_ffn_in['gate_w'], 'L0_ffn_w1': _L0_ffn_in['w1'], 'L0_ffn_w2': _L0_ffn_in['w2'], 'L0_ffn_w3': _L0_ffn_in['w3'], 'L0_ffn_sw1': _L0_ffn_in['sw1'], 'L0_ffn_sw2': _L0_ffn_in['sw2'], 'L0_ffn_sw3': _L0_ffn_in['sw3'], 'L0_c': _L0_c, 'L0_wmod': _L0_wmod}
    _x0 = _d['L0_attn_x']
    _d['L0_attn_x'] = jax.random.normal(jax.random.fold_in(jax.random.key(seed), 1), (2, 1024, 256), dtype=_x0.dtype)
    del _x0
    return _d

def reference(L0_attn_x, L0_attn_Wq, L0_attn_bq, L0_attn_Wk, L0_attn_bk, L0_attn_Wv, L0_attn_bv, L0_attn_Wo, L0_attn_bo, L0_ffn_gate_w, L0_ffn_w1, L0_ffn_w2, L0_ffn_w3, L0_ffn_sw1, L0_ffn_sw2, L0_ffn_sw3, L0_c, L0_wmod):

    def _L0_attn_ref(x, Wq, bq, Wk, bk, Wv, bv, Wo, bo):
        import jax, jax.numpy as jnp
        import numpy as np
        B, S, D, H = (2, 256, 256, 16)
        HD = D // H

        def _alibi_slopes(num_heads):
            ratio = 2.0 ** (-8.0 / num_heads)
            return ratio ** jnp.arange(1, num_heads + 1, dtype=jnp.float32)
        b, s, d = x.shape

        def proj(W, bias):
            return (x @ W + bias).reshape(b, s, H, HD).transpose(0, 2, 1, 3)
        q, k, v = (proj(Wq, bq), proj(Wk, bk), proj(Wv, bv))
        scores = jnp.einsum('bhqd,bhkd->bhqk', q, k) / jnp.sqrt(jnp.float32(HD))
        distances = jnp.arange(1 - s, 1, dtype=jnp.float32)
        bias = _alibi_slopes(H)[None, :, None, None] * distances[None, None, None, :]
        scores = scores + bias
        causal = jnp.tril(jnp.ones((s, s), dtype=bool))[None, None]
        scores = jnp.where(causal, scores, jnp.finfo(scores.dtype).min)
        attn = jax.nn.softmax(scores, axis=-1)
        ctx = jnp.einsum('bhqk,bhkd->bhqd', attn, v)
        ctx = ctx.transpose(0, 2, 1, 3).reshape(b, s, d)
        return ctx @ Wo + bo

    def _L0_ffn_ref(x, gate_w, w1, w2, w3, sw1, sw2, sw3):
        import jax, jax.numpy as jnp
        import numpy as np
        from jax import lax
        DIM = 256
        INTER = 176
        N_EXPERTS = 32
        TOP_K = 6
        N_SHARED = 2
        CAPACITY = 256
        ROUTE_SCALE = 1.0

        def _gate(xf, gate_w):
            logits = xf @ gate_w.T
            scores = jax.nn.softmax(logits.astype(jnp.float32), axis=-1)
            top_w, top_i = lax.top_k(scores, TOP_K)
            return ((top_w * ROUTE_SCALE).astype(xf.dtype), top_i)

        def _moe(xf, gate_w, w1, w2, w3):
            T, D = xf.shape
            E, CAP = (N_EXPERTS, CAPACITY)
            top_w, top_i = _gate(xf, gate_w)
            e_flat = top_i.reshape(-1)
            t_flat = jnp.repeat(jnp.arange(T), TOP_K)
            w_flat = top_w.reshape(-1)
            order = jnp.argsort(e_flat)
            e_s, t_s, w_s = (e_flat[order], t_flat[order], w_flat[order])
            counts = jnp.zeros((E,), jnp.int32).at[e_s].add(1)
            starts = jnp.concatenate([jnp.zeros((1,), jnp.int32), jnp.cumsum(counts)[:-1]])
            pos = jnp.arange(T * TOP_K, dtype=jnp.int32) - starts[e_s]
            valid = pos < CAP
            buf_idx = jnp.where(valid, e_s * CAP + pos, E * CAP)
            xbuf = jnp.zeros((E * CAP + 1, D), xf.dtype).at[buf_idx].set(xf[t_s])
            xb = xbuf[:E * CAP].reshape(E, CAP, D)
            h = jax.nn.silu(jnp.einsum('ecd,edi->eci', xb, w1)) * jnp.einsum('ecd,edi->eci', xb, w3)
            ob = jnp.einsum('eci,eid->ecd', h, w2).reshape(E * CAP, D)
            ob = jnp.concatenate([ob, jnp.zeros((1, D), ob.dtype)], axis=0)
            y_pairs = ob[buf_idx] * w_s[:, None]
            y = jnp.zeros((T, D), xf.dtype).at[t_s].add(y_pairs)
            return y
        shape = x.shape
        xf = x.reshape(-1, DIM)
        y = _moe(xf, gate_w, w1, w2, w3)
        shared = jax.nn.silu(xf @ sw1) * (xf @ sw3) @ sw2
        return (y + shared).reshape(shape)
    x = L0_attn_x
    mod = (_silu(L0_c) @ L0_wmod).reshape(L0_c.shape[0], 6, 1, -1)
    sa, ca, ga, sb, cb, gb = (mod[:, 0], mod[:, 1], mod[:, 2], mod[:, 3], mod[:, 4], mod[:, 5])
    ga = (2 * (ga >= 0) - 1) * jnp.maximum(jnp.abs(ga), 0.25)
    gb = (2 * (gb >= 0) - 1) * jnp.maximum(jnp.abs(gb), 0.25)
    h = _layernorm(x, axis=-1) * (1 + ca) + sa
    x = x + ga * _L0_attn_ref(h, L0_attn_Wq, L0_attn_bq, L0_attn_Wk, L0_attn_bk, L0_attn_Wv, L0_attn_bv, L0_attn_Wo, L0_attn_bo)
    h = _layernorm(x, axis=-1) * (1 + cb) + sb
    x = x + gb * _L0_ffn_ref(h, L0_ffn_gate_w, L0_ffn_w1, L0_ffn_w2, L0_ffn_w3, L0_ffn_sw1, L0_ffn_sw2, L0_ffn_sw3)
    return x

_drawn_inputs = setup_inputs


def setup_inputs(seed=0):
    import zlib

    import numpy as np

    out = dict(_drawn_inputs(seed))
    spreads = {}
    factors = {'L0_attn_bq': 36.038, 'L0_attn_bk': 64.0, 'L0_attn_bv': 6.486, 'L0_attn_bo': 6.523}
    for name, (base, spread) in spreads.items():
        noise = np.random.default_rng([zlib.crc32(name.encode()), seed]).standard_normal(out[name].shape)
        drawn = base * np.exp(spread * noise) if base else spread * noise
        out[name] = jnp.asarray(drawn.astype(out[name].dtype))
    for name, factor in factors.items():
        out[name] = (out[name] * factor).astype(out[name].dtype)
    return out
```

```python
from contextlib import ExitStack

import numpy as np

import concourse.bass as bass
from concourse import mybir

F32 = mybir.dt.float32
BF16 = mybir.dt.bfloat16
U32 = mybir.dt.uint32
ALU = mybir.AluOpType
ACT = mybir.ActivationFunctionType
AX = mybir.AxisListType

P = 128
B, S, D = 2, 1024, 256
T = B * S
NT = T // P
BLK = 512
NB = T // BLK
TPB = BLK // P
H, HD = 16, 16
HG = 4
NG = H // HG
DC = D // P
E, TOPK, CAP, INTER = 32, 6, 256, 176
IB = INTER - P
SI = 2 * INTER
SM = [(0, 128), (128, 128), (256, SI - 256)]
NMOD = 6
NEG = -1.0e30
EPS = 1e-5
MIN_GATE = 0.25
Q_SCALE = float(HD) ** -0.5
VW = HD + 1
QPARTS = (0, 0, 1, 1, 0, 2)
KPARTS = (0, 1, 0, 1, 2, 0)
NPROD = len(QPARTS)
ROW_ALIBI = NPROD * HD
ROW_NMAX = ROW_ALIBI + 3
K_MAX = ROW_NMAX
K_EXP = ROW_NMAX + 2
SLOTS = E * CAP
SPT = SLOTS // P
SPE = CAP // P
RING = 4
COL_B = 2 * P
W13 = COL_B + 64 + IB
S_RING, M_RING, STACKS, VRING = 3, 2, 3, 3

UNITS = [(b, qb, g) for b in range(B) for qb in range(S // BLK) for g in range(NG)]
NU = len(UNITS)


def merge(*lists):
    at = sorted(((i + 1) / len(x), n, i) for n, x in enumerate(lists) for i in range(len(x)))
    return [lists[n][i] for _, n, i in at]


def plan():

    def maxes(u):
        return [("max", u, qt, hl, half) for qt in range(TPB) for hl in range(HG) for half in range(UNITS[u][1] + 1)]

    def exps(u):
        n, out = TPB * (UNITS[u][1] + 1), []
        for kt in range(n + 1):
            if kt < n:
                out += [("qk", u, kt, hl) for hl in range(HG)]
            if kt:
                out.append(("pv", u, kt - 1))
        return out

    def normed(tb):
        return [("ln", tb, pr) for pr in range(2)] + [("resid", tb)]

    def project(tb):
        return [("qkp", tb, s, c) for c in range(DC) for s in range(2)] + [("vp", tb, pr) for pr in range(2)]

    def close_x(tb):
        return [("ctxT", tb, 0), ("ctxT", tb, 1), ("wo", tb, 0), ("wo", tb, 1), ("ln2", tb)]

    def close_h(tb):
        return [("h2T", tb, 0), ("h2T", tb, 1), ("gate", tb)]

    def close_r(tb):
        return [("route", tb), ("pos", tb)]

    def shared(tb):
        return [("su", tb, m) for m in range(len(SM))] + [("sd", tb, pr) for pr in range(2)]

    items = [("stat", 0), ("mod",)] + normed(0) + project(0) + [("stk", 0), ("stk", 1)]
    items += [("stat", t) for t in range(1, NB)] + maxes(0) + [("nmax", 0)]
    for u in range(NU):
        tb, step, extra = u // NG, u % NG, []
        if u == 0:
            extra += [("row", b, k) for b in range(B) for k in range(2)] + [("wog",)]
        if step == 0 and tb:
            extra += close_x(tb - 1)
        if step == 1:
            extra += (close_h(tb - 1) if tb else []) + (normed(tb + 1) if tb + 1 < NB else [])
        if step == 2:
            extra += (close_r(tb - 1) if tb else []) + (project(tb + 1) if tb + 1 < NB else [])
        if u + 2 < NU:
            extra.append(("stk", u + 2))
        ex = exps(u)
        if u + 1 < NU:
            cut = (len(ex) * 3) // 4
            items += merge(ex[:cut], maxes(u + 1), extra) + [("nmax", u + 1)] + ex[cut:]
        else:
            items += ex
        items.append(("ctx", u))
    s0, x, last = shared(0), close_x(NB - 1), NB - 1
    items += [("free",)] + x[:2] + s0[:1] + x[2:4] + s0[1:2] + x[4:] + s0[2:] + close_h(last) + shared(1)
    items += close_r(last) + shared(2) + shared(3)
    return items


def load_expert(sp, e, w1, w3, w2, w13_slot, w2_slot, loaded):
    w13 = w13_slot[:, 0:DC * W13].rearrange("p (c n) -> p c n", c=DC)
    for w, k in ((w1, 0), (w3, 1)):
        src = w[bass.ds(e, 1)].rearrange("e (c p) i -> p (e c) i", p=P)
        sp.dma_start(w13[:, :, P * k:P * (k + 1)], src[:, :, 0:P]).then_inc(loaded, 16)
        sp.dma_start(w13[:, :, COL_B + 64 * k:COL_B + 64 * k + IB], src[:, :, P:INTER]).then_inc(loaded, 16)
    sp.dma_start(w2_slot[:, 0, :], w2[bass.ds(e, 1), 0:P, :].rearrange("e p d -> (e p) d")).then_inc(loaded, 16)
    sp.dma_start(w2_slot[0:IB, 1, :], w2[bass.ds(e, 1), P:INTER, :].rearrange("e p d -> (e p) d")).then_inc(loaded, 16)


LOADS_PER_EXPERT = 6


def adaln_kernel(nc, x, Wq, bq, Wk, bk, Wv, bv, Wo, bo, gate_w, w1, w2, w3, sw1, sw2, sw3, c_in, wmod,
                 alibi, ones_rows, zero_row, masks, ident_in, tri_in, iota_in, tok_in, slot_init, out):
    ITEMS = plan()
    ORD, total = {}, {}
    for it in ITEMS:
        ORD[it] = total.get(it[0], 0)
        total[it[0]] = ORD[it] + 1
    VAR = {it: n for n, it in enumerate(i for i in ITEMS if i[0] in ("stat", "ln2"))}
    READER = {"ln": "A", "qkp": "A", "vp": "D", "nmax": "A", "ctx": "D", "ctxT": "A", "wo": "D",
              "h2T": "A", "gate": "D", "pos": "D", "row": "D"}
    jobs = []
    for it in ITEMS:
        if it[0] == "mod":
            jobs += [("cT", "D"), ("gwT", "D"), ("modT", "D")]
        if it[0] in READER:
            jobs.append((it, READER[it[0]]))
    JOB = {n: j for j, (n, _) in enumerate(jobs)}
    seen, READ = {"A": 0, "D": 0}, []
    for _, r in jobs:
        seen[r] += 1
        READ.append((r, seen[r]))

    def upto(kind, accepts):
        return max(ORD[it] + 1 for it in ITEMS if it[0] == kind and accepts(it))

    def key_block(u, kt):
        return 2 * UNITS[u][0] + kt // TPB

    def diagonal(u, kt):
        j = kt - TPB * UNITS[u][1]
        return (j * P, True) if j >= 0 else (0, False)

    ctx = ExitStack()
    with ctx:
        def sb(name, shape, dt=F32):
            return ctx.enter_context(nc.sbuf_tensor(name, shape, dt))

        def sem(name):
            return ctx.enter_context(nc.semaphore(name))

        q_parts = [nc.dram_tensor(f"q_parts{i}", [3, D, S], BF16, kind="Internal").ap() for i in range(B)]
        k_parts = [nc.dram_tensor(f"k_parts{i}", [3, D, S], BF16, kind="Internal").ap() for i in range(B)]
        h2_rows = nc.dram_tensor("h2_rows", [T + CAP, D], F32, kind="Internal").ap()
        y_rows = nc.dram_tensor("y_rows", [T + CAP, D], F32, kind="Internal").ap()
        slot_table = nc.dram_tensor("slot_table", [SLOTS, 2], F32, kind="Internal").ap()

        bank = [ctx.enter_context(nc.psum_tensor(f"bank{i}", [P, 512], F32)) for i in range(8)]
        s_bank, m_bank, pv_bank, job_bank = bank[0:3], bank[3:5], bank[5], bank[6:8]

        ident = sb("ident", [P, P])
        identb = sb("identb", [P, P], BF16)
        mask_qk = sb("mask_qk", [P, 2, P], BF16)
        tri = sb("tri", [P, 2, P], BF16)
        iota_e = sb("iota_e", [P, E])
        tok_id = sb("tok_id", [P, NT])
        neg_half = sb("neg_half", [P, TPB])
        zero_b = sb("zero_b", [P, BLK], BF16)
        wo_sb = sb("wo_sb", [P, DC, D])
        wo_g = sb("wo_g", [P, B, DC, D])
        bqk = sb("bqk", [P, 2, DC])
        bq_s = sb("bq_s", [P, DC])
        bv_row, bo_row = sb("bv_row", [P, D]), sb("bo_row", [P, D])
        gw_in = sb("gw_in", [E, D])
        gwT = sb("gwT", [P, DC, E])
        c_sb, c_exp_sb, c_den, c_rec, c_act = (sb(n, [B, D]) for n in ("c_sb", "c_exp_sb", "c_den", "c_rec", "c_act"))
        cT = sb("cT", [P, DC, B])
        sa, ca1 = sb("sa", [P, DC, B]), sb("ca1", [P, DC, B])
        ga, sb_row, cb1, gb, ga_bo = (sb(n, [P, B, D]) for n in ("ga", "sb_row", "cb1", "gb", "ga_bo"))
        sign2, sign, mag = (sb(n, [P, D]) for n in ("sign2", "sign", "mag"))
        x_sb = sb("x_sb", [P, NT, D])
        stats = sb("stats", [P, TPB, 6])
        mv, mv2 = sb("mv", [P, NT, 2]), sb("mv2", [P, NT, 2])
        var_e, rstd, rstd2 = sb("var_e", [P, NT]), sb("rstd", [P, NT]), sb("rstd2", [P, NT])
        ctx_tok = sb("ctx_tok", [P, TPB, D])
        ctxT = sb("ctxT", [P, 2, 2 * DC * P])
        h2 = sb("h2", [P, TPB, D])
        h2T = sb("h2T", [P, DC, T])
        lg, sc_exp, score = (sb(n, [P, TPB, E]) for n in ("lg", "sc_exp", "score"))
        nlmax, esum, rsum = (sb(n, [P, TPB]) for n in ("nlmax", "esum", "rsum"))
        top = sb("top", [P, TPB, 8])
        topi = sb("topi", [P, TPB, 8], U32)
        topf = sb("topf", [P, TPB, 8])
        onehot = sb("onehot", [P, TPB, TOPK, E])
        onepos = sb("onepos", [P, TPB, TOPK, E])
        member = sb("member", [P, TPB, E], BF16)
        before = sb("before", [P, NT + 1, E], BF16)
        posk, addr, upper = (sb(n, [P, TPB, TOPK]) for n in ("posk", "addr", "upper"))
        slot_ix = sb("slot_ix", [P, NB, TPB, TOPK], U32)
        payload = sb("payload", [P, NB, TPB, TOPK, 2])
        tab = sb("tab", [P, SPT, 2])
        tab_ix = sb("tab_ix", [P, SPT], U32)

        with ExitStack() as first:
            def sb1(name, shape, dt=F32):
                return first.enter_context(nc.sbuf_tensor(name, shape, dt))

            wq_sb, wk_sb, wv_sb = (sb1(n, [P, DC, D]) for n in ("wq_sb", "wk_sb", "wv_sb"))
            wm = sb1("wm", [P, DC, NMOD * D])
            c_rep = sb1("c_rep", [P, DC * B, P])
            hT = sb1("hT", [P, DC, BLK])
            xhat = sb1("xhat", [P, 2, 2, D])
            v32 = sb1("v32", [P, 2, BLK])
            res = sb1("res", [P, BLK])
            parts = sb1("parts", [P, 2, 3, BLK], BF16)
            q_stack = [sb1(f"q_stack{i}", [P, HG, BLK], BF16) for i in range(STACKS)]
            k_stack = [sb1(f"k_stack{i}", [P, HG, S], BF16) for i in range(STACKS)]
            v_aug = [sb1(f"v_aug{i}", [P, TPB, H, VW]) for i in range(VRING)]
            p_t = sb1("p_t", [P, 2, HG, BLK])
            rmax = sb1("rmax", [P, 2, TPB, HG])
            rmax1 = sb1("rmax1", [P, TPB, HG])
            nm = sb1("nm", [P, TPB, 2, HG], BF16)
            nmT = sb1("nmT", [2 * HG, 2, BLK], BF16)
            ctx_f = sb1("ctx_f", [P, BLK])
            ctx_r = sb1("ctx_r", [P, TPB, HG, 1])
        sw1_sb, sw3_sb = sb("sw1_sb", [P, DC, SI]), sb("sw3_sb", [P, DC, SI])
        sw2_sb = sb("sw2_sb", [P, len(SM), D])
        s_sig = sb("s_sig", [P, 2, BLK])
        s_hid = sb("s_hid", [P, 2, len(SM), BLK])
        y_init = sb("y_init", [P, 2, 2, D])
        w13_sb = [sb(f"w13_sb{i}", [P, DC * W13]) for i in range(RING)]
        w2_sb = [sb(f"w2_sb{i}", [P, 2, D]) for i in range(RING)]
        idx_st = [sb(f"idx_st{i}", [P, SPE], U32) for i in range(RING)]
        wt_st = [sb(f"wt_st{i}", [P, SPE]) for i in range(RING)]
        xg = [sb(f"xg{i}", [P, SPE, D]) for i in range(RING)]
        xgT = [sb(f"xgT{i}", [P, DC, CAP]) for i in range(2)]
        sigA, hidA = ([sb(f"{n}{i}", [P, CAP]) for i in range(2)] for n in ("sigA", "hidA"))
        sigB, hidB = ([sb(f"{n}{i}", [IB, CAP]) for i in range(2)] for n in ("sigB", "hidB"))
        ob = [sb(f"ob{i}", [P, SPE, D]) for i in range(2)]
        y_ld = sb("y_ld", [P, 2, TPB, D])

        l_x = [sem(f"l_x{i}") for i in range(NB)]
        l_const, l_c, l_wm, l_wqk, l_wvo, l_ones, l_init, l_sw, l_h2, l_scat, l_tab = (
            sem("l_" + n) for n in ("const", "c", "wm", "wqk", "wvo", "ones", "init", "sw", "h2", "scat", "tab"))
        l_parts, l_nm, l_y, l_yl, l_out = ([sem(f"l_{n}{i}") for i in range(2)] for n in ("parts", "nm", "y", "yl", "out"))
        l_stack = [sem(f"l_stack{i}") for i in range(STACKS)]
        e_w, e_x = ([sem(f"{n}{i}") for i in range(RING)] for n in ("e_w", "e_x"))
        e_added, pool_at = sem("e_added"), sem("pool_at")
        dve_chain, act_chain, pool_chain = sem("dve_chain"), sem("act_chain"), sem("pool_chain")
        job_full = sem("job_full")
        job_read = {"A": sem("job_read_act"), "D": sem("job_read_dve")}
        (set_up, c_exped, c_acted, wo_scaled, var_set, rstd_set, xhat_set, resid_set, parts_first, parts_set,
         max_full, max_read, nm_set, score_full, exp_done, pv_done, ctxf_set, h2_set, nlmax_set, sexp_set,
         member_set, slots_set, su_full, sig_set, hid_set, sd_full, y_set, tabix_set, pads_set) = (sem(n) for n in (
             "set_up", "c_exped", "c_acted", "wo_scaled", "var_set", "rstd_set", "xhat_set", "resid_set", "parts_first",
             "parts_set", "max_full", "max_read", "nm_set", "score_full", "exp_done", "pv_done", "ctxf_set",
             "h2_set", "nlmax_set", "sexp_set", "member_set", "slots_set", "su_full", "sig_set", "hid_set",
             "sd_full", "y_set", "tabix_set", "pads_set"))
        e_staged, e_turned, e_xT, e_up, e_sig, e_hid, e_down, e_ob = (sem(n) for n in (
            "e_staged", "e_turned", "e_xT", "e_up", "e_sig", "e_hid", "e_down", "e_ob"))
        y_scaled, out_set = sem("y_scaled"), sem("out_set")
        N_CONST = 12

        block = ctx.enter_context(nc.Block())

        def wait_read(eng, name):
            r, n = READ[JOB[name]]
            eng.wait_ge(job_read[r], n)

        def wait_full(eng, name):
            eng.wait_ge(job_full, JOB[name] + 1)

        def parts_of(unit):
            return (parts_first, unit + 1) if unit < 4 else (parts_set, unit + 1 - 4)

        @block.sync
        def _(sp):
            with nc.allow_non_contiguous_dma(reason="biases by feature"):
                sp.dma_start(c_sb[:, :], c_in).then_inc(l_c, 16)
                sp.dma_start(x_sb[:, 0:TPB, :], x[0:BLK, :].rearrange("(t p) d -> p t d", p=P)).then_inc(l_x[0], 16)
                row = lambda v: v.rearrange("(a d) -> a d", a=1).to_broadcast([P, D])
                consts = ((ident[:, :], ident_in[0]), (gw_in[:, :], gate_w),
                          (bqk[:, 0, :], bq.rearrange("(c p) -> p c", p=P)),
                          (bqk[:, 1, :], bk.rearrange("(c p) -> p c", p=P)),
                          (identb[:, :], masks[2]), (mask_qk[:, 0, :], masks[0]), (mask_qk[:, 1, :], masks[1]),
                          (tri[:, :, :], tri_in), (iota_e[:, :], iota_in), (tok_id[:, :], tok_in),
                          (bv_row[:, :], row(bv)), (bo_row[:, :], row(bo)))
                assert len(consts) == N_CONST
                for dst, src in consts:
                    sp.dma_start(dst, src).then_inc(l_const, 16)
            sp.dma_start(wm[:, :, :], wmod.rearrange("(c p) n -> p c n", p=P)).then_inc(l_wm, 16)
            for w, src, s in ((wq_sb, Wq, l_wqk), (wk_sb, Wk, l_wqk), (wv_sb, Wv, l_wvo), (wo_sb, Wo, l_wvo)):
                sp.dma_start(w[:, :, :], src.rearrange("(c p) n -> p c n", p=P)).then_inc(s, 16)
            for i in range(STACKS):
                sp.dma_start(q_stack[i][ROW_ALIBI:ROW_NMAX, :, :], ones_rows[0:3, :, 0:BLK]).then_inc(l_ones, 16)
                sp.dma_start(k_stack[i][ROW_NMAX:K_EXP, :, :], ones_rows[0:2]).then_inc(l_ones, 16)
            for tb in range(1, NB):
                sp.dma_start(x_sb[:, TPB * tb:TPB * (tb + 1), :],
                             x[BLK * tb:BLK * (tb + 1), :].rearrange("(t p) d -> p t d", p=P)).then_inc(l_x[tb], 16)
            sp.dma_start(slot_table, slot_init).then_inc(l_init, 16)
            sp.dma_start(h2_rows[T:T + CAP, :], zero_row.to_broadcast([CAP, D])).then_inc(l_init, 16)
            sp.dma_start(y_rows[T:T + CAP, :], zero_row.to_broadcast([CAP, D])).then_inc(l_init, 16)
            for it in ITEMS:
                kind = it[0]
                if kind == "qkp":
                    _, tb, side, c = it
                    n = ORD[it]
                    sp.wait_ge(*parts_of(n))
                    dst = (q_parts, k_parts)[side][tb // 2][:, c * P:(c + 1) * P, (tb % 2) * BLK:(tb % 2 + 1) * BLK]
                    sp.dma_start(dst.rearrange("j p t -> p j t"), parts[:, n % 2, :, :]).then_inc(l_parts[n % 2], 16)
                if kind == "stk":
                    u = it[1]
                    b, qb, g = UNITS[u]
                    s_, rows = l_stack[u % STACKS], slice(HG * HD * g, HG * HD * (g + 1))
                    for i in range(2):
                        sp.wait_ge(l_parts[i], 16 * 2 * (u // NG + 1))
                    if u >= STACKS:
                        sp.wait_ge(score_full, upto("qk", lambda i: i[1] == u - STACKS))
                    keys = BLK * (qb + 1)
                    for j in range(NPROD):
                        sp.dma_start(q_stack[u % STACKS][HD * j:HD * (j + 1), :, :],
                                     q_parts[b][QPARTS[j], rows, BLK * qb:BLK * (qb + 1)]
                                     .rearrange("(h d) t -> d h t", d=HD)).then_inc(s_, 16)
                        sp.dma_start(k_stack[u % STACKS][HD * j:HD * (j + 1), :, 0:keys],
                                     k_parts[b][KPARTS[j], rows, 0:keys]
                                     .rearrange("(h d) t -> d h t", d=HD)).then_inc(s_, 16)
                    sp.dma_start(k_stack[u % STACKS][ROW_ALIBI:ROW_NMAX, :, 0:keys],
                                 alibi[:, HG * g:HG * (g + 1), 0:keys]).then_inc(s_, 16)
                if kind == "nmax":
                    u = it[1]
                    wait_read(sp, it)
                    for part in range(2):
                        sp.dma_start(q_stack[u % STACKS][ROW_NMAX + part:ROW_NMAX + part + 1, :, :],
                                     nmT[HG * part:HG * (part + 1), u % 2, :]).then_inc(l_nm[u % 2], 16)
                if kind == "ln2":
                    tb = it[1]
                    sp.wait_ge(h2_set, tb + 1)
                    sp.dma_start(h2_rows[BLK * tb:BLK * (tb + 1), :].rearrange("(t p) d -> p t d", p=P),
                                 h2[:, :, :]).then_inc(l_h2, 16)
                if kind == "free":
                    wait_read(sp, ("ctx", NU - 1))
                    sp.wait_ge(exp_done, total["qk"])
                    sp.wait_ge(wo_scaled, 1)
                    sp.dma_start(sw1_sb[:, :, :], sw1.rearrange("(c p) n -> p c n", p=P)).then_inc(l_sw, 16)
                    sp.dma_start(sw3_sb[:, :, :], sw3.rearrange("(c p) n -> p c n", p=P)).then_inc(l_sw, 16)
                    for m, (r0, rn) in enumerate(SM):
                        sp.dma_start(sw2_sb[0:rn, m, :], sw2[r0:r0 + rn, :]).then_inc(l_sw, 16)
                    for r in range(RING):
                        load_expert(sp, r, w1, w3, w2, w13_sb[r], w2_sb[r], e_w[r])
                if kind == "sd":
                    _, tb, pr = it
                    n, r0 = ORD[it], BLK * tb + 2 * P * pr
                    sp.wait_ge(y_set, n + 1)
                    sp.dma_start(y_rows[r0:r0 + 2 * P, :].rearrange("(t p) d -> p t d", p=P),
                                 y_init[:, n % 2, :, :]).then_inc(l_y[n % 2], 16)
            sp.wait_ge(l_scat, 16 * NT * TOPK)
            sp.dma_start(tab[:, :, :], slot_table.rearrange("(p j) n -> p j n", p=P)).then_inc(l_tab, 16)
            with sp.Fori(1, E // RING) as i:
                for r in range(RING):
                    sp.wait_ge(e_down, (i - 1) * RING + r + 1)
                    load_expert(sp, i * RING + r, w1, w3, w2, w13_sb[r], w2_sb[r], e_w[r])
            sp.wait_ge(e_added, 16 * SPE * E)
            for tb in range(NB):
                if tb >= 2:
                    sp.wait_ge(out_set, tb - 1)
                    sp.dma_start(out[BLK * (tb - 2):BLK * (tb - 1), :].rearrange("(t p) d -> p t d", p=P),
                                 y_ld[:, tb % 2, :, :]).then_inc(l_out[tb % 2], 16)
                    sp.wait_ge(l_out[tb % 2], 16)
                sp.dma_start(y_ld[:, tb % 2, :, :],
                             y_rows[BLK * tb:BLK * (tb + 1), :].rearrange("(t p) d -> p t d", p=P)).then_inc(l_yl[tb % 2], 16)
            for tb in range(NB - 2, NB):
                sp.wait_ge(out_set, tb + 1)
                sp.dma_start(out[BLK * tb:BLK * (tb + 1), :].rearrange("(t p) d -> p t d", p=P),
                             y_ld[:, tb % 2, :, :]).then_inc(l_out[tb % 2], 16)
            for i in range(2):
                sp.wait_ge(l_out[i], 16 * NB // 2)

        @block.tensor
        def _(pe):
            def begin(name):
                j = JOB[name]
                if j >= 2:
                    r, n = READ[j - 2]
                    pe.wait_ge(job_read[r], n)
                return job_bank[j % 2]

            pe.wait_ge(set_up, 1)
            pe.wait_ge(l_const, 16 * N_CONST)
            pe.matmul(pv_bank[:, :], identb[:, :], zero_b[:, :], start=True, stop=True)
            for it in ITEMS:
                kind = it[0]
                if kind == "mod":
                    jb = begin("cT")
                    pe.wait_ge(c_acted, 1)
                    for c in range(DC):
                        ins = pe.transpose(jb[:, B * c:B * (c + 1)], c_act[:, c * P:(c + 1) * P], ident[0:B, 0:B])
                    ins.then_inc(job_full, 1)
                    jb = begin("gwT")
                    for c in range(DC):
                        ins = pe.transpose(jb[:, E * c:E * (c + 1)], gw_in[:, c * P:(c + 1) * P], ident[0:E, 0:E])
                    ins.then_inc(job_full, 1)
                    jb = begin("modT")
                    wait_read(pe, "cT")
                    pe.wait_ge(l_wm, 16)
                    for q in range(2 * DC):
                        for c in range(DC):
                            ins = pe.matmul(jb[:, B * q:B * (q + 1)], wm[:, c, q * P:(q + 1) * P], cT[:, c, :],
                                            start=(c == 0), stop=(c == DC - 1))
                    ins.then_inc(job_full, 1)
                elif kind == "row":
                    _, b, k = it
                    jb = begin(it)
                    for c in range(DC):
                        ins = pe.matmul(jb[:, :], c_rep[:, c * B + b, :], wm[:, c, 2 * D * (k + 1):2 * D * (k + 2)],
                                        start=(c == 0), stop=(c == DC - 1))
                    ins.then_inc(job_full, 1)
                elif kind == "ln":
                    _, tb, pr = it
                    jb = begin(it)
                    pe.wait_ge(xhat_set, ORD[it] + 1)
                    for c in range(DC):
                        for i in range(2):
                            ins = pe.transpose(jb[:, (2 * c + i) * P:(2 * c + i + 1) * P],
                                               xhat[:, ORD[it] % 2, i, c * P:(c + 1) * P], ident[:, :])
                    ins.then_inc(job_full, 1)
                elif kind == "qkp":
                    _, tb, side, co = it
                    jb = begin(it)
                    wait_read(pe, ("ln", tb, 1))
                    pe.wait_ge(l_wqk, 32)
                    for c in range(DC):
                        ins = pe.matmul(jb[:, :], (wq_sb, wk_sb)[side][:, c, co * P:(co + 1) * P], hT[:, c, :],
                                        start=(c == 0), stop=(c == DC - 1))
                    ins.then_inc(job_full, 1)
                elif kind == "vp":
                    _, tb, pr = it
                    jb = begin(it)
                    pe.wait_ge(l_wvo, 32)
                    for i in range(2):
                        for c in range(DC):
                            ins = pe.matmul(jb[:, D * i:D * (i + 1)], hT[:, c, (2 * pr + i) * P:(2 * pr + i + 1) * P],
                                            wv_sb[:, c, :], start=(c == 0), stop=(c == DC - 1))
                    ins.then_inc(job_full, 1)
                elif kind == "max":
                    _, u, qt, hl, half = it
                    n, mb, ring = ORD[it], m_bank[ORD[it] % M_RING], u % STACKS
                    crossed = half == UNITS[u][1]
                    w = (qt + 1) * P if crossed else BLK
                    if (qt, hl, half) == (0, 0, 0):
                        pe.wait_ge(l_stack[ring], 16 * (2 * NPROD + 1) * (u // STACKS + 1))
                        pe.wait_ge(l_ones, 32 * STACKS)
                    if n >= M_RING:
                        pe.wait_ge(max_read, n - M_RING + 1)
                    ins = pe.matmul(mb[:, 0:w], q_stack[ring][0:K_MAX, hl, qt * P:(qt + 1) * P],
                                    k_stack[ring][0:K_MAX, hl, half * BLK:half * BLK + w], start=True, stop=not crossed)
                    if crossed:
                        ins = pe.matmul(mb[:, w - P:w], identb[:, :], mask_qk[:, 0, :], start=False, stop=True)
                    ins.then_inc(max_full, 1)
                elif kind == "nmax":
                    jb = begin(it)[:, :].bitcast(BF16)
                    pe.wait_ge(nm_set, it[1] + 1)
                    for qt in range(TPB):
                        ins = pe.transpose(jb[0:2 * HG, qt * P:(qt + 1) * P],
                                           nm[:, qt, :, :].rearrange("p a h -> p (a h)"), identb[:, :])
                    ins.then_inc(job_full, 1)
                elif kind == "qk":
                    _, u, kt, hl = it
                    n, sbk, ring = ORD[it], s_bank[ORD[it] % S_RING], u % STACKS
                    q0, crossed = diagonal(u, kt)
                    if (kt, hl) == (0, 0):
                        pe.wait_ge(l_nm[u % 2], 32 * (u // 2 + 1))
                    if n >= S_RING:
                        pe.wait_ge(exp_done, n - S_RING + 1)
                    ins = pe.matmul(sbk[:, q0:BLK], k_stack[ring][0:K_EXP, hl, kt * P:(kt + 1) * P],
                                    q_stack[ring][0:K_EXP, hl, q0:BLK], start=True, stop=not crossed)
                    if crossed:
                        ins = pe.matmul(sbk[:, q0:q0 + P], identb[:, :], mask_qk[:, 1, :], start=False, stop=True)
                    ins.then_inc(score_full, 1)
                elif kind == "pv":
                    _, u, kt = it
                    m, kb = ORD[it], key_block(u, kt)
                    q0, _ = diagonal(u, kt)
                    pe.wait_ge(exp_done, HG * (m + 1))
                    if kt == 0:
                        wait_read(pe, ("vp", kb, 1))
                        if u:
                            pe.wait_ge(ctxf_set, u)
                    if kt == TPB:
                        wait_read(pe, ("vp", kb, 1))
                    last = kt == TPB * (UNITS[u][1] + 1) - 1
                    for hl in range(HG):
                        ins = pe.matmul(pv_bank[32 * hl:32 * hl + VW, q0:BLK],
                                        v_aug[kb % VRING][:, kt % TPB, HG * UNITS[u][2] + hl, :],
                                        p_t[:, m % 2, hl, q0:BLK], start=(kt == 0), stop=last)
                    ins.then_inc(pv_done, 1)
                elif kind == "ctx":
                    jb = begin(it)
                    pe.wait_ge(ctxf_set, it[1] + 1)
                    for qt in range(TPB):
                        ins = pe.transpose(jb[:, qt * P:(qt + 1) * P], ctx_f[:, qt * P:(qt + 1) * P], ident[:, :])
                    ins.then_inc(job_full, 1)
                elif kind == "ctxT":
                    _, tb, pr = it
                    jb = begin(it)
                    wait_read(pe, ("ctx", NG * tb + NG - 1))
                    for i in range(2):
                        for c in range(DC):
                            j = DC * i + c
                            ins = pe.transpose(jb[:, j * P:(j + 1) * P], ctx_tok[:, 2 * pr + i, c * P:(c + 1) * P], ident[:, :])
                    ins.then_inc(job_full, 1)
                elif kind == "wo":
                    _, tb, pr = it
                    jb = begin(it)
                    wait_read(pe, ("ctxT", tb, pr))
                    pe.wait_ge(wo_scaled, 1)
                    for i in range(2):
                        for c in range(DC):
                            j = DC * i + c
                            ins = pe.matmul(jb[:, D * i:D * (i + 1)], ctxT[:, pr, j * P:(j + 1) * P],
                                            wo_g[:, tb // 2, c, :], start=(c == 0), stop=(c == DC - 1))
                    ins.then_inc(job_full, 1)
                elif kind == "h2T":
                    _, tb, pr = it
                    jb = begin(it)
                    pe.wait_ge(h2_set, tb + 1)
                    for c in range(DC):
                        for i in range(2):
                            ins = pe.transpose(jb[:, (2 * c + i) * P:(2 * c + i + 1) * P],
                                               h2[:, 2 * pr + i, c * P:(c + 1) * P], ident[:, :])
                    ins.then_inc(job_full, 1)
                elif kind == "gate":
                    tb = it[1]
                    jb = begin(it)
                    wait_read(pe, ("h2T", tb, 1))
                    wait_read(pe, "gwT")
                    for i in range(TPB):
                        t0 = (TPB * tb + i) * P
                        for c in range(DC):
                            ins = pe.matmul(jb[:, E * i:E * (i + 1)], h2T[:, c, t0:t0 + P], gwT[:, c, :],
                                            start=(c == 0), stop=(c == DC - 1))
                    ins.then_inc(job_full, 1)
                elif kind == "pos":
                    tb = it[1]
                    jb = begin(it)
                    pe.wait_ge(member_set, tb + 1)
                    for i in range(TPB):
                        pe.matmul(jb[:, E * i:E * (i + 1)], tri[:, 0, :], member[:, i, :], start=True, stop=False)
                        ins = pe.matmul(jb[:, E * i:E * (i + 1)], tri[:, 1, :], before[:, TPB * tb + i, :],
                                        start=False, stop=True)
                    ins.then_inc(job_full, 1)
                elif kind == "su":
                    _, tb, m = it
                    n, (r0, rn) = ORD[it], SM[m]
                    if n == 0:
                        pe.wait_ge(l_sw, 16 * (2 + len(SM)))
                        pe.wait_ge(max_read, total["max"])
                    if m == 0:
                        wait_read(pe, ("h2T", tb, 1))
                    if n >= 2:
                        pe.wait_ge(hid_set, n - 1)
                    for w, k in ((sw1_sb, 0), (sw3_sb, 1)):
                        for c in range(DC):
                            ins = pe.matmul(bank[2 * (n % 2) + k][0:rn, :], w[:, c, r0:r0 + rn],
                                            h2T[:, c, BLK * tb:BLK * (tb + 1)], start=(c == 0), stop=(c == DC - 1))
                    ins.then_inc(su_full, 1)
                elif kind == "sd":
                    _, tb, pr = it
                    n = ORD[it]
                    pe.wait_ge(hid_set, len(SM) * (tb + 1))
                    if n >= 2:
                        pe.wait_ge(y_set, n - 1)
                    for i in range(2):
                        for m, (_, rn) in enumerate(SM):
                            ins = pe.matmul(bank[4 + n % 2][:, D * i:D * (i + 1)],
                                            s_hid[0:rn, tb % 2, m, (2 * pr + i) * P:(2 * pr + i + 1) * P],
                                            sw2_sb[0:rn, m, :], start=(m == 0), stop=(m == len(SM) - 1))
                    ins.then_inc(sd_full, 1)

            pe.wait_ge(pads_set, 1)
            pe.wait_ge(y_set, total["sd"])

            def turn(i, r):
                e = i * RING + r
                pe.wait_ge(e_x[r], 32 * i + 32)
                if not (isinstance(e, int) and e < 2):
                    pe.wait_ge(e_xT, e - 1)
                for c in range(DC):
                    for s in range(SPE):
                        ins = pe.transpose(bank[6 + r % 2][:, (SPE * c + s) * P:(SPE * c + s + 1) * P],
                                           xg[r][:, s, c * P:(c + 1) * P], ident[:, :])
                ins.then_inc(e_turned, 1)

            def up(i, r):
                e = i * RING + r
                pe.wait_ge(e_w[r], 16 * LOADS_PER_EXPERT * i + 16 * LOADS_PER_EXPERT)
                pe.wait_ge(e_xT, e + 1)
                if not (isinstance(e, int) and e < 2):
                    pe.wait_ge(e_hid, e - 1)
                a_bank, c_bank = bank[2 * (r % 2)], bank[2 * (r % 2) + 1]
                for k in range(2):
                    for c in range(DC):
                        w0 = c * W13 + k * P
                        pe.matmul(a_bank[:, CAP * k:CAP * (k + 1)], w13_sb[r][:, w0:w0 + P], xgT[r % 2][:, c, :],
                                  start=(c == 0), stop=(c == DC - 1))
                for c in range(DC):
                    w = w13_sb[r][:, c * W13 + COL_B:(c + 1) * W13]
                    ins = pe.matmul(c_bank[0:W13 - COL_B, 0:CAP], w, xgT[r % 2][:, c, :], start=(c == 0), stop=(c == DC - 1))
                ins.then_inc(e_up, 1)

            def down(i, r):
                e = i * RING + r
                pe.wait_ge(e_hid, e + 1)
                if not (isinstance(e, int) and e < 2):
                    pe.wait_ge(e_ob, e - 1)
                for s in range(SPE):
                    o = bank[4 + r % 2][:, D * s:D * (s + 1)]
                    pe.matmul(o, hidA[r % 2][:, s * P:(s + 1) * P], w2_sb[r][:, 0, :], start=True, stop=False)
                    ins = pe.matmul(o, hidB[r % 2][:, s * P:(s + 1) * P], w2_sb[r][0:IB, 1, :], start=False, stop=True)
                ins.then_inc(e_down, 1)

            turn(0, 0)

            def body(i, first=False, last=False):
                for r in range(RING):
                    if not (last and r == RING - 1):
                        turn(i + (r + 1) // RING, (r + 1) % RING)
                    up(i, r)
                    if not (first and r == 0):
                        down(i if r else i - 1, (r - 1) % RING)

            body(0, first=True)
            with pe.Fori(1, E // RING - 1) as i:
                body(i)
            body(E // RING - 1, last=True)
            down(E // RING - 1, RING - 1)

        @block.scalar
        def _(act):
            act.wait_ge(l_c, 16)
            act.activation(c_exp_sb[:, :], c_sb[:, :], ACT.Exp, scale=-1.0).then_inc(c_exped, 1)
            for it in ITEMS:
                kind = it[0]
                if kind == "ln":
                    _, tb, pr = it
                    wait_full(act, it)
                    wait_read(act, "modT")
                    if tb:
                        wait_full(act, ("vp", tb - 1, 1))
                    for c in range(DC):
                        ins = act.activation(hT[:, c, 2 * P * pr:2 * P * (pr + 1)],
                                             job_bank[JOB[it] % 2][:, 2 * P * c:2 * P * (c + 1)], ACT.Identity,
                                             bias=sa[:, c, tb // 2:tb // 2 + 1], scale=ca1[:, c, tb // 2:tb // 2 + 1])
                    ins.then_inc(job_read["A"], 1)
                elif kind == "qkp":
                    _, tb, side, c = it
                    n = ORD[it]
                    wait_full(act, it)
                    if n >= 2:
                        act.wait_ge(*parts_of(n - 2))
                    bias = bq_s[:, c:c + 1] if side == 0 else bqk[:, 1, c:c + 1]
                    act.activation(v32[:, n % 2, :], job_bank[JOB[it] % 2][:, :], ACT.Identity, bias=bias,
                                   scale=Q_SCALE if side == 0 else 1.0).then_inc(job_read["A"], 1)
                elif kind == "nmax":
                    u = it[1]
                    wait_full(act, it)
                    if u >= 2:
                        act.wait_ge(l_nm[u % 2], 32 * (u // 2))
                    act.activation(nmT[:, u % 2, :], job_bank[JOB[it] % 2][:, :].bitcast(BF16)[0:2 * HG, 0:BLK],
                                   ACT.Copy).then_inc(job_read["A"], 1)
                elif kind == "qk":
                    _, u, kt, hl = it
                    m = ORD[("pv", u, kt)]
                    q0, _ = diagonal(u, kt)
                    act.wait_ge(score_full, ORD[it] + 1)
                    if m >= 2 and hl == 0:
                        act.wait_ge(pv_done, m - 1)
                    act.activation(p_t[:, m % 2, hl, q0:BLK], s_bank[ORD[it] % S_RING][:, q0:BLK],
                                   ACT.Exp).then_inc(exp_done, 1)
                elif kind == "ctxT":
                    _, tb, pr = it
                    wait_full(act, it)
                    if tb:
                        wait_full(act, ("wo", tb - 1, pr))
                    act.activation(ctxT[:, pr, :], job_bank[JOB[it] % 2][:, :], ACT.Copy).then_inc(job_read["A"], 1)
                elif kind == "h2T":
                    _, tb, pr = it
                    t0 = BLK * tb + 2 * P * pr
                    wait_full(act, it)
                    act.activation(h2T[:, :, t0:t0 + 2 * P],
                                   job_bank[JOB[it] % 2][:, :].rearrange("p (c t) -> p c t", c=DC),
                                   ACT.Copy).then_inc(job_read["A"], 1)
                elif kind == "route":
                    act.wait_ge(nlmax_set, it[1] + 1)
                    for i in range(TPB):
                        ins = act.activation(sc_exp[:, i, :], lg[:, i, :], ACT.Exp, bias=nlmax[:, i:i + 1],
                                             accum_out=esum[:, i:i + 1])
                    ins.then_inc(sexp_set, 1)
                elif kind == "su":
                    _, tb, m = it
                    n, rn = ORD[it], SM[m][1]
                    act.wait_ge(su_full, n + 1)
                    if n >= 2:
                        act.wait_ge(hid_set, n - 1)
                    act.activation(s_sig[0:rn, n % 2, :], bank[2 * (n % 2)][0:rn, :], ACT.Silu).then_inc(sig_set, 1)

            def sigs(i, r):
                e = i * RING + r
                act.wait_ge(e_up, e + 1)
                if not (isinstance(e, int) and e < 2):
                    act.wait_ge(e_hid, e - 1)
                act.activation(sigA[r % 2][:, :], bank[2 * (r % 2)][:, 0:CAP], ACT.Silu)
                act.activation(sigB[r % 2][:, :], bank[2 * (r % 2) + 1][0:IB, 0:CAP], ACT.Silu).then_inc(e_sig, 1)

            def weigh(i, r):
                e = i * RING + r
                act.wait_ge(e_down, e + 1)
                act.wait_ge(e_staged, e + 1)
                if not (isinstance(e, int) and e < 2):
                    act.wait_ge(e_added, 16 * SPE * (e - 1))
                for s in range(SPE):
                    ins = act.activation(ob[r % 2][:, s, :], bank[4 + r % 2][:, D * s:D * (s + 1)], ACT.Copy,
                                         scale=wt_st[r][:, s:s + 1])
                ins.then_inc(e_ob, 1)

            def body(i, first=False):
                for r in range(RING):
                    sigs(i, r)
                    if not (first and r == 0):
                        weigh(i if r else i - 1, (r - 1) % RING)

            body(0, first=True)
            with act.Fori(1, E // RING) as i:
                body(i)
            weigh(E // RING - 1, RING - 1)

        @block.vector
        def _(dve):
            chain = [0]

            def link(ins):
                chain[0] += 1
                ins.then_inc(dve_chain, 1)
                dve.wait_ge(dve_chain, chain[0])

            def split(it):
                n = ORD[it]
                wait_read(dve, it)
                if n >= 2:
                    dve.wait_ge(l_parts[n % 2], 16 * (n // 2))
                v, pt = v32[:, n % 2, :], parts[:, n % 2, :, :]
                link(dve.tensor_copy(pt[:, 0, :], v))
                link(dve.tensor_tensor(res[:, :], v, pt[:, 0, :], ALU.subtract))
                link(dve.tensor_copy(pt[:, 1, :], res[:, :]))
                dve.tensor_tensor(pt[:, 2, :], res[:, :], pt[:, 1, :], ALU.subtract).then_inc(parts_first, 1)

            def gate_of(dst, src):
                link(dve.tensor_scalar(sign2[:, :], src, 0.0, 2.0, ALU.is_ge, ALU.mult))
                link(dve.tensor_scalar(sign[:, :], sign2[:, :], -1.0, None, ALU.add))
                link(dve.tensor_tensor(mag[:, :], src, sign[:, :], ALU.mult))
                return dve.scalar_tensor_tensor(out=dst, in0=mag[:, :], scalar=MIN_GATE, in1=sign[:, :],
                                                op0=ALU.max, op1=ALU.mult)

            def row_stats(tiles, into, n):
                if n:
                    dve.wait_ge(var_set, n)
                for i in range(TPB):
                    ins = dve.bn_stats(stats[:, i, :], x_sb[:, tiles + i, :])
                link(ins)
                for i in range(TPB):
                    ins = dve.bn_aggr(into[:, tiles + i, :], stats[:, i, :])
                ins.then_inc(var_set, 1)

            link(dve.memset(before[:, 0, :], 0.0))
            dve.wait_ge(c_exped, 1)
            link(dve.tensor_scalar(c_den[:, :], c_exp_sb[:, :], 1.0, None, ALU.add))
            link(dve.reciprocal(c_rec[:, :], c_den[:, :]))
            dve.tensor_tensor(c_act[:, :], c_sb[:, :], c_rec[:, :], ALU.mult).then_inc(c_acted, 1)
            for it in ITEMS:
                kind = it[0]
                if kind == "stat":
                    dve.wait_ge(l_x[it[1]], 16)
                    row_stats(TPB * it[1], mv, VAR[it])
                elif kind == "mod":
                    dve.wait_ge(l_const, 16 * N_CONST)
                    dve.tensor_scalar(bq_s[:, :], bqk[:, 0, :], Q_SCALE, None, ALU.mult)
                    wait_full(dve, "cT")
                    jb = job_bank[JOB["cT"] % 2]
                    dve.tensor_copy(c_rep[:, :, :], jb[:, 0:DC * B].rearrange("p (k a) -> p k a", a=1)
                                    .to_broadcast([P, DC * B, P]))
                    dve.tensor_copy(cT[:, :, :], jb[:, 0:DC * B].rearrange("p (c b) -> p c b", c=DC)).then_inc(job_read["D"], 1)
                    wait_full(dve, "gwT")
                    dve.tensor_copy(gwT[:, :, :], job_bank[JOB["gwT"] % 2][:, 0:DC * E].rearrange("p (c e) -> p c e", c=DC))\
                       .then_inc(job_read["D"], 1)
                    wait_full(dve, "modT")
                    jb = job_bank[JOB["modT"] % 2][:, 0:2 * DC * B].rearrange("p (k c b) -> p k c b", k=2, c=DC)
                    dve.tensor_copy(sa[:, :, :], jb[:, 0])
                    dve.tensor_scalar(ca1[:, :, :], jb[:, 1], 1.0, None, ALU.add).then_inc(job_read["D"], 1)
                elif kind == "row":
                    _, b, k = it
                    wait_full(dve, it)
                    jb = job_bank[JOB[it] % 2]
                    if k == 0:
                        dve.tensor_copy(sb_row[:, b, :], jb[:, D:2 * D])
                        gate_of(ga[:, b, :], jb[:, 0:D]).then_inc(job_read["D"], 1)
                    else:
                        dve.tensor_scalar(cb1[:, b, :], jb[:, 0:D], 1.0, None, ALU.add)
                        gate_of(gb[:, b, :], jb[:, D:2 * D]).then_inc(job_read["D"], 1)
                elif kind == "ln":
                    _, tb, pr = it
                    n = ORD[it]
                    dve.wait_ge(rstd_set, VAR[("stat", tb)] + 1)
                    if n >= 2:
                        wait_full(dve, ("ln", tb - 1, pr))
                    for i in range(2):
                        t = TPB * tb + 2 * pr + i
                        ins = dve.tensor_scalar(xhat[:, n % 2, i, :], x_sb[:, t, :], mv[:, t, 0:1], rstd[:, t:t + 1],
                                                ALU.subtract, ALU.mult)
                    ins.then_inc(xhat_set, 1)
                elif kind == "qkp":
                    if it[1] == 0:
                        split(it)
                elif kind == "vp":
                    _, tb, pr = it
                    wait_full(dve, it)
                    if pr == 0:
                        if tb == 0:
                            dve.wait_ge(set_up, 1)
                        if tb >= VRING:
                            dve.wait_ge(pv_done, upto("pv", lambda i: key_block(i[1], i[2]) == tb - VRING))
                    for i in range(2):
                        ins = dve.tensor_tensor(v_aug[tb % VRING][:, 2 * pr + i, :, 0:HD],
                                                job_bank[JOB[it] % 2][:, D * i:D * (i + 1)].rearrange("p (h d) -> p h d", h=H),
                                                bv_row[:, :].rearrange("p (h d) -> p h d", h=H), ALU.add)
                    ins.then_inc(job_read["D"], 1)
                elif kind == "max":
                    _, u, qt, hl, half = it
                    w = (qt + 1) * P if half == UNITS[u][1] else BLK
                    dve.wait_ge(max_full, ORD[it] + 1)
                    dve.reduce_max(rmax[:, half, qt, hl:hl + 1], m_bank[ORD[it] % M_RING][:, 0:w], AX.X).then_inc(max_read, 1)
                elif kind == "nmax":
                    u = it[1]
                    dve.wait_ge(max_read, upto("max", lambda i: i[1] == u))
                    if u:
                        wait_full(dve, ("nmax", u - 1))
                    m = rmax[:, 0]
                    if UNITS[u][1]:
                        m = rmax1[:, :, :]
                        link(dve.tensor_tensor(m, rmax[:, 0], rmax[:, 1], ALU.max))
                    link(dve.tensor_scalar(nm[:, :, 0, :], m, -1.0, None, ALU.mult))
                    dve.scalar_tensor_tensor(out=nm[:, :, 1, :], in0=m, scalar=-1.0, in1=nm[:, :, 0, :],
                                             op0=ALU.mult, op1=ALU.subtract).then_inc(nm_set, 1)
                elif kind == "ctx":
                    u = it[1]
                    b, qb, g = UNITS[u]
                    dve.wait_ge(pv_done, upto("pv", lambda i: i[1] == u))
                    if u:
                        wait_full(dve, ("ctx", u - 1))
                    dve.tensor_copy(ctx_f[:, :], pv_bank[:, :]).then_inc(ctxf_set, 1)
                    wait_full(dve, it)
                    if g == 0 and u:
                        wait_full(dve, ("ctxT", u // NG - 1, 1))
                    jb = job_bank[JOB[it] % 2][:, :].rearrange("p (t h d) -> p t h d", t=TPB, h=HG)
                    link(dve.reciprocal(ctx_r[:, :, :, :], jb[:, :, :, HD:HD + 1]))
                    dve.tensor_tensor(ctx_tok[:, :, HG * HD * g:HG * HD * (g + 1)].rearrange("p t (h d) -> p t h d", h=HG),
                                      jb[:, :, :, 0:HD], ctx_r[:, :, :, :].to_broadcast([P, TPB, HG, HD]),
                                      ALU.mult).then_inc(job_read["D"], 1)
                elif kind == "wo":
                    _, tb, pr = it
                    wait_full(dve, it)
                    dve.wait_ge(resid_set, tb + 1)
                    xs = x_sb[:, TPB * tb + 2 * pr:TPB * tb + 2 * pr + 2, :]
                    dve.tensor_tensor(xs, job_bank[JOB[it] % 2][:, :].rearrange("p (t d) -> p t d", t=2), xs,
                                      ALU.add).then_inc(job_read["D"], 1)
                elif kind == "ln2":
                    tb = it[1]
                    wait_read(dve, ("wo", tb, 1))
                    row_stats(TPB * tb, mv2, VAR[it])
                    dve.wait_ge(rstd_set, VAR[it] + 1)
                    if tb:
                        dve.wait_ge(l_h2, 16 * tb)
                        wait_full(dve, ("h2T", tb - 1, 1))
                    for i in range(TPB):
                        t = TPB * tb + i
                        ins = dve.tensor_scalar(h2[:, i, :], x_sb[:, t, :], mv2[:, t, 0:1], rstd2[:, t:t + 1],
                                                ALU.subtract, ALU.mult)
                    link(ins)
                    wait_read(dve, ("row", B - 1, 1))
                    for i in range(TPB):
                        ins = dve.tensor_tensor(h2[:, i, :], h2[:, i, :], cb1[:, tb // 2, :], ALU.mult)
                    link(ins)
                    for i in range(TPB):
                        ins = dve.tensor_tensor(h2[:, i, :], h2[:, i, :], sb_row[:, tb // 2, :], ALU.add)
                    ins.then_inc(h2_set, 1)
                elif kind == "gate":
                    wait_full(dve, it)
                    jb = job_bank[JOB[it] % 2][:, 0:TPB * E].rearrange("p (t e) -> p t e", t=TPB)
                    dve.tensor_copy(lg[:, :, :], jb).then_inc(job_read["D"], 1)
                    wait_read(dve, it)
                    dve.tensor_reduce(nlmax[:, :], lg[:, :, :], AX.X, ALU.max, negate=True).then_inc(nlmax_set, 1)
                elif kind == "route":
                    tb = it[1]
                    dve.wait_ge(sexp_set, tb + 1)
                    link(dve.reciprocal(rsum[:, :], esum[:, :]))
                    for i in range(TPB):
                        ins = dve.tensor_scalar(score[:, i, :], sc_exp[:, i, :], rsum[:, i:i + 1], None, ALU.mult)
                    link(ins)
                    for i in range(TPB):
                        ins = dve.max(top[:, i, :], score[:, i, :])
                    link(ins)
                    for i in range(TPB):
                        ins = dve.max_index(topi[:, i, :], top[:, i, :], score[:, i, :])
                    link(ins)
                    link(dve.tensor_copy(topf[:, :, :], topi[:, :, :]))
                    for i in range(TPB):
                        ins = dve.tensor_tensor(onehot[:, i, :, :],
                                                iota_e[:, :].rearrange("p (a e) -> p a e", a=1).to_broadcast([P, TOPK, E]),
                                                topf[:, i, 0:TOPK].rearrange("p (k a) -> p k a", a=1)
                                                .to_broadcast([P, TOPK, E]), ALU.is_equal)
                    link(ins)
                    if tb:
                        wait_full(dve, ("pos", tb - 1))
                    with nc.allow_low_precision(reason="counts up to one are exact"):
                        link(dve.tensor_reduce(member[:, :, :], onehot[:, :, :, :].rearrange("p t k e -> p t e k"),
                                               AX.X, ALU.add))
                    for i in range(TPB):
                        t = TPB * tb + i
                        ins = dve.tensor_tensor(before[:, t + 1, :], before[:, t, :], member[:, i, :], ALU.add)
                        if i < TPB - 1:
                            link(ins)
                    ins.then_inc(member_set, 1)
                elif kind == "pos":
                    tb = it[1]
                    wait_full(dve, it)
                    jb = job_bank[JOB[it] % 2]
                    for i in range(TPB):
                        ins = dve.tensor_tensor(onepos[:, i, :, :], onehot[:, i, :, :],
                                                jb[:, E * i:E * (i + 1)].rearrange("p (a e) -> p a e", a=1)
                                                .to_broadcast([P, TOPK, E]), ALU.mult)
                    ins.then_inc(job_read["D"], 1)
                    wait_read(dve, it)
                    link(dve.tensor_reduce(posk[:, :, :], onepos[:, :, :, :], AX.X, ALU.add))
                    link(dve.tensor_scalar(upper[:, :, :], posk[:, :, :], float(P), float(1 - P * SPT), ALU.is_ge, ALU.mult))
                    link(dve.scalar_tensor_tensor(out=addr[:, :, :], in0=posk[:, :, :], scalar=float(SPT),
                                                  in1=upper[:, :, :], op0=ALU.mult, op1=ALU.add))
                    link(dve.tensor_scalar(upper[:, :, :], posk[:, :, :], float(CAP), float(2 * SLOTS), ALU.is_ge, ALU.mult))
                    link(dve.tensor_tensor(addr[:, :, :], addr[:, :, :], upper[:, :, :], ALU.add))
                    dve.scalar_tensor_tensor(out=slot_ix[:, tb, :, :], in0=topf[:, :, 0:TOPK], scalar=float(SPE),
                                             in1=addr[:, :, :], op0=ALU.mult, op1=ALU.add)
                    dve.tensor_copy(payload[:, tb, :, :, 1], top[:, :, 0:TOPK])
                    dve.tensor_copy(payload[:, tb, :, :, 0],
                                    tok_id[:, TPB * tb:TPB * (tb + 1)].rearrange("p (t a) -> p t a", a=1)
                                    .to_broadcast([P, TPB, TOPK])).then_inc(slots_set, 1)
                elif kind == "su":
                    _, tb, m = it
                    n, rn = ORD[it], SM[m][1]
                    dve.wait_ge(sig_set, n + 1)
                    if m == 0 and tb >= 2:
                        dve.wait_ge(sd_full, 2 * (tb - 1))
                    dve.tensor_tensor(s_hid[0:rn, tb % 2, m, :], s_sig[0:rn, n % 2, :], bank[2 * (n % 2) + 1][0:rn, :],
                                      ALU.mult).then_inc(hid_set, 1)
                elif kind == "sd":
                    n = ORD[it]
                    dve.wait_ge(sd_full, n + 1)
                    if n >= 2:
                        dve.wait_ge(l_y[n % 2], 16 * (n // 2))
                    dve.tensor_copy(y_init[:, n % 2, :, :], bank[4 + n % 2][:, :].rearrange("p (t d) -> p t d", t=2))\
                       .then_inc(y_set, 1)
            dve.wait_ge(l_tab, 16)
            dve.tensor_copy(tab_ix[:, :], tab[:, :, 0]).then_inc(tabix_set, 1)

            def keep_xT(i, r):
                e = i * RING + r
                dve.wait_ge(e_turned, e + 1)
                if not (isinstance(e, int) and e < 2):
                    dve.wait_ge(e_up, e - 1)
                dve.tensor_copy(xgT[r % 2][:, :, :], bank[6 + r % 2][:, :].rearrange("p (c t) -> p c t", c=DC))\
                   .then_inc(e_xT, 1)

            def hids(i, r):
                e = i * RING + r
                dve.wait_ge(e_sig, e + 1)
                if not (isinstance(e, int) and e < 2):
                    dve.wait_ge(e_down, e - 1)
                dve.tensor_tensor(hidA[r % 2][:, :], sigA[r % 2][:, :], bank[2 * (r % 2)][:, CAP:2 * CAP], ALU.mult)
                dve.tensor_tensor(hidB[r % 2][:, :], sigB[r % 2][:, :], bank[2 * (r % 2) + 1][64:64 + IB, 0:CAP],
                                  ALU.mult).then_inc(e_hid, 1)

            keep_xT(0, 0)

            def body(i, last=False):
                for r in range(RING):
                    if not (last and r == RING - 1):
                        keep_xT(i + (r + 1) // RING, (r + 1) % RING)
                    hids(i, r)

            body(0)
            with dve.Fori(1, E // RING - 1) as i:
                body(i)
            body(E // RING - 1, last=True)
            for tb in range(NB):
                dve.wait_ge(l_yl[tb % 2], 16 * (tb // 2 + 1))
                for i in range(TPB):
                    ins = dve.tensor_tensor(y_ld[:, tb % 2, i, :], y_ld[:, tb % 2, i, :], gb[:, tb // 2, :], ALU.mult)
                ins.then_inc(y_scaled, 1)
                dve.wait_ge(y_scaled, tb + 1)
                dve.tensor_tensor(y_ld[:, tb % 2, :, :], y_ld[:, tb % 2, :, :], x_sb[:, TPB * tb:TPB * (tb + 1), :],
                                  ALU.add).then_inc(out_set, 1)

        @block.gpsimd
        def _(pool):
            chain = [0]

            def link(ins):
                chain[0] += 1
                ins.then_inc(pool_chain, 1)
                pool.wait_ge(pool_chain, chain[0])

            link(pool.memset(neg_half[:, :], -0.5))
            for v in v_aug:
                pool.memset(v[:, :, :, HD:VW], 1.0)
            pool.memset(zero_b[:, :], 0.0).then_inc(set_up, 1)
            for it in ITEMS:
                kind = it[0]
                if kind in ("stat", "ln2"):
                    into, mvx = (rstd, mv) if kind == "stat" else (rstd2, mv2)
                    t = slice(TPB * it[1], TPB * (it[1] + 1))
                    pool.wait_ge(var_set, VAR[it] + 1)
                    link(pool.tensor_scalar(var_e[:, t], mvx[:, t, 1], 1.0, EPS, ALU.mult, ALU.add))
                    pool.tensor_tensor(into[:, t], var_e[:, t], neg_half[:, :], ALU.pow).then_inc(rstd_set, 1)
                elif kind == "qkp" and it[1]:
                    n = ORD[it]
                    wait_read(pool, it)
                    pool.wait_ge(l_parts[n % 2], 16 * (n // 2))
                    v, pt = v32[:, n % 2, :], parts[:, n % 2, :, :]
                    link(pool.tensor_scalar(pt[:, 0, :], v, 1.0, 0.0, ALU.mult, ALU.add))
                    link(pool.tensor_tensor(res[:, :], v, pt[:, 0, :], ALU.subtract))
                    link(pool.tensor_scalar(pt[:, 1, :], res[:, :], 1.0, 0.0, ALU.mult, ALU.add))
                    pool.tensor_tensor(pt[:, 2, :], res[:, :], pt[:, 1, :], ALU.subtract).then_inc(parts_set, 1)
                elif kind == "wog":
                    wait_read(pool, ("row", B - 1, 1))
                    pool.wait_ge(l_wvo, 32)
                    for b in range(B):
                        for c in range(DC):
                            pool.tensor_tensor(wo_g[:, b, c, :], wo_sb[:, c, :], ga[:, b, :], ALU.mult)
                        ins = pool.tensor_tensor(ga_bo[:, b, :], bo_row[:, :], ga[:, b, :], ALU.mult)
                    ins.then_inc(wo_scaled, 1)
                    pool.wait_ge(wo_scaled, 1)
                    pool.wait_ge(xhat_set, 2)
                    for i in range(TPB):
                        ins = pool.tensor_tensor(x_sb[:, i, :], x_sb[:, i, :], ga_bo[:, 0, :], ALU.add)
                    ins.then_inc(resid_set, 1)
                elif kind == "resid" and it[1]:
                    tb = it[1]
                    pool.wait_ge(xhat_set, 2 * (tb + 1))
                    for i in range(TPB):
                        t = TPB * tb + i
                        ins = pool.tensor_tensor(x_sb[:, t, :], x_sb[:, t, :], ga_bo[:, tb // 2, :], ALU.add)
                    ins.then_inc(resid_set, 1)
                elif kind == "pos":
                    tb = it[1]
                    pool.wait_ge(slots_set, tb + 1)
                    pool.wait_ge(l_init, 48)
                    for i in range(TPB):
                        for k in range(TOPK):
                            pool.indirect_dma_start(
                                slot_table, bass.IndirectOffsetOnAxis(ap=slot_ix[:, tb, i, k:k + 1], axis=0),
                                payload[:, tb, i, k, :], None, bounds_check=SLOTS - 1, oob_is_err=False).then_inc(l_scat, 16)
                elif kind == "su" and ORD[it] == 0:
                    pool.wait_ge(l_sw, 16 * (2 + len(SM)))
                    for r in range(RING):
                        ins = pool.memset(w13_sb[r][:, 0:DC * W13].rearrange("p (c n) -> p c n", c=DC)[:, :, COL_B + IB:COL_B + 64], 0.0)
                    ins.then_inc(pads_set, 1)
            pool.wait_ge(tabix_set, 1)
            pool.wait_ge(l_h2, 16 * NB)
            for i in range(2):
                pool.wait_ge(l_y[i], 16 * total["sd"] // 2)

            def stage(i, r):
                e = i * RING + r
                if not (isinstance(e, int) and e < RING):
                    pool.wait_ge(e_turned, e - RING + 1)
                    pool.wait_ge(e_added, 16 * SPE * (e - RING + 1))
                pool.tensor_copy(wt_st[r][:, :], tab[:, bass.ds(SPE * e, SPE), 1])
                pool.tensor_copy(idx_st[r][:, :], tab_ix[:, bass.ds(SPE * e, SPE)]).then_inc(e_staged, 1)
                pool.wait_ge(e_staged, e + 1)
                pool.sem_inc(pool_at, 1)
                for s in range(SPE):
                    pool.indirect_dma_start(xg[r][:, s, :], None, h2_rows,
                                            bass.IndirectOffsetOnAxis(ap=idx_st[r][:, s:s + 1], axis=0)).then_inc(e_x[r], 16)

            def add(i, r):
                e = i * RING + r
                pool.wait_ge(e_ob, e + 1)
                if not (isinstance(e, int) and e < 1):
                    pool.wait_ge(e_added, 16 * SPE * e)
                pool.sem_inc(pool_at, 1)
                for s in range(SPE):
                    pool.indirect_dma_start(y_rows, bass.IndirectOffsetOnAxis(ap=idx_st[r][:, s:s + 1], axis=0),
                                            ob[r % 2][:, s, :], None, compute_op=ALU.add).then_inc(e_added, 16)

            AHEAD = 2
            for r in range(AHEAD):
                stage(0, r)

            def body(i, first=False, last=False):
                for r in range(RING):
                    if not (first and r == 0):
                        add(i if r else i - 1, (r - 1) % RING)
                    if not (last and r >= RING - AHEAD):
                        stage(i + (r + AHEAD) // RING, (r + AHEAD) % RING)

            body(0, first=True)
            with pool.Fori(1, E // RING - 1) as i:
                body(i)
            body(E // RING - 1, last=True)
            add(E // RING - 1, RING - 1)


def constants():
    bf = np.dtype("bfloat16")
    slope = np.float32(2.0 ** (-8.0 / H)) ** np.arange(1, H + 1, dtype=np.float32)
    bias = slope[:, None] * np.arange(1 - S, 1, dtype=np.float32)[None, :]
    alibi = []
    for _ in range(3):
        alibi.append(bias.astype(bf))
        bias = bias - alibi[-1].astype(np.float32)
    q, k = np.arange(P)[:, None], np.arange(P)[None, :]
    masks = np.stack([np.where(k > q, NEG, 0.0), np.where(q > k, NEG, 0.0), (q == k) * 1.0]).astype(bf)
    tri = np.stack([(q < k) * 1.0, np.ones((P, P))], axis=1).astype(bf)
    slot = np.zeros((P, E, SPE, 2), np.float32)
    slot[..., 0] = T + np.arange(SPE)[None, None, :] * P + np.arange(P)[:, None, None]
    return {
        "alibi": np.stack(alibi), "ones_rows": np.ones((3, HG, S), bf), "zero_row": np.zeros((1, D), np.float32),
        "masks": masks, "ident": np.eye(P, dtype=np.float32)[None], "tri": tri,
        "iota": np.tile(np.arange(E, dtype=np.float32), (P, 1)),
        "tok": (np.arange(P)[:, None] + P * np.arange(NT)[None, :]).astype(np.float32),
        "slot_init": slot.reshape(SLOTS, 2),
    }


_INS = ["L0_attn_x", "L0_attn_Wq", "L0_attn_bq", "L0_attn_Wk", "L0_attn_bk", "L0_attn_Wv", "L0_attn_bv", "L0_attn_Wo",
        "L0_attn_bo", "L0_ffn_gate_w", "L0_ffn_w1", "L0_ffn_w2", "L0_ffn_w3", "L0_ffn_sw1", "L0_ffn_sw2", "L0_ffn_sw3",
        "L0_c", "L0_wmod"]


def kernel(**inputs):
    import numpy as _np
    import concourse.bacc as _bacc
    from concourse import mybir as _mybir
    from concourse.bass_utils import run_bass_kernel_spmd as _run

    nc = _bacc.Bacc("TRN2", target_bir_lowering=False, num_devices=1)
    arrays, args = {}, []
    data = {n: _np.asarray(inputs[n]) for n in _INS}
    data["L0_attn_x"] = data["L0_attn_x"].reshape(T, D)
    for name, a in {**data, **constants()}.items():
        a = _np.ascontiguousarray(a)
        arrays[f"in_{name}"] = a
        args.append(nc.dram_tensor(f"in_{name}", a.shape, _mybir.dt.from_np(a.dtype), kind="ExternalInput").ap())
    args.append(nc.dram_tensor("out_0", (T, D), _mybir.dt.float32, kind="ExternalOutput").ap())
    adaln_kernel(nc, *args)
    r = _run(nc, [arrays], core_ids=[0])
    return r.results[0]["out_0"].reshape(B, S, D)
```

```python
from contextlib import ExitStack

import numpy as np

import concourse.bass as bass
from concourse import mybir

F32 = mybir.dt.float32
BF16 = mybir.dt.bfloat16
U32 = mybir.dt.uint32
ALU = mybir.AluOpType
ACT = mybir.ActivationFunctionType
AX = mybir.AxisListType

P = 128
B, S, D = 2, 1024, 256
T = B * S
NT = T // P
BLK = 512
NB = T // BLK
TPB = BLK // P
H, HD = 16, 16
HG = 4
NG = H // HG
DC = D // P
E, TOPK, CAP, INTER = 32, 6, 256, 176
IB = INTER - P
SI = 2 * INTER
SM = [(0, 128), (128, 128), (256, SI - 256)]
NMOD = 6
NEG = -1.0e30
EPS = 1e-5
MIN_GATE = 0.25
Q_SCALE = float(HD) ** -0.5
VW = HD + 1
QPARTS = (0, 0, 1, 1, 0, 2)
KPARTS = (0, 1, 0, 1, 2, 0)
NPROD = len(QPARTS)
ROW_ALIBI = NPROD * HD
ROW_NMAX = ROW_ALIBI + 3
K_MAX = ROW_NMAX
K_EXP = ROW_NMAX + 2
SLOTS = E * CAP
SPT = SLOTS // P
SPE = CAP // P
RING = 4
COL_B = 2 * P
W13 = COL_B + 64 + IB
S_RING, M_RING, STACKS, VRING = 3, 2, 3, 3

UNITS = [(b, qb, g) for b in range(B) for qb in range(S // BLK) for g in range(NG)]
NU = len(UNITS)


def merge(*lists):
    at = sorted(((i + 1) / len(x), n, i) for n, x in enumerate(lists) for i in range(len(x)))
    return [lists[n][i] for _, n, i in at]


def plan():

    def maxes(u):
        return [("max", u, qt, hl, half) for qt in range(TPB) for hl in range(HG) for half in range(UNITS[u][1] + 1)]

    def exps(u):
        n, out = TPB * (UNITS[u][1] + 1), []
        for kt in range(n + 1):
            if kt < n:
                out += [("qk", u, kt, hl) for hl in range(HG)]
            if kt:
                out.append(("pv", u, kt - 1))
        return out

    def normed(tb):
        return [("ln", tb, pr) for pr in range(2)] + [("resid", tb)]

    def project(tb):
        return [("qkp", tb, s, c) for c in range(DC) for s in range(2)] + [("vp", tb, pr) for pr in range(2)]

    def close_x(tb):
        return [("ctxT", tb, 0), ("ctxT", tb, 1), ("wo", tb, 0), ("wo", tb, 1), ("ln2s", tb), ("ln2", tb)]

    def close_h(tb):
        return [("h2T", tb, 0), ("h2T", tb, 1), ("gate", tb)]

    def close_r(tb):
        return [("route", tb, n) for n in range(5)] + [("rank", tb), ("pos", tb)]

    def shared(tb):
        return [("su", tb, m) for m in range(len(SM))] + [("sd", tb, pr) for pr in range(2)]

    items = [("stat", 0), ("mod",)] + normed(0) + project(0) + [("stk", 0), ("stk", 1)]
    items += [("stat", t) for t in range(1, NB)] + maxes(0) + [("neg", 0), ("nmax", 0)]
    for u in range(NU):
        tb, step = u // NG, u % NG
        extra = [("ctx", u - 1)] if u else []
        if u == 0:
            extra += [("row", b, k) for b in range(B) for k in range(2)] + [("wog",)]
        if step == 0 and tb:
            extra += close_x(tb - 1)
        if step == 1:
            extra += (close_h(tb - 1) if tb else []) + (normed(tb + 1) if tb + 1 < NB else [])
        if step == 2:
            extra += (close_r(tb - 1) if tb else []) + (project(tb + 1) if tb + 1 < NB else [])
        if u + 2 < NU:
            extra.append(("stk", u + 2))
        ex = exps(u)
        if u + 1 < NU:
            cut = (len(ex) * 3) // 4
            items += merge(ex[:cut], maxes(u + 1), extra) + [("neg", u + 1)] + ex[cut:-5] + [("nmax", u + 1)] + ex[-5:]
        else:
            items += merge(ex, extra)
        items.append(("acc", u))
    s0, x, last = shared(0), close_x(NB - 1), NB - 1
    items += [("ctx", NU - 1), ("free",)] + x[:2] + s0[:1] + x[2:4] + s0[1:2] + x[4:] + s0[2:] + close_h(last) + shared(1)
    items += close_r(last) + shared(2) + shared(3)
    return items


def load_expert(sp, e, w1, w3, w2, w13_slot, w2_slot, loaded):
    w13 = w13_slot[:, 0:DC * W13].rearrange("p (c n) -> p c n", c=DC)
    for w, k in ((w1, 0), (w3, 1)):
        src = w[bass.ds(e, 1)].rearrange("e (c p) i -> p (e c) i", p=P)
        sp.dma_start(w13[:, :, P * k:P * (k + 1)], src[:, :, 0:P]).then_inc(loaded, 16)
        sp.dma_start(w13[:, :, COL_B + 64 * k:COL_B + 64 * k + IB], src[:, :, P:INTER]).then_inc(loaded, 16)
    sp.dma_start(w2_slot[:, 0, :], w2[bass.ds(e, 1), 0:P, :].rearrange("e p d -> (e p) d")).then_inc(loaded, 16)
    sp.dma_start(w2_slot[0:IB, 1, :], w2[bass.ds(e, 1), P:INTER, :].rearrange("e p d -> (e p) d")).then_inc(loaded, 16)


LOADS_PER_EXPERT = 6


def adaln_kernel(nc, x, Wq, bq, Wk, bk, Wv, bv, Wo, bo, gate_w, w1, w2, w3, sw1, sw2, sw3, c_in, wmod,
                 alibi, ones_rows, zero_row, masks, ident_in, tri_in, iota_in, tok_in, slot_init, out):
    ITEMS = plan()
    ORD, total = {}, {}
    for it in ITEMS:
        ORD[it] = total.get(it[0], 0)
        total[it[0]] = ORD[it] + 1
    VAR = {it: n for n, it in enumerate(i for i in ITEMS if i[0] in ("stat", "ln2s"))}
    READER = {"ln": "A", "qkp": "A", "vp": "D", "nmax": "A", "ctx": "D", "ctxT": "A", "wo": "D",
              "h2T": "A", "gate": "D", "pos": "D", "row": "D"}
    jobs = []
    for it in ITEMS:
        if it[0] == "mod":
            jobs += [("cT", "D"), ("gwT", "D"), ("modT", "D")]
        if it[0] in READER:
            jobs.append((it, READER[it[0]]))
    JOB = {n: j for j, (n, _) in enumerate(jobs)}
    seen, READ = {"A": 0, "D": 0}, []
    for _, r in jobs:
        seen[r] += 1
        READ.append((r, seen[r]))

    def upto(kind, accepts):
        return max(ORD[it] + 1 for it in ITEMS if it[0] == kind and accepts(it))

    def key_block(u, kt):
        return 2 * UNITS[u][0] + kt // TPB

    def diagonal(u, kt):
        j = kt - TPB * UNITS[u][1]
        return (j * P, True) if j >= 0 else (0, False)

    ctx = ExitStack()
    with ctx:
        def sb(name, shape, dt=F32):
            return ctx.enter_context(nc.sbuf_tensor(name, shape, dt))

        def sem(name):
            return ctx.enter_context(nc.semaphore(name))

        q_parts = [nc.dram_tensor(f"q_parts{i}", [3, D, S], BF16, kind="Internal").ap() for i in range(B)]
        k_parts = [nc.dram_tensor(f"k_parts{i}", [3, D, S], BF16, kind="Internal").ap() for i in range(B)]
        h2_rows = nc.dram_tensor("h2_rows", [T + CAP, D], F32, kind="Internal").ap()
        slot_table = nc.dram_tensor("slot_table", [SLOTS, 2], F32, kind="Internal").ap()

        bank = [ctx.enter_context(nc.psum_tensor(f"bank{i}", [P, 512], F32)) for i in range(8)]
        s_bank, m_bank, pv_bank, job_bank = bank[0:3], bank[3:5], bank[5], bank[6:8]

        ident = sb("ident", [P, P])
        identb = sb("identb", [P, P], BF16)
        mask_qk = sb("mask_qk", [P, 2, P], BF16)
        tri = sb("tri", [P, 2, P], BF16)
        iota_e = sb("iota_e", [P, E])
        tok_id = sb("tok_id", [P, NT])
        neg_half = sb("neg_half", [P, TPB])
        zero_b = sb("zero_b", [P, BLK], BF16)
        wo_sb = sb("wo_sb", [P, DC, D])
        wo_g = sb("wo_g", [P, B, DC, D])
        bqk = sb("bqk", [P, 2, DC])
        bq_s = sb("bq_s", [P, DC])
        bv_row, bo_row = sb("bv_row", [P, D]), sb("bo_row", [P, D])
        gw_in = sb("gw_in", [E, D])
        gwT = sb("gwT", [P, DC, E])
        c_sb, c_exp_sb, c_den, c_rec, c_act = (sb(n, [B, D]) for n in ("c_sb", "c_exp_sb", "c_den", "c_rec", "c_act"))
        cT = sb("cT", [P, DC, B])
        sa, ca1 = sb("sa", [P, DC, B]), sb("ca1", [P, DC, B])
        ga, sb_row, cb1, gb, ga_bo = (sb(n, [P, B, D]) for n in ("ga", "sb_row", "cb1", "gb", "ga_bo"))
        sign2, sign, mag = (sb(n, [P, D]) for n in ("sign2", "sign", "mag"))
        x_sb = sb("x_sb", [P, NT, D])
        stats = sb("stats", [P, TPB, 6])
        mv, mv2 = sb("mv", [P, NT, 2]), sb("mv2", [P, NT, 2])
        var_e, rstd, rstd2 = sb("var_e", [P, NT]), sb("rstd", [P, NT]), sb("rstd2", [P, NT])
        ctx_tok = sb("ctx_tok", [P, TPB, D])
        ctxT = sb("ctxT", [P, 2, 2 * DC * P])
        h2 = sb("h2", [P, TPB, D])
        h2T = sb("h2T", [P, DC, T])
        lg, sc_exp, score = (sb(n, [P, TPB, E]) for n in ("lg", "sc_exp", "score"))
        nlmax, esum, rsum = (sb(n, [P, TPB]) for n in ("nlmax", "esum", "rsum"))
        top = sb("top", [P, TPB, 8])
        topi = sb("topi", [P, TPB, 8], U32)
        topf = sb("topf", [P, TPB, 8])
        onehot = sb("onehot", [P, TPB, TOPK, E])
        onepos = sb("onepos", [P, TPB, TOPK, E])
        member = sb("member", [P, TPB, E], BF16)
        before = sb("before", [P, NT + 1, E], BF16)
        posk, addr, upper = (sb(n, [P, TPB, TOPK]) for n in ("posk", "addr", "upper"))
        slot_ix = sb("slot_ix", [P, NB, TPB, TOPK], U32)
        payload = sb("payload", [P, NB, TPB, TOPK, 2])
        tab = sb("tab", [P, SPT, 2])
        tab_ix = sb("tab_ix", [P, SPT], U32)
        tab_w = sb("tab_w", [P, B, SPT])

        with ExitStack() as first:
            def sb1(name, shape, dt=F32):
                return first.enter_context(nc.sbuf_tensor(name, shape, dt))

            wq_sb, wk_sb, wv_sb = (sb1(n, [P, DC, D]) for n in ("wq_sb", "wk_sb", "wv_sb"))
            wm = sb1("wm", [P, DC, NMOD * D])
            c_rep = sb1("c_rep", [P, DC * B, P])
            hT = sb1("hT", [P, DC, BLK])
            xhat = sb1("xhat", [P, 2, 2, D])
            v32 = sb1("v32", [P, 2, BLK])
            res = sb1("res", [P, BLK])
            parts = sb1("parts", [P, 2, 3, BLK], BF16)
            q_stack = [sb1(f"q_stack{i}", [P, HG, BLK], BF16) for i in range(STACKS)]
            k_stack = [sb1(f"k_stack{i}", [P, HG, S], BF16) for i in range(STACKS)]
            v_aug = [sb1(f"v_aug{i}", [P, TPB, H, VW]) for i in range(VRING)]
            p_t = sb1("p_t", [P, 2, HG, BLK])
            rmax = sb1("rmax", [P, 2, TPB, HG])
            rmax1 = sb1("rmax1", [P, TPB, HG])
            nm = sb1("nm", [P, TPB, 2, HG], BF16)
            nmT = sb1("nmT", [2 * HG, 2, BLK], BF16)
            ctx_f = sb1("ctx_f", [P, BLK])
            ctx_r = sb1("ctx_r", [P, TPB, HG, 1])
        sw1_sb, sw3_sb = sb("sw1_sb", [P, DC, SI]), sb("sw3_sb", [P, DC, SI])
        sw2_sb = sb("sw2_sb", [P, len(SM), D])
        s_sig = sb("s_sig", [P, 2, BLK])
        s_hid = sb("s_hid", [P, 2, len(SM), BLK])
        y_init = sb("y_init", [P, 2, 2, D])
        w13_sb = [sb(f"w13_sb{i}", [P, DC * W13]) for i in range(RING)]
        w2_sb = [sb(f"w2_sb{i}", [P, 2, D]) for i in range(RING)]
        idx_st = [sb(f"idx_st{i}", [P, SPE], U32) for i in range(RING)]
        idx_add = [sb(f"idx_add{i}", [P, SPE], U32) for i in range(2)]
        wt_st = [sb(f"wt_st{i}", [P, B, SPE]) for i in range(RING)]
        gate_0 = [sb(f"gate_0{i}", [P, SPE, D]) for i in range(2)]
        gate_w_sb = [sb(f"gate_w_sb{i}", [P, SPE, D]) for i in range(2)]
        xg = [sb(f"xg{i}", [P, SPE, D]) for i in range(RING)]
        xgT = [sb(f"xgT{i}", [P, DC, CAP]) for i in range(2)]
        sigA, hidA = ([sb(f"{n}{i}", [P, CAP]) for i in range(2)] for n in ("sigA", "hidA"))
        sigB, hidB = ([sb(f"{n}{i}", [IB, CAP]) for i in range(2)] for n in ("sigB", "hidB"))
        ob = [sb(f"ob{i}", [P, SPE, D]) for i in range(2)]

        l_x = [sem(f"l_x{i}") for i in range(NB)]
        l_const, l_c, l_wm, l_wqk, l_wvo, l_ones, l_init, l_sw, l_h2, l_scat, l_tab = (
            sem("l_" + n) for n in ("const", "c", "wm", "wqk", "wvo", "ones", "init", "sw", "h2", "scat", "tab"))
        l_parts, l_nm, l_y = ([sem(f"l_{n}{i}") for i in range(2)] for n in ("parts", "nm", "y"))
        l_stack = [sem(f"l_stack{i}") for i in range(STACKS)]
        e_w, e_x = ([sem(f"{n}{i}") for i in range(RING)] for n in ("e_w", "e_x"))
        e_added, pool_at, add_ix = sem("e_added"), sem("pool_at"), sem("add_ix")
        dve_chain, act_chain, pool_chain = sem("dve_chain"), sem("act_chain"), sem("pool_chain")
        job_full = sem("job_full")
        job_read = {"A": sem("job_read_act"), "D": sem("job_read_dve")}
        (set_up, c_exped, c_acted, wo_scaled, var_set, rstd_set, xhat_set, resid_set, parts_set,
         max_full, max_read, nm_set, score_full, exp_done, pv_done, ctxf_set, x2hat_set, h2_set, nlmax_set, sexp_set,
         member_set, slots_set, route_step, ranks_set, su_full, sig_set, hid_set, sd_full, y_set, tabix_set, pads_set) = (sem(n) for n in (
             "set_up", "c_exped", "c_acted", "wo_scaled", "var_set", "rstd_set", "xhat_set", "resid_set", "parts_set", "max_full", "max_read", "nm_set", "score_full", "exp_done", "pv_done", "ctxf_set",
             "x2hat_set", "h2_set", "nlmax_set", "sexp_set", "member_set", "slots_set", "route_step", "ranks_set", "su_full", "sig_set", "hid_set",
             "sd_full", "y_set", "tabix_set", "pads_set"))
        e_staged, e_turned, e_xT, e_up, e_sig, e_hid, e_down, e_ob, e_gate0, e_gate = (sem(n) for n in (
            "e_staged", "e_turned", "e_xT", "e_up", "e_sig", "e_hid", "e_down", "e_ob", "e_gate0", "e_gate"))
        N_CONST = 12

        block = ctx.enter_context(nc.Block())

        def wait_read(eng, name):
            r, n = READ[JOB[name]]
            eng.wait_ge(job_read[r], n)

        def wait_full(eng, name):
            eng.wait_ge(job_full, JOB[name] + 1)

        @block.sync
        def _(sp):
            with nc.allow_non_contiguous_dma(reason="biases by feature"):
                sp.dma_start(c_sb[:, :], c_in).then_inc(l_c, 16)
                sp.dma_start(x_sb[:, 0:TPB, :], x[0:BLK, :].rearrange("(t p) d -> p t d", p=P)).then_inc(l_x[0], 16)
                row = lambda v: v.rearrange("(a d) -> a d", a=1).to_broadcast([P, D])
                consts = ((ident[:, :], ident_in[0]), (gw_in[:, :], gate_w),
                          (bqk[:, 0, :], bq.rearrange("(c p) -> p c", p=P)),
                          (bqk[:, 1, :], bk.rearrange("(c p) -> p c", p=P)),
                          (identb[:, :], masks[2]), (mask_qk[:, 0, :], masks[0]), (mask_qk[:, 1, :], masks[1]),
                          (tri[:, :, :], tri_in), (iota_e[:, :], iota_in), (tok_id[:, :], tok_in),
                          (bv_row[:, :], row(bv)), (bo_row[:, :], row(bo)))
                assert len(consts) == N_CONST
                for dst, src in consts:
                    sp.dma_start(dst, src).then_inc(l_const, 16)
            sp.dma_start(wm[:, :, :], wmod.rearrange("(c p) n -> p c n", p=P)).then_inc(l_wm, 16)
            for w, src, s in ((wq_sb, Wq, l_wqk), (wk_sb, Wk, l_wqk), (wv_sb, Wv, l_wvo), (wo_sb, Wo, l_wvo)):
                sp.dma_start(w[:, :, :], src.rearrange("(c p) n -> p c n", p=P)).then_inc(s, 16)
            for i in range(STACKS):
                sp.dma_start(q_stack[i][ROW_ALIBI:ROW_NMAX, :, :], ones_rows[0:3, :, 0:BLK]).then_inc(l_ones, 16)
                sp.dma_start(k_stack[i][ROW_NMAX:K_EXP, :, :], ones_rows[0:2]).then_inc(l_ones, 16)
            for tb in range(1, NB):
                sp.dma_start(x_sb[:, TPB * tb:TPB * (tb + 1), :],
                             x[BLK * tb:BLK * (tb + 1), :].rearrange("(t p) d -> p t d", p=P)).then_inc(l_x[tb], 16)
            sp.dma_start(slot_table, slot_init).then_inc(l_init, 16)
            sp.dma_start(h2_rows[T:T + CAP, :], zero_row.to_broadcast([CAP, D])).then_inc(l_init, 16)
            sp.dma_start(out[T:T + CAP, :], zero_row.to_broadcast([CAP, D])).then_inc(l_init, 16)
            for it in ITEMS:
                kind = it[0]
                if kind == "qkp":
                    _, tb, side, c = it
                    n = ORD[it]
                    sp.wait_ge(parts_set, n + 1)
                    dst = (q_parts, k_parts)[side][tb // 2][:, c * P:(c + 1) * P, (tb % 2) * BLK:(tb % 2 + 1) * BLK]
                    sp.dma_start(dst.rearrange("j p t -> p j t"), parts[:, n % 2, :, :]).then_inc(l_parts[n % 2], 16)
                if kind == "stk":
                    u = it[1]
                    b, qb, g = UNITS[u]
                    s_, rows = l_stack[u % STACKS], slice(HG * HD * g, HG * HD * (g + 1))
                    for i in range(2):
                        sp.wait_ge(l_parts[i], 16 * 2 * (u // NG + 1))
                    if u >= STACKS:
                        sp.wait_ge(score_full, upto("qk", lambda i: i[1] == u - STACKS))
                    keys = BLK * (qb + 1)
                    for j in range(NPROD):
                        sp.dma_start(q_stack[u % STACKS][HD * j:HD * (j + 1), :, :],
                                     q_parts[b][QPARTS[j], rows, BLK * qb:BLK * (qb + 1)]
                                     .rearrange("(h d) t -> d h t", d=HD)).then_inc(s_, 16)
                        sp.dma_start(k_stack[u % STACKS][HD * j:HD * (j + 1), :, 0:keys],
                                     k_parts[b][KPARTS[j], rows, 0:keys]
                                     .rearrange("(h d) t -> d h t", d=HD)).then_inc(s_, 16)
                    sp.dma_start(k_stack[u % STACKS][ROW_ALIBI:ROW_NMAX, :, 0:keys],
                                 alibi[:, HG * g:HG * (g + 1), 0:keys]).then_inc(s_, 16)
                if kind == "nmax":
                    u = it[1]
                    wait_read(sp, it)
                    for part in range(2):
                        sp.dma_start(q_stack[u % STACKS][ROW_NMAX + part:ROW_NMAX + part + 1, :, :],
                                     nmT[HG * part:HG * (part + 1), u % 2, :]).then_inc(l_nm[u % 2], 16)
                if kind == "ln2":
                    tb = it[1]
                    sp.wait_ge(h2_set, tb + 1)
                    sp.dma_start(h2_rows[BLK * tb:BLK * (tb + 1), :].rearrange("(t p) d -> p t d", p=P),
                                 h2[:, :, :]).then_inc(l_h2, 16)
                if kind == "free":
                    wait_read(sp, ("ctx", NU - 1))
                    sp.wait_ge(exp_done, total["qk"])
                    sp.wait_ge(wo_scaled, 1)
                    sp.dma_start(sw1_sb[:, :, :], sw1.rearrange("(c p) n -> p c n", p=P)).then_inc(l_sw, 16)
                    sp.dma_start(sw3_sb[:, :, :], sw3.rearrange("(c p) n -> p c n", p=P)).then_inc(l_sw, 16)
                    for m, (r0, rn) in enumerate(SM):
                        sp.dma_start(sw2_sb[0:rn, m, :], sw2[r0:r0 + rn, :]).then_inc(l_sw, 16)
                    for r in range(RING):
                        load_expert(sp, r, w1, w3, w2, w13_sb[r], w2_sb[r], e_w[r])
                if kind == "sd":
                    _, tb, pr = it
                    n, r0 = ORD[it], BLK * tb + 2 * P * pr
                    sp.wait_ge(y_set, n + 1)
                    sp.dma_start(out[r0:r0 + 2 * P, :].rearrange("(t p) d -> p t d", p=P),
                                 y_init[:, n % 2, :, :]).then_inc(l_y[n % 2], 16)
            sp.wait_ge(l_scat, 16 * NT * TOPK)
            sp.dma_start(tab[:, :, :], slot_table.rearrange("(p j) n -> p j n", p=P)).then_inc(l_tab, 16)
            with sp.Fori(1, E // RING) as i:
                for r in range(RING):
                    sp.wait_ge(e_down, (i - 1) * RING + r + 1)
                    load_expert(sp, i * RING + r, w1, w3, w2, w13_sb[r], w2_sb[r], e_w[r])
            sp.wait_ge(e_added, 16 * SPE * E)

        @block.tensor
        def _(pe):
            def begin(name):
                j = JOB[name]
                if j >= 2:
                    r, n = READ[j - 2]
                    pe.wait_ge(job_read[r], n)
                return job_bank[j % 2]

            pe.wait_ge(set_up, 1)
            pe.wait_ge(l_const, 16 * N_CONST)
            pe.matmul(pv_bank[:, :], identb[:, :], zero_b[:, :], start=True, stop=True)
            for it in ITEMS:
                kind = it[0]
                if kind == "mod":
                    jb = begin("cT")
                    pe.wait_ge(c_acted, 1)
                    for c in range(DC):
                        ins = pe.transpose(jb[:, B * c:B * (c + 1)], c_act[:, c * P:(c + 1) * P], ident[0:B, 0:B])
                    ins.then_inc(job_full, 1)
                    jb = begin("gwT")
                    for c in range(DC):
                        ins = pe.transpose(jb[:, E * c:E * (c + 1)], gw_in[:, c * P:(c + 1) * P], ident[0:E, 0:E])
                    ins.then_inc(job_full, 1)
                    jb = begin("modT")
                    wait_read(pe, "cT")
                    pe.wait_ge(l_wm, 16)
                    for q in range(2 * DC):
                        for c in range(DC):
                            ins = pe.matmul(jb[:, B * q:B * (q + 1)], wm[:, c, q * P:(q + 1) * P], cT[:, c, :],
                                            start=(c == 0), stop=(c == DC - 1))
                    ins.then_inc(job_full, 1)
                elif kind == "row":
                    _, b, k = it
                    jb = begin(it)
                    for c in range(DC):
                        ins = pe.matmul(jb[:, :], c_rep[:, c * B + b, :], wm[:, c, 2 * D * (k + 1):2 * D * (k + 2)],
                                        start=(c == 0), stop=(c == DC - 1))
                    ins.then_inc(job_full, 1)
                elif kind == "ln":
                    _, tb, pr = it
                    jb = begin(it)
                    pe.wait_ge(xhat_set, ORD[it] + 1)
                    for c in range(DC):
                        for i in range(2):
                            ins = pe.transpose(jb[:, (2 * c + i) * P:(2 * c + i + 1) * P],
                                               xhat[:, ORD[it] % 2, i, c * P:(c + 1) * P], ident[:, :])
                    ins.then_inc(job_full, 1)
                elif kind == "qkp":
                    _, tb, side, co = it
                    jb = begin(it)
                    wait_read(pe, ("ln", tb, 1))
                    pe.wait_ge(l_wqk, 32)
                    for c in range(DC):
                        ins = pe.matmul(jb[:, :], (wq_sb, wk_sb)[side][:, c, co * P:(co + 1) * P], hT[:, c, :],
                                        start=(c == 0), stop=(c == DC - 1))
                    ins.then_inc(job_full, 1)
                elif kind == "vp":
                    _, tb, pr = it
                    jb = begin(it)
                    pe.wait_ge(l_wvo, 32)
                    for i in range(2):
                        for c in range(DC):
                            ins = pe.matmul(jb[:, D * i:D * (i + 1)], hT[:, c, (2 * pr + i) * P:(2 * pr + i + 1) * P],
                                            wv_sb[:, c, :], start=(c == 0), stop=(c == DC - 1))
                    ins.then_inc(job_full, 1)
                elif kind == "max":
                    _, u, qt, hl, half = it
                    n, mb, ring = ORD[it], m_bank[ORD[it] % M_RING], u % STACKS
                    crossed = half == UNITS[u][1]
                    w = (qt + 1) * P if crossed else BLK
                    if (qt, hl, half) == (0, 0, 0):
                        pe.wait_ge(l_stack[ring], 16 * (2 * NPROD + 1) * (u // STACKS + 1))
                        pe.wait_ge(l_ones, 32 * STACKS)
                    if n >= M_RING:
                        pe.wait_ge(max_read, n - M_RING + 1)
                    ins = pe.matmul(mb[:, 0:w], q_stack[ring][0:K_MAX, hl, qt * P:(qt + 1) * P],
                                    k_stack[ring][0:K_MAX, hl, half * BLK:half * BLK + w], start=True, stop=not crossed)
                    if crossed:
                        ins = pe.matmul(mb[:, w - P:w], identb[:, :], mask_qk[:, 0, :], start=False, stop=True)
                    ins.then_inc(max_full, 1)
                elif kind == "nmax":
                    jb = begin(it)[:, :].bitcast(BF16)
                    pe.wait_ge(nm_set, it[1] + 1)
                    for qt in range(TPB):
                        ins = pe.transpose(jb[0:2 * HG, qt * P:(qt + 1) * P],
                                           nm[:, qt, :, :].rearrange("p a h -> p (a h)"), identb[:, :])
                    ins.then_inc(job_full, 1)
                elif kind == "qk":
                    _, u, kt, hl = it
                    n, sbk, ring = ORD[it], s_bank[ORD[it] % S_RING], u % STACKS
                    q0, crossed = diagonal(u, kt)
                    if (kt, hl) == (0, 0):
                        pe.wait_ge(l_nm[u % 2], 32 * (u // 2 + 1))
                    if n >= S_RING:
                        pe.wait_ge(exp_done, n - S_RING + 1)
                    ins = pe.matmul(sbk[:, q0:BLK], k_stack[ring][0:K_EXP, hl, kt * P:(kt + 1) * P],
                                    q_stack[ring][0:K_EXP, hl, q0:BLK], start=True, stop=not crossed)
                    if crossed:
                        ins = pe.matmul(sbk[:, q0:q0 + P], identb[:, :], mask_qk[:, 1, :], start=False, stop=True)
                    ins.then_inc(score_full, 1)
                elif kind == "pv":
                    _, u, kt = it
                    m, kb = ORD[it], key_block(u, kt)
                    q0, _ = diagonal(u, kt)
                    pe.wait_ge(exp_done, HG * (m + 1))
                    if kt == 0:
                        wait_read(pe, ("vp", kb, 1))
                        if u:
                            pe.wait_ge(ctxf_set, u)
                    if kt == TPB:
                        wait_read(pe, ("vp", kb, 1))
                    last = kt == TPB * (UNITS[u][1] + 1) - 1
                    for hl in range(HG):
                        ins = pe.matmul(pv_bank[32 * hl:32 * hl + VW, q0:BLK],
                                        v_aug[kb % VRING][:, kt % TPB, HG * UNITS[u][2] + hl, :],
                                        p_t[:, m % 2, hl, q0:BLK], start=(kt == 0), stop=last)
                    ins.then_inc(pv_done, 1)
                elif kind == "ctx":
                    jb = begin(it)
                    pe.wait_ge(ctxf_set, it[1] + 1)
                    for qt in range(TPB):
                        ins = pe.transpose(jb[:, qt * P:(qt + 1) * P], ctx_f[:, qt * P:(qt + 1) * P], ident[:, :])
                    ins.then_inc(job_full, 1)
                elif kind == "ctxT":
                    _, tb, pr = it
                    jb = begin(it)
                    wait_read(pe, ("ctx", NG * tb + NG - 1))
                    for i in range(2):
                        for c in range(DC):
                            j = DC * i + c
                            ins = pe.transpose(jb[:, j * P:(j + 1) * P], ctx_tok[:, 2 * pr + i, c * P:(c + 1) * P], ident[:, :])
                    ins.then_inc(job_full, 1)
                elif kind == "wo":
                    _, tb, pr = it
                    jb = begin(it)
                    wait_read(pe, ("ctxT", tb, pr))
                    pe.wait_ge(wo_scaled, 1)
                    for i in range(2):
                        for c in range(DC):
                            j = DC * i + c
                            ins = pe.matmul(jb[:, D * i:D * (i + 1)], ctxT[:, pr, j * P:(j + 1) * P],
                                            wo_g[:, tb // 2, c, :], start=(c == 0), stop=(c == DC - 1))
                    ins.then_inc(job_full, 1)
                elif kind == "h2T":
                    _, tb, pr = it
                    jb = begin(it)
                    pe.wait_ge(h2_set, tb + 1)
                    for c in range(DC):
                        for i in range(2):
                            ins = pe.transpose(jb[:, (2 * c + i) * P:(2 * c + i + 1) * P],
                                               h2[:, 2 * pr + i, c * P:(c + 1) * P], ident[:, :])
                    ins.then_inc(job_full, 1)
                elif kind == "gate":
                    tb = it[1]
                    jb = begin(it)
                    wait_read(pe, ("h2T", tb, 1))
                    wait_read(pe, "gwT")
                    for i in range(TPB):
                        t0 = (TPB * tb + i) * P
                        for c in range(DC):
                            ins = pe.matmul(jb[:, E * i:E * (i + 1)], h2T[:, c, t0:t0 + P], gwT[:, c, :],
                                            start=(c == 0), stop=(c == DC - 1))
                    ins.then_inc(job_full, 1)
                elif kind == "pos":
                    tb = it[1]
                    jb = begin(it)
                    pe.wait_ge(member_set, tb + 1)
                    for i in range(TPB):
                        pe.matmul(jb[:, E * i:E * (i + 1)], tri[:, 0, :], member[:, i, :], start=True, stop=False)
                        ins = pe.matmul(jb[:, E * i:E * (i + 1)], tri[:, 1, :], before[:, TPB * tb + i, :],
                                        start=False, stop=True)
                    ins.then_inc(job_full, 1)
                elif kind == "su":
                    _, tb, m = it
                    n, (r0, rn) = ORD[it], SM[m]
                    if n == 0:
                        pe.wait_ge(l_sw, 16 * (2 + len(SM)))
                        pe.wait_ge(max_read, total["max"])
                    if m == 0:
                        wait_read(pe, ("h2T", tb, 1))
                    if n >= 2:
                        pe.wait_ge(hid_set, n - 1)
                    for w, k in ((sw1_sb, 0), (sw3_sb, 1)):
                        for c in range(DC):
                            ins = pe.matmul(bank[2 * (n % 2) + k][0:rn, :], w[:, c, r0:r0 + rn],
                                            h2T[:, c, BLK * tb:BLK * (tb + 1)], start=(c == 0), stop=(c == DC - 1))
                    ins.then_inc(su_full, 1)
                elif kind == "sd":
                    _, tb, pr = it
                    n = ORD[it]
                    pe.wait_ge(hid_set, len(SM) * (tb + 1))
                    if n >= 2:
                        pe.wait_ge(y_set, n - 1)
                    for i in range(2):
                        for m, (_, rn) in enumerate(SM):
                            ins = pe.matmul(bank[4 + n % 2][:, D * i:D * (i + 1)],
                                            s_hid[0:rn, tb % 2, m, (2 * pr + i) * P:(2 * pr + i + 1) * P],
                                            sw2_sb[0:rn, m, :], start=(m == 0), stop=(m == len(SM) - 1))
                    ins.then_inc(sd_full, 1)

            pe.wait_ge(pads_set, 1)
            pe.wait_ge(y_set, total["sd"])

            def turn(i, r):
                e = i * RING + r
                pe.wait_ge(e_x[r], 32 * i + 32)
                if not (isinstance(e, int) and e < 2):
                    pe.wait_ge(e_xT, e - 1)
                for c in range(DC):
                    for s in range(SPE):
                        ins = pe.transpose(bank[6 + r % 2][:, (SPE * c + s) * P:(SPE * c + s + 1) * P],
                                           xg[r][:, s, c * P:(c + 1) * P], ident[:, :])
                ins.then_inc(e_turned, 1)

            def up(i, r):
                e = i * RING + r
                pe.wait_ge(e_w[r], 16 * LOADS_PER_EXPERT * i + 16 * LOADS_PER_EXPERT)
                pe.wait_ge(e_xT, e + 1)
                if not (isinstance(e, int) and e < 2):
                    pe.wait_ge(e_hid, e - 1)
                a_bank, c_bank = bank[2 * (r % 2)], bank[2 * (r % 2) + 1]
                for k in range(2):
                    for c in range(DC):
                        w0 = c * W13 + k * P
                        pe.matmul(a_bank[:, CAP * k:CAP * (k + 1)], w13_sb[r][:, w0:w0 + P], xgT[r % 2][:, c, :],
                                  start=(c == 0), stop=(c == DC - 1))
                for c in range(DC):
                    w = w13_sb[r][:, c * W13 + COL_B:(c + 1) * W13]
                    ins = pe.matmul(c_bank[0:W13 - COL_B, 0:CAP], w, xgT[r % 2][:, c, :], start=(c == 0), stop=(c == DC - 1))
                ins.then_inc(e_up, 1)

            def down(i, r):
                e = i * RING + r
                pe.wait_ge(e_hid, e + 1)
                if not (isinstance(e, int) and e < 2):
                    pe.wait_ge(e_ob, e - 1)
                for s in range(SPE):
                    o = bank[4 + r % 2][:, D * s:D * (s + 1)]
                    pe.matmul(o, hidA[r % 2][:, s * P:(s + 1) * P], w2_sb[r][:, 0, :], start=True, stop=False)
                    ins = pe.matmul(o, hidB[r % 2][:, s * P:(s + 1) * P], w2_sb[r][0:IB, 1, :], start=False, stop=True)
                ins.then_inc(e_down, 1)

            turn(0, 0)

            def body(i, first=False, last=False):
                for r in range(RING):
                    if not (last and r == RING - 1):
                        turn(i + (r + 1) // RING, (r + 1) % RING)
                    up(i, r)
                    if not (first and r == 0):
                        down(i if r else i - 1, (r - 1) % RING)

            body(0, first=True)
            with pe.Fori(1, E // RING - 1) as i:
                body(i)
            body(E // RING - 1, last=True)
            down(E // RING - 1, RING - 1)

        @block.scalar
        def _(act):
            act.wait_ge(l_c, 16)
            act.activation(c_exp_sb[:, :], c_sb[:, :], ACT.Exp, scale=-1.0).then_inc(c_exped, 1)
            for it in ITEMS:
                kind = it[0]
                if kind == "ln":
                    _, tb, pr = it
                    wait_full(act, it)
                    wait_read(act, "modT")
                    if tb:
                        wait_full(act, ("vp", tb - 1, 1))
                    for c in range(DC):
                        ins = act.activation(hT[:, c, 2 * P * pr:2 * P * (pr + 1)],
                                             job_bank[JOB[it] % 2][:, 2 * P * c:2 * P * (c + 1)], ACT.Identity,
                                             bias=sa[:, c, tb // 2:tb // 2 + 1], scale=ca1[:, c, tb // 2:tb // 2 + 1])
                    ins.then_inc(job_read["A"], 1)
                elif kind == "qkp":
                    _, tb, side, c = it
                    n = ORD[it]
                    wait_full(act, it)
                    if n >= 2:
                        act.wait_ge(parts_set, n - 1)
                        act.wait_ge(l_parts[n % 2], 16 * (n // 2))
                    bias = bq_s[:, c:c + 1] if side == 0 else bqk[:, 1, c:c + 1]
                    for dst in (v32[:, n % 2, :], parts[:, n % 2, 0, :]):
                        ins = act.activation(dst, job_bank[JOB[it] % 2][:, :], ACT.Identity, bias=bias,
                                             scale=Q_SCALE if side == 0 else 1.0)
                    ins.then_inc(job_read["A"], 1)
                elif kind == "nmax":
                    u = it[1]
                    wait_full(act, it)
                    if u >= 2:
                        act.wait_ge(l_nm[u % 2], 32 * (u // 2))
                    act.activation(nmT[:, u % 2, :], job_bank[JOB[it] % 2][:, :].bitcast(BF16)[0:2 * HG, 0:BLK],
                                   ACT.Copy).then_inc(job_read["A"], 1)
                elif kind == "qk":
                    _, u, kt, hl = it
                    m = ORD[("pv", u, kt)]
                    q0, _ = diagonal(u, kt)
                    act.wait_ge(score_full, ORD[it] + 1)
                    if m >= 2 and hl == 0:
                        act.wait_ge(pv_done, m - 1)
                    act.activation(p_t[:, m % 2, hl, q0:BLK], s_bank[ORD[it] % S_RING][:, q0:BLK],
                                   ACT.Exp).then_inc(exp_done, 1)
                elif kind == "ctxT":
                    _, tb, pr = it
                    wait_full(act, it)
                    if tb:
                        wait_full(act, ("wo", tb - 1, pr))
                    act.activation(ctxT[:, pr, :], job_bank[JOB[it] % 2][:, :], ACT.Copy).then_inc(job_read["A"], 1)
                elif kind == "h2T":
                    _, tb, pr = it
                    t0 = BLK * tb + 2 * P * pr
                    wait_full(act, it)
                    act.activation(h2T[:, :, t0:t0 + 2 * P],
                                   job_bank[JOB[it] % 2][:, :].rearrange("p (c t) -> p c t", c=DC),
                                   ACT.Copy).then_inc(job_read["A"], 1)
                elif kind == "route" and it[2] == 0:
                    act.wait_ge(nlmax_set, it[1] + 1)
                    for i in range(TPB):
                        ins = act.activation(sc_exp[:, i, :], lg[:, i, :], ACT.Exp, bias=nlmax[:, i:i + 1],
                                             accum_out=esum[:, i:i + 1])
                    ins.then_inc(sexp_set, 1)
                elif kind == "su":
                    _, tb, m = it
                    n, rn = ORD[it], SM[m][1]
                    act.wait_ge(su_full, n + 1)
                    if n >= 2:
                        act.wait_ge(hid_set, n - 1)
                    act.activation(s_sig[0:rn, n % 2, :], bank[2 * (n % 2)][0:rn, :], ACT.Silu).then_inc(sig_set, 1)

            def sigs(i, r):
                e = i * RING + r
                act.wait_ge(e_up, e + 1)
                if not (isinstance(e, int) and e < 2):
                    act.wait_ge(e_hid, e - 1)
                act.activation(sigA[r % 2][:, :], bank[2 * (r % 2)][:, 0:CAP], ACT.Silu)
                act.activation(sigB[r % 2][:, :], bank[2 * (r % 2) + 1][0:IB, 0:CAP], ACT.Silu).then_inc(e_sig, 1)

            def gates(i, r):
                e = i * RING + r
                act.wait_ge(e_staged, e + 1)
                if not (isinstance(e, int) and e < 2):
                    act.wait_ge(e_gate, e - 1)
                for s in range(SPE):
                    ins = act.activation(gate_0[r % 2][:, s, :], gb[:, 0, :], ACT.Copy, scale=wt_st[r][:, 0, s:s + 1])
                ins.then_inc(e_gate0, 1)

            def body(i):
                for r in range(RING):
                    gates(i, r)
                    sigs(i, r)

            body(0)
            with act.Fori(1, E // RING) as i:
                body(i)

        @block.vector
        def _(dve):
            chain = [0]

            def link(ins):
                chain[0] += 1
                ins.then_inc(dve_chain, 1)
                dve.wait_ge(dve_chain, chain[0])

            def split(it):
                n = ORD[it]
                wait_read(dve, it)
                v, pt = v32[:, n % 2, :], parts[:, n % 2, :, :]
                if n:
                    dve.wait_ge(parts_set, n)
                link(dve.tensor_tensor(res[:, :], v, pt[:, 0, :], ALU.subtract))
                link(dve.tensor_copy(pt[:, 1, :], res[:, :]))
                dve.tensor_tensor(pt[:, 2, :], res[:, :], pt[:, 1, :], ALU.subtract).then_inc(parts_set, 1)

            def gate_of(dst, src):
                link(dve.tensor_scalar(sign2[:, :], src, 0.0, 2.0, ALU.is_ge, ALU.mult))
                link(dve.tensor_scalar(sign[:, :], sign2[:, :], -1.0, None, ALU.add))
                link(dve.tensor_tensor(mag[:, :], src, sign[:, :], ALU.mult))
                return dve.scalar_tensor_tensor(out=dst, in0=mag[:, :], scalar=MIN_GATE, in1=sign[:, :],
                                                op0=ALU.max, op1=ALU.mult)

            def row_stats(tiles, into, n):
                if n:
                    dve.wait_ge(var_set, n)
                for i in range(TPB):
                    ins = dve.bn_stats(stats[:, i, :], x_sb[:, tiles + i, :])
                link(ins)
                for i in range(TPB):
                    ins = dve.bn_aggr(into[:, tiles + i, :], stats[:, i, :])
                ins.then_inc(var_set, 1)

            dve.wait_ge(c_exped, 1)
            link(dve.tensor_scalar(c_den[:, :], c_exp_sb[:, :], 1.0, None, ALU.add))
            link(dve.reciprocal(c_rec[:, :], c_den[:, :]))
            dve.tensor_tensor(c_act[:, :], c_sb[:, :], c_rec[:, :], ALU.mult).then_inc(c_acted, 1)
            for it in ITEMS:
                kind = it[0]
                if kind == "stat":
                    dve.wait_ge(l_x[it[1]], 16)
                    row_stats(TPB * it[1], mv, VAR[it])
                elif kind == "mod":
                    dve.wait_ge(l_const, 16 * N_CONST)
                    dve.tensor_scalar(bq_s[:, :], bqk[:, 0, :], Q_SCALE, None, ALU.mult)
                    wait_full(dve, "cT")
                    jb = job_bank[JOB["cT"] % 2]
                    dve.tensor_copy(c_rep[:, :, :], jb[:, 0:DC * B].rearrange("p (k a) -> p k a", a=1)
                                    .to_broadcast([P, DC * B, P]))
                    dve.tensor_copy(cT[:, :, :], jb[:, 0:DC * B].rearrange("p (c b) -> p c b", c=DC)).then_inc(job_read["D"], 1)
                    wait_full(dve, "gwT")
                    dve.tensor_copy(gwT[:, :, :], job_bank[JOB["gwT"] % 2][:, 0:DC * E].rearrange("p (c e) -> p c e", c=DC))\
                       .then_inc(job_read["D"], 1)
                    wait_full(dve, "modT")
                    jb = job_bank[JOB["modT"] % 2][:, 0:2 * DC * B].rearrange("p (k c b) -> p k c b", k=2, c=DC)
                    dve.tensor_copy(sa[:, :, :], jb[:, 0])
                    dve.tensor_scalar(ca1[:, :, :], jb[:, 1], 1.0, None, ALU.add).then_inc(job_read["D"], 1)
                elif kind == "row":
                    _, b, k = it
                    wait_full(dve, it)
                    jb = job_bank[JOB[it] % 2]
                    if k == 0:
                        dve.tensor_copy(sb_row[:, b, :], jb[:, D:2 * D])
                        gate_of(ga[:, b, :], jb[:, 0:D]).then_inc(job_read["D"], 1)
                    else:
                        dve.tensor_scalar(cb1[:, b, :], jb[:, 0:D], 1.0, None, ALU.add)
                        gate_of(gb[:, b, :], jb[:, D:2 * D]).then_inc(job_read["D"], 1)
                elif kind == "ln":
                    _, tb, pr = it
                    n = ORD[it]
                    dve.wait_ge(rstd_set, VAR[("stat", tb)] + 1)
                    if n >= 2:
                        wait_full(dve, ("ln", tb - 1, pr))
                    for i in range(2):
                        t = TPB * tb + 2 * pr + i
                        ins = dve.tensor_scalar(xhat[:, n % 2, i, :], x_sb[:, t, :], mv[:, t, 0:1], rstd[:, t:t + 1],
                                                ALU.subtract, ALU.mult)
                    ins.then_inc(xhat_set, 1)
                elif kind == "qkp":
                    split(it)
                elif kind == "vp":
                    _, tb, pr = it
                    wait_full(dve, it)
                    if pr == 0:
                        if tb == 0:
                            dve.wait_ge(set_up, 1)
                        if tb >= VRING:
                            dve.wait_ge(pv_done, upto("pv", lambda i: key_block(i[1], i[2]) == tb - VRING))
                    for i in range(2):
                        ins = dve.tensor_tensor(v_aug[tb % VRING][:, 2 * pr + i, :, 0:HD],
                                                job_bank[JOB[it] % 2][:, D * i:D * (i + 1)].rearrange("p (h d) -> p h d", h=H),
                                                bv_row[:, :].rearrange("p (h d) -> p h d", h=H), ALU.add)
                    ins.then_inc(job_read["D"], 1)
                elif kind == "max":
                    _, u, qt, hl, half = it
                    w = (qt + 1) * P if half == UNITS[u][1] else BLK
                    dve.wait_ge(max_full, ORD[it] + 1)
                    dve.reduce_max(rmax[:, half, qt, hl:hl + 1], m_bank[ORD[it] % M_RING][:, 0:w], AX.X).then_inc(max_read, 1)
                elif kind == "neg":
                    u = it[1]
                    dve.wait_ge(max_read, upto("max", lambda i: i[1] == u))
                    if u:
                        wait_full(dve, ("nmax", u - 1))
                    m = rmax[:, 0]
                    if UNITS[u][1]:
                        m = rmax1[:, :, :]
                        link(dve.tensor_tensor(m, rmax[:, 0], rmax[:, 1], ALU.max))
                    link(dve.tensor_scalar(nm[:, :, 0, :], m, -1.0, None, ALU.mult))
                    dve.scalar_tensor_tensor(out=nm[:, :, 1, :], in0=m, scalar=-1.0, in1=nm[:, :, 0, :],
                                             op0=ALU.mult, op1=ALU.subtract).then_inc(nm_set, 1)
                elif kind == "acc":
                    u = it[1]
                    dve.wait_ge(pv_done, upto("pv", lambda i: i[1] == u))
                    if u:
                        wait_full(dve, ("ctx", u - 1))
                    dve.tensor_copy(ctx_f[:, :], pv_bank[:, :]).then_inc(ctxf_set, 1)
                elif kind == "ctx":
                    u = it[1]
                    g = UNITS[u][2]
                    wait_full(dve, it)
                    if g == 0 and u:
                        wait_full(dve, ("ctxT", u // NG - 1, 1))
                    jb = job_bank[JOB[it] % 2][:, :].rearrange("p (t h d) -> p t h d", t=TPB, h=HG)
                    link(dve.reciprocal(ctx_r[:, :, :, :], jb[:, :, :, HD:HD + 1]))
                    dve.tensor_tensor(ctx_tok[:, :, HG * HD * g:HG * HD * (g + 1)].rearrange("p t (h d) -> p t h d", h=HG),
                                      jb[:, :, :, 0:HD], ctx_r[:, :, :, :].to_broadcast([P, TPB, HG, HD]),
                                      ALU.mult).then_inc(job_read["D"], 1)
                elif kind == "wo":
                    _, tb, pr = it
                    wait_full(dve, it)
                    dve.wait_ge(resid_set, tb + 1)
                    xs = x_sb[:, TPB * tb + 2 * pr:TPB * tb + 2 * pr + 2, :]
                    dve.tensor_tensor(xs, job_bank[JOB[it] % 2][:, :].rearrange("p (t d) -> p t d", t=2), xs,
                                      ALU.add).then_inc(job_read["D"], 1)
                elif kind == "ln2s":
                    wait_read(dve, ("wo", it[1], 1))
                    row_stats(TPB * it[1], mv2, VAR[it])
                elif kind == "ln2":
                    tb = it[1]
                    dve.wait_ge(rstd_set, VAR[("ln2s", tb)] + 1)
                    if tb:
                        dve.wait_ge(l_h2, 16 * tb)
                        wait_full(dve, ("h2T", tb - 1, 1))
                    for i in range(TPB):
                        t = TPB * tb + i
                        ins = dve.tensor_scalar(h2[:, i, :], x_sb[:, t, :], mv2[:, t, 0:1], rstd2[:, t:t + 1],
                                                ALU.subtract, ALU.mult)
                    ins.then_inc(x2hat_set, 1)
                elif kind == "gate":
                    wait_full(dve, it)
                    jb = job_bank[JOB[it] % 2][:, 0:TPB * E].rearrange("p (t e) -> p t e", t=TPB)
                    dve.tensor_copy(lg[:, :, :], jb).then_inc(job_read["D"], 1)
                    wait_read(dve, it)
                    dve.tensor_reduce(nlmax[:, :], lg[:, :, :], AX.X, ALU.max, negate=True).then_inc(nlmax_set, 1)
                elif kind == "route":
                    _, tb, n = it
                    if n:
                        dve.wait_ge(route_step, 5 * tb + n)
                    if n == 0:
                        dve.wait_ge(sexp_set, tb + 1)
                        if tb:
                            dve.wait_ge(slots_set, tb)
                        link(dve.reciprocal(rsum[:, :], esum[:, :]))
                        for i in range(TPB):
                            ins = dve.tensor_scalar(score[:, i, :], sc_exp[:, i, :], rsum[:, i:i + 1], None, ALU.mult)
                    elif n == 1:
                        for i in range(TPB):
                            ins = dve.max(top[:, i, :], score[:, i, :])
                    elif n == 2:
                        for i in range(TPB):
                            ins = dve.max_index(topi[:, i, :], top[:, i, :], score[:, i, :])
                    elif n == 3:
                        dve_copy = dve.tensor_copy(topf[:, :, :], topi[:, :, :])
                        link(dve_copy)
                        for i in range(TPB):
                            ins = dve.tensor_tensor(onehot[:, i, :, :],
                                                    iota_e[:, :].rearrange("p (a e) -> p a e", a=1).to_broadcast([P, TOPK, E]),
                                                    topf[:, i, 0:TOPK].rearrange("p (k a) -> p k a", a=1)
                                                    .to_broadcast([P, TOPK, E]), ALU.is_equal)
                    else:
                        if tb:
                            wait_full(dve, ("pos", tb - 1))
                        with nc.allow_low_precision(reason="counts up to one are exact"):
                            ins = dve.tensor_reduce(member[:, :, :], onehot[:, :, :, :].rearrange("p t k e -> p t e k"),
                                                    AX.X, ALU.add)
                    ins.then_inc(route_step, 1)
                elif kind == "pos":
                    tb = it[1]
                    wait_full(dve, it)
                    jb = job_bank[JOB[it] % 2]
                    for i in range(TPB):
                        ins = dve.tensor_tensor(onepos[:, i, :, :], onehot[:, i, :, :],
                                                jb[:, E * i:E * (i + 1)].rearrange("p (a e) -> p a e", a=1)
                                                .to_broadcast([P, TOPK, E]), ALU.mult)
                    ins.then_inc(job_read["D"], 1)
                    wait_read(dve, it)
                    dve.tensor_reduce(posk[:, :, :], onepos[:, :, :, :], AX.X, ALU.add).then_inc(ranks_set, 1)
                elif kind == "su":
                    _, tb, m = it
                    n, rn = ORD[it], SM[m][1]
                    dve.wait_ge(sig_set, n + 1)
                    if m == 0 and tb >= 2:
                        dve.wait_ge(sd_full, 2 * (tb - 1))
                    dve.tensor_tensor(s_hid[0:rn, tb % 2, m, :], s_sig[0:rn, n % 2, :], bank[2 * (n % 2) + 1][0:rn, :],
                                      ALU.mult).then_inc(hid_set, 1)
                elif kind == "sd":
                    _, tb, pr = it
                    n = ORD[it]
                    dve.wait_ge(sd_full, n + 1)
                    if n >= 2:
                        dve.wait_ge(l_y[n % 2], 16 * (n // 2))
                    wait_read(dve, ("wo", tb, 1))
                    if n:
                        dve.wait_ge(y_set, n)
                    for i in range(2):
                        ins = dve.tensor_tensor(y_init[:, n % 2, i, :], bank[4 + n % 2][:, D * i:D * (i + 1)],
                                                gb[:, tb // 2, :], ALU.mult)
                    link(ins)
                    t = TPB * tb + 2 * pr
                    dve.tensor_tensor(y_init[:, n % 2, :, :], y_init[:, n % 2, :, :], x_sb[:, t:t + 2, :],
                                      ALU.add).then_inc(y_set, 1)
            dve.wait_ge(l_tab, 16)
            link(dve.tensor_scalar(tab_w[:, 1, :], tab[:, :, 0], float(S), None, ALU.is_ge))
            link(dve.tensor_tensor(tab_w[:, 1, :], tab_w[:, 1, :], tab[:, :, 1], ALU.mult))
            dve.tensor_tensor(tab_w[:, 0, :], tab[:, :, 1], tab_w[:, 1, :], ALU.subtract)
            dve.tensor_copy(tab_ix[:, :], tab[:, :, 0]).then_inc(tabix_set, 1)

            def keep_xT(i, r):
                e = i * RING + r
                dve.wait_ge(e_turned, e + 1)
                if not (isinstance(e, int) and e < 2):
                    dve.wait_ge(e_up, e - 1)
                dve.tensor_copy(xgT[r % 2][:, :, :], bank[6 + r % 2][:, :].rearrange("p (c t) -> p c t", c=DC))\
                   .then_inc(e_xT, 1)

            def hids(i, r):
                e = i * RING + r
                dve.wait_ge(e_sig, e + 1)
                if not (isinstance(e, int) and e < 2):
                    dve.wait_ge(e_down, e - 1)
                dve.tensor_tensor(hidA[r % 2][:, :], sigA[r % 2][:, :], bank[2 * (r % 2)][:, CAP:2 * CAP], ALU.mult)
                dve.tensor_tensor(hidB[r % 2][:, :], sigB[r % 2][:, :], bank[2 * (r % 2) + 1][64:64 + IB, 0:CAP],
                                  ALU.mult).then_inc(e_hid, 1)

            def gates(i, r):
                e = i * RING + r
                dve.wait_ge(e_gate0, e + 1)
                if not (isinstance(e, int) and e < 2):
                    dve.wait_ge(e_ob, e - 1)
                for s in range(SPE):
                    ins = dve.scalar_tensor_tensor(out=gate_w_sb[r % 2][:, s, :], in0=gb[:, 1, :], scalar=wt_st[r][:, 1, s:s + 1],
                                                   in1=gate_0[r % 2][:, s, :], op0=ALU.mult, op1=ALU.add)
                ins.then_inc(e_gate, 1)

            def weigh(i, r):
                e = i * RING + r
                dve.wait_ge(e_down, e + 1)
                dve.wait_ge(e_gate, e + 1)
                if not (isinstance(e, int) and e < 2):
                    dve.wait_ge(e_added, 16 * SPE * (e - 1))
                dve.tensor_tensor(ob[r % 2][:, :, :], bank[4 + r % 2][:, :].rearrange("p (s d) -> p s d", s=SPE),
                                  gate_w_sb[r % 2][:, :, :], ALU.mult).then_inc(e_ob, 1)

            keep_xT(0, 0)

            def body(i, first=False, last=False):
                for r in range(RING):
                    if not (last and r == RING - 1):
                        keep_xT(i + (r + 1) // RING, (r + 1) % RING)
                    gates(i, r)
                    hids(i, r)
                    if not (first and r == 0):
                        weigh(i if r else i - 1, (r - 1) % RING)

            body(0, first=True)
            with dve.Fori(1, E // RING - 1) as i:
                body(i)
            body(E // RING - 1, last=True)
            weigh(E // RING - 1, RING - 1)

        @block.gpsimd
        def _(pool):
            chain = [0]

            def link(ins):
                chain[0] += 1
                ins.then_inc(pool_chain, 1)
                pool.wait_ge(pool_chain, chain[0])

            link(pool.memset(neg_half[:, :], -0.5))
            pool.memset(before[:, 0, :], 0.0)
            for v in v_aug:
                pool.memset(v[:, :, :, HD:VW], 1.0)
            pool.memset(zero_b[:, :], 0.0).then_inc(set_up, 1)
            for it in ITEMS:
                kind = it[0]
                if kind in ("stat", "ln2s"):
                    into, mvx = (rstd, mv) if kind == "stat" else (rstd2, mv2)
                    t = slice(TPB * it[1], TPB * (it[1] + 1))
                    pool.wait_ge(var_set, VAR[it] + 1)
                    link(pool.tensor_scalar(var_e[:, t], mvx[:, t, 1], 1.0, EPS, ALU.mult, ALU.add))
                    pool.tensor_tensor(into[:, t], var_e[:, t], neg_half[:, :], ALU.pow).then_inc(rstd_set, 1)
                elif kind == "ln2":
                    tb = it[1]
                    pool.wait_ge(x2hat_set, tb + 1)
                    h2b = lambda v: v[:, tb // 2:tb // 2 + 1, :].to_broadcast([P, TPB, D])
                    link(pool.tensor_tensor(h2[:, :, :], h2[:, :, :], h2b(cb1), ALU.mult))
                    pool.tensor_tensor(h2[:, :, :], h2[:, :, :], h2b(sb_row), ALU.add).then_inc(h2_set, 1)
                elif kind == "wog":
                    wait_read(pool, ("row", B - 1, 1))
                    pool.wait_ge(l_wvo, 32)
                    for b in range(B):
                        for c in range(DC):
                            pool.tensor_tensor(wo_g[:, b, c, :], wo_sb[:, c, :], ga[:, b, :], ALU.mult)
                        ins = pool.tensor_tensor(ga_bo[:, b, :], bo_row[:, :], ga[:, b, :], ALU.mult)
                    ins.then_inc(wo_scaled, 1)
                    pool.wait_ge(wo_scaled, 1)
                    pool.wait_ge(xhat_set, 2)
                    for i in range(TPB):
                        ins = pool.tensor_tensor(x_sb[:, i, :], x_sb[:, i, :], ga_bo[:, 0, :], ALU.add)
                    ins.then_inc(resid_set, 1)
                elif kind == "resid" and it[1]:
                    tb = it[1]
                    pool.wait_ge(xhat_set, 2 * (tb + 1))
                    for i in range(TPB):
                        t = TPB * tb + i
                        ins = pool.tensor_tensor(x_sb[:, t, :], x_sb[:, t, :], ga_bo[:, tb // 2, :], ALU.add)
                    ins.then_inc(resid_set, 1)
                elif kind == "rank":
                    tb = it[1]
                    pool.wait_ge(route_step, 5 * (tb + 1))
                    for i in range(TPB):
                        t = TPB * tb + i
                        ins = pool.tensor_tensor(before[:, t + 1, :], before[:, t, :], member[:, i, :], ALU.add)
                        if i < TPB - 1:
                            link(ins)
                    ins.then_inc(member_set, 1)
                elif kind == "pos":
                    tb = it[1]
                    pool.wait_ge(ranks_set, tb + 1)
                    pool.wait_ge(member_set, tb + 1)
                    link(pool.tensor_scalar(upper[:, :, :], posk[:, :, :], float(P), float(1 - P * SPT), ALU.is_ge, ALU.mult))
                    link(pool.tensor_scalar(addr[:, :, :], posk[:, :, :], float(SPT), None, ALU.mult))
                    link(pool.tensor_tensor(addr[:, :, :], addr[:, :, :], upper[:, :, :], ALU.add))
                    link(pool.tensor_scalar(upper[:, :, :], posk[:, :, :], float(CAP), float(2 * SLOTS), ALU.is_ge, ALU.mult))
                    link(pool.tensor_tensor(addr[:, :, :], addr[:, :, :], upper[:, :, :], ALU.add))
                    link(pool.tensor_scalar(upper[:, :, :], topf[:, :, 0:TOPK], float(SPE), None, ALU.mult))
                    link(pool.tensor_tensor(addr[:, :, :], upper[:, :, :], addr[:, :, :], ALU.add))
                    pool.tensor_copy(slot_ix[:, tb, :, :], addr[:, :, :])
                    pool.tensor_copy(payload[:, tb, :, :, 1], top[:, :, 0:TOPK])
                    pool.tensor_copy(payload[:, tb, :, :, 0],
                                     tok_id[:, TPB * tb:TPB * (tb + 1)].rearrange("p (t a) -> p t a", a=1)
                                     .to_broadcast([P, TPB, TOPK])).then_inc(slots_set, 1)
                    pool.wait_ge(slots_set, tb + 1)
                    pool.wait_ge(l_init, 48)
                    for i in range(TPB):
                        for k in range(TOPK):
                            pool.indirect_dma_start(
                                slot_table, bass.IndirectOffsetOnAxis(ap=slot_ix[:, tb, i, k:k + 1], axis=0),
                                payload[:, tb, i, k, :], None, bounds_check=SLOTS - 1, oob_is_err=False).then_inc(l_scat, 16)
                elif kind == "su" and ORD[it] == 0:
                    pool.wait_ge(l_sw, 16 * (2 + len(SM)))
                    for r in range(RING):
                        ins = pool.memset(w13_sb[r][:, 0:DC * W13].rearrange("p (c n) -> p c n", c=DC)[:, :, COL_B + IB:COL_B + 64], 0.0)
                    ins.then_inc(pads_set, 1)
            pool.wait_ge(tabix_set, 1)
            pool.wait_ge(l_h2, 16 * NB)
            for i in range(2):
                pool.wait_ge(l_y[i], 16 * total["sd"] // 2)

            def stage(i, r):
                e = i * RING + r
                if not (isinstance(e, int) and e < RING):
                    pool.wait_ge(e_turned, e - RING + 1)
                    pool.wait_ge(e_gate, e - RING + 1)
                pool.sem_inc(pool_at, 1)
                pool.tensor_copy(wt_st[r][:, :, :], tab_w[:, :, bass.ds(SPE * e, SPE)])
                pool.tensor_copy(idx_st[r][:, :], tab_ix[:, bass.ds(SPE * e, SPE)]).then_inc(e_staged, 1)
                pool.wait_ge(e_staged, e + 1)
                pool.sem_inc(pool_at, 1)
                for s in range(SPE):
                    pool.indirect_dma_start(xg[r][:, s, :], None, h2_rows,
                                            bass.IndirectOffsetOnAxis(ap=idx_st[r][:, s:s + 1], axis=0)).then_inc(e_x[r], 16)

            def add(i, r):
                e = i * RING + r
                pool.wait_ge(e_ob, e + 1)
                if not (isinstance(e, int) and e < 1):
                    pool.wait_ge(e_added, 16 * SPE * e)
                pool.sem_inc(pool_at, 1)
                pool.tensor_copy(idx_add[r % 2][:, :], tab_ix[:, bass.ds(SPE * e, SPE)]).then_inc(add_ix, 1)
                pool.wait_ge(add_ix, e + 1)
                pool.sem_inc(pool_at, 1)
                for s in range(SPE):
                    pool.indirect_dma_start(out, bass.IndirectOffsetOnAxis(ap=idx_add[r % 2][:, s:s + 1], axis=0),
                                            ob[r % 2][:, s, :], None, compute_op=ALU.add).then_inc(e_added, 16)

            AHEAD = 3
            for r in range(AHEAD):
                stage(0, r)

            def body(i, first=False, last=False):
                for r in range(RING):
                    if not (last and r >= RING - AHEAD):
                        stage(i + (r + AHEAD) // RING, (r + AHEAD) % RING)
                    if not (first and r == 0):
                        add(i if r else i - 1, (r - 1) % RING)

            body(0, first=True)
            with pool.Fori(1, E // RING - 1) as i:
                body(i)
            body(E // RING - 1, last=True)
            add(E // RING - 1, RING - 1)


def constants():
    bf = np.dtype("bfloat16")
    slope = np.float32(2.0 ** (-8.0 / H)) ** np.arange(1, H + 1, dtype=np.float32)
    bias = slope[:, None] * np.arange(1 - S, 1, dtype=np.float32)[None, :]
    alibi = []
    for _ in range(3):
        alibi.append(bias.astype(bf))
        bias = bias - alibi[-1].astype(np.float32)
    q, k = np.arange(P)[:, None], np.arange(P)[None, :]
    masks = np.stack([np.where(k > q, NEG, 0.0), np.where(q > k, NEG, 0.0), (q == k) * 1.0]).astype(bf)
    tri = np.stack([(q < k) * 1.0, np.ones((P, P))], axis=1).astype(bf)
    slot = np.zeros((P, E, SPE, 2), np.float32)
    slot[..., 0] = T + np.arange(SPE)[None, None, :] * P + np.arange(P)[:, None, None]
    return {
        "alibi": np.stack(alibi), "ones_rows": np.ones((3, HG, S), bf), "zero_row": np.zeros((1, D), np.float32),
        "masks": masks, "ident": np.eye(P, dtype=np.float32)[None], "tri": tri,
        "iota": np.tile(np.arange(E, dtype=np.float32), (P, 1)),
        "tok": (np.arange(P)[:, None] + P * np.arange(NT)[None, :]).astype(np.float32),
        "slot_init": slot.reshape(SLOTS, 2),
    }


_INS = ["L0_attn_x", "L0_attn_Wq", "L0_attn_bq", "L0_attn_Wk", "L0_attn_bk", "L0_attn_Wv", "L0_attn_bv", "L0_attn_Wo",
        "L0_attn_bo", "L0_ffn_gate_w", "L0_ffn_w1", "L0_ffn_w2", "L0_ffn_w3", "L0_ffn_sw1", "L0_ffn_sw2", "L0_ffn_sw3",
        "L0_c", "L0_wmod"]


def kernel(**inputs):
    import numpy as _np
    import concourse.bacc as _bacc
    from concourse import mybir as _mybir
    from concourse.bass_utils import run_bass_kernel_spmd as _run

    nc = _bacc.Bacc("TRN2", target_bir_lowering=False, num_devices=1)
    arrays, args = {}, []
    data = {n: _np.asarray(inputs[n]) for n in _INS}
    data["L0_attn_x"] = data["L0_attn_x"].reshape(T, D)
    for name, a in {**data, **constants()}.items():
        a = _np.ascontiguousarray(a)
        arrays[f"in_{name}"] = a
        args.append(nc.dram_tensor(f"in_{name}", a.shape, _mybir.dt.from_np(a.dtype), kind="ExternalInput").ap())
    args.append(nc.dram_tensor("out_0", (T + CAP, D), _mybir.dt.float32, kind="ExternalOutput").ap())
    adaln_kernel(nc, *args)
    r = _run(nc, [arrays], core_ids=[0])
    return r.results[0]["out_0"][0:T].reshape(B, S, D)
```

```python
from contextlib import ExitStack

import numpy as np

import concourse.bass as bass
from concourse import mybir

F32 = mybir.dt.float32
BF16 = mybir.dt.bfloat16
U32 = mybir.dt.uint32
ALU = mybir.AluOpType
ACT = mybir.ActivationFunctionType
AX = mybir.AxisListType

P = 128
B, S, D = 2, 1024, 256
T = B * S
NT = T // P
BLK = 512
NB = T // BLK
TPB = BLK // P
H, HD = 16, 16
HG = 4
NG = H // HG
DC = D // P
E, TOPK, CAP, INTER = 32, 6, 256, 176
IB = INTER - P
SI = 2 * INTER
SM = [(0, 128), (128, 128), (256, SI - 256)]
NMOD = 6
NEG = -1.0e30
EPS = 1e-5
MIN_GATE = 0.25
Q_SCALE = float(HD) ** -0.5
VW = HD + 1
NPARTS = 3
ROW_OF_KPART = (0, 3, 5)
NPROD = 6
ROW_ALIBI = NPROD * HD
ROW_NMAX = ROW_ALIBI + 3
K_MAX = ROW_NMAX
K_EXP = ROW_NMAX + 2
SLOTS = E * CAP
SPT = SLOTS // P
SPE = CAP // P
RING = 4
COL_B = 2 * P
W13 = COL_B + 64 + IB
STACKS, VRING = 3, 3
NBANKS = 7

UNITS = [(b, qb, g) for b in range(B) for qb in range(S // BLK) for g in range(NG)]
NU = len(UNITS)


MAX_TILES, EXP_TILES, JOB_TILES = 4, 3, 3
PE_FIXED, DVE_FIXED, ACT_FIXED = 0.04, 0.12, 0.1
ACT_LATENCY = 0.4
EXTRA_GAP = 0.5
FILL_COST = 1.0
EARLY_SHARED = 1
CHAIN_FIRST = 1.5



class Clocks:

    def __init__(self):
        self.free = dict.fromkeys(("PE", "ACT", "DVE", "POOL", "SP"), 0.0)
        self.at = {}
        self.parts = []
        self.ring = {}
        self.banks, self.user, self.bank_of = [0.0] * NBANKS, [None] * NBANKS, {}

    def steps(self, it):
        kind = it[0]
        if kind in ("max", "qk", "pv"):
            w = self.width(it)
            if kind == "max":
                return [("PE", PE_FIXED + 0.42e-3 * w, 0.2), ("DVE", DVE_FIXED + 1.05e-3 * w, 0.1)]
            if kind == "qk":
                return [("PE", PE_FIXED + 0.42e-3 * w, 0.2), ("ACT", ACT_FIXED + 0.82e-3 * w, ACT_LATENCY)]
            return [("PE", 1.9e-3 * w, 0.2)]
        return {
            "neg": [("DVE", 0.6, 0.2)], "nmax": [("PE", 0.25, 0.2), ("ACT", 0.5, 0.2), ("SP", 1.2, 2.5)],
            "acc": [("ACT", 0.55, 0.2)], "ctx": [("PE", 0.25, 0.2), ("DVE", 0.7, 0.2)],
            "stk": [("SP", 3.5 + 1.5 * (UNITS[it[1]][1] if kind == "stk" else 0), 2.5)],
            "stat": [("DVE", 1.7, 0.2), ("POOL", 1.2, 0.2)], "ln2s": [("DVE", 1.7, 0.2), ("POOL", 1.2, 0.2)],
            "ln": [("DVE", 0.7, 0.2), ("PE", 0.25, 0.2), ("ACT", 0.9, 0.2)], "resid": [("POOL", 2.7, 0.2)],
            "qkp": [("PE", 1.75, 0.2), ("ACT", 1.15, 0.2), ("DVE", 1.8, 0.2), ("SP", 0.6, 2.2)],
            "vp": [("PE", 1.75, 0.2), ("DVE", 0.7, 0.2)], "row": [("PE", 1.75, 0.2), ("DVE", 1.9, 0.2)],
            "wog": [("POOL", 7.0, 0.2)], "ctxT": [("PE", 0.25, 0.2), ("ACT", 0.5, 0.2)],
            "wo": [("PE", 1.75, 0.2), ("DVE", 0.7, 0.2)],
            "ln2": [("DVE", 1.4, 0.2), ("POOL", 4.5, 0.2)], "h2T": [("PE", 0.25, 0.2), ("ACT", 0.5, 0.2)],
            "gate": [("PE", 0.7, 0.2), ("DVE", 0.5, 0.2)], "route": [("DVE", 1.2, 0.3)],
            "rank": [("POOL", 1.0, 0.2)], "pos": [("PE", 0.4, 0.2), ("DVE", 1.8, 0.2), ("POOL", 26.0, 2.0)],
            "sg": [("PE", 1.75, 0.2), ("ACT", 0.6, 0.2), ("DVE", 0.7, 0.2)], "sm": [("PE", 1.75, 0.2), ("DVE", 0.7, 0.2)],
            "sd": [("PE", 2.6, 0.2), ("DVE", 1.5, 0.2)], "free": [("SP", 12.0, 2.5)], "sw": [("SP", 3.0, 2.5)],
        }[kind]

    @staticmethod
    def width(it):
        u = it[1]
        if it[0] == "max":
            return (it[2] + 1) * P if it[4] == UNITS[u][1] else BLK
        return BLK - max(0, it[2] - TPB * UNITS[u][1]) * P

    def needs(self, it):
        kind, u = it[0], it[1] if len(it) > 1 else 0
        tb = u
        if kind == "max":
            return [("stk", u)]
        if kind == "qk":
            return [("nmax", u)]
        if kind == "pv":
            return [("qk", u, it[2], HG - 1)] + ([("acc", u - 1)] if it[2] == 0 else [])
        if kind == "neg":
            return [("max", u, TPB - 1, HG - 1, UNITS[u][1])]
        if kind == "route":
            return [("route", tb, it[2] - 1)] if it[2] else [("gate", tb)]
        if kind == "acc":
            return [("pv", u, TPB * (UNITS[u][1] + 1) - 1)]
        return {"nmax": [("neg", u)], "ctx": [("acc", u)], "stk": [("qkp", u // NG, 1, DC - 1),
                        ("qk", u - STACKS, TPB * (UNITS[u - STACKS][1] + 1) - 1, HG - 1)],
                "ln": [("stat", tb)], "qkp": [("ln", tb, 1)], "vp": [("ln", tb, 1)],
                "ctxT": [("ctx", NG * tb + NG - 1)], "wo": [("ctxT",) + it[1:]], "ln2s": [("wo", tb, 1)],
                "ln2": [("ln2s", tb)], "h2T": [("ln2", tb)], "gate": [("h2T", tb, 1)],
                "rank": [("route", tb, 4)], "pos": [("rank", tb)], "sg": [("h2T", tb, 1)], "sm": [("sg",) + it[1:]],
                "sd": [("sm", tb, len(SM) - 1)]}.get(kind, [])

    RINGS = {"max": "M", "qk": "S"}
    DEPTH = {"M": MAX_TILES, "S": EXP_TILES, "job": JOB_TILES}

    def run(self, it, commit):
        free = self.free if commit else dict(self.free)
        ready = max([self.at.get(n, 0.0) for n in self.needs(it)] + [0.0])
        kind = it[0]
        ring = self.RINGS.get(kind)
        if kind in ("nmax", "ctx", "ln", "qkp", "vp", "row", "ctxT", "wo", "h2T", "gate", "pos", "sg", "sm", "sd"):
            ring = "job"
        uses = self.ring.setdefault(ring, []) if ring in self.DEPTH else None
        stall, lost = 0.0, 0.0
        for n, (engine, cost, latency) in enumerate(self.steps(it)):
            if kind == "qkp" and engine == "ACT" and len(self.parts) > 1:
                ready = max(ready, self.parts[-2])
            if engine == "PE" and uses is not None:
                k = min(range(NBANKS), key=lambda i: self.banks[i])
                ready = max(ready, self.banks[k])
                if len(uses) >= self.DEPTH[ring]:
                    ready = max(ready, uses[-self.DEPTH[ring]])
            now = max(free["PE"], free[engine]) if engine in ("ACT", "DVE") else free[engine]
            if engine in ("PE", "ACT", "DVE"):
                lost = max(0.0, ready - now)
                stall = max(stall, lost if engine == "PE" or n == 0 else lost - 1.0)
            start = max(free[engine], ready)
            free[engine] = start + cost
            ready = start + cost + latency
            if n < 2 or kind in ("ln", "sg"):
                bank_read = ready
        if commit:
            self.at[it] = ready
            if kind == "qkp":
                self.parts.append(ready)
            if uses is not None:
                uses.append(bank_read)
                self.bank_of[it] = k, self.user[k]
                self.banks[k], self.user[k] = bank_read, it
        return stall


def plan():

    def maxes(u):
        return [("max", u, qt, hl, half) for qt in range(TPB) for hl in range(HG)
                for half in range(UNITS[u][1] + 1)] + [("neg", u), ("nmax", u)]

    def exps(u):
        n, out = TPB * (UNITS[u][1] + 1), []
        for kt in range(n + 1):
            if kt < n:
                out += [("qk", u, kt, hl) for hl in range(HG)]
            if kt:
                out.append(("pv", u, kt - 1))
        return out + [("acc", u)]

    def normed(tb):
        return [("ln", tb, pr) for pr in range(2)] + [("resid", tb)]

    def project(tb):
        return [("qkp", tb, s, c) for c in range(DC) for s in range(2)] + [("vp", tb, pr) for pr in range(2)]

    def close_x(tb):
        return [("ctxT", tb, 0), ("ctxT", tb, 1), ("wo", tb, 0), ("wo", tb, 1), ("ln2s", tb), ("ln2", tb)]

    def close_h(tb):
        return [("h2T", tb, 0), ("h2T", tb, 1), ("gate", tb)]

    def close_r(tb):
        return [("route", tb, n) for n in range(5)] + [("rank", tb), ("pos", tb)]

    def shared(tb):
        return [(k, tb, m) for m in range(len(SM)) for k in ("sg", "sm")] + [("sd", tb, pr) for pr in range(2)]

    clocks, items = Clocks(), []

    def straight(part):
        for it in part:
            if it[0] != "mod":
                clocks.run(it, True)
                continue
            for k, name in enumerate(("cT", "gwT", "modT")):
                clocks.bank_of[name], clocks.user[k], clocks.banks[k] = (k, None), name, clocks.free["DVE"]
        items.extend(part)

    start, rows = project(0), [("row", b, k) for b in range(B) for k in range(2)]
    straight([("stat", 0), ("mod",)] + normed(0) + start[:4] + [("stk", 0), ("stat", 1)] + rows + start[4:]
             + [("wog",), ("sw",), ("stk", 1)])
    extras = [(0, it) for it in normed(1) + project(1)[:4] + [("stk", 2)] + project(1)[4:]
              + [("stat", 2), ("stat", 3)]]
    for u in range(1, NU):
        tb, step = u // NG, u % NG
        extra = [("ctx", u - 1)] + ([("stk", u + 2)] if u + 2 < NU else [])
        if step == 0:
            extra += close_x(tb - 1) + (normed(tb + 1) if tb + 1 < NB else [])
        if step == 1 and tb:
            extra += (project(tb + 1) if tb + 1 < NB else []) + close_h(tb - 1)
        if step == 2 and tb:
            extra += close_r(tb - 1)
        extras += [(u, it) for it in extra]
    unit_of = dict((it, u) for u, it in extras)
    streams = [[x for u in range(NU) for x in maxes(u)], [x for u in range(NU) for x in exps(u)],
               [it for _, it in extras], [x for tb in range(EARLY_SHARED) for x in shared(tb)]]
    MAXIMA, EXPONENTIALS, EXTRAS, SHARED = range(len(streams))
    placed, now, extra_at = set(items), 0, 0.0

    def may_stand(n, it):
        if n == MAXIMA:
            return it[0] != "max" or ("stk", it[1]) in placed
        if n == EXPONENTIALS:
            return not (it[0] == "qk" and ("nmax", it[1]) not in placed
                        or it[0] == "acc" and it[1] and ("ctx", it[1] - 1) not in placed)
        if n == SHARED:
            return ("sw",) in placed and ("h2T", it[1], 1) in placed
        return now >= unit_of[it] and all(x in placed for x in clocks.needs(it) if x[0] == "acc")

    while any(streams[:SHARED]):
        choices = []
        for n, s in enumerate(streams):
            if s and may_stand(n, s[0]):
                due = n == EXTRAS and ("nmax", 0) in placed and clocks.free["PE"] - extra_at > EXTRA_GAP
                stall = round(max(0.0, clocks.run(s[0], False)), 1)
                choices.append((stall + (FILL_COST if n == SHARED else 0.0), -1 if due else n, n))
        n = min(choices)[2]
        it = streams[n].pop(0)
        clocks.run(it, True)
        if n == EXTRAS:
            extra_at = clocks.free["PE"]
        if it[0] == "qk":
            now = it[1]
        items.append(it)
        placed.add(it)
    last = NB - 1
    straight([("ctx", NU - 1), ("free",)])
    chain = close_x(last) + close_h(last) + close_r(last)
    others = streams[SHARED] + [x for tb in range(EARLY_SHARED, NB) for x in shared(tb)]
    while chain or others:
        s = chain if chain and (not others or clocks.run(chain[0], False) < CHAIN_FIRST) else others
        if s is others and others[0][1] == last and ("h2T", last, 1) in chain:
            s = chain
        if s is others and others[0] == ("sd", last, 0) and ("tab",) not in items:
            items.append(("tab",))
        it = s.pop(0)
        clocks.run(it, True)
        items.append(it)
    return items, clocks.bank_of


def load_expert(sp, e, w1, w3, w2, w13_slot, w2_slot, loaded):
    w13 = w13_slot[:, 0:DC * W13].rearrange("p (c n) -> p c n", c=DC)
    for w, k in ((w1, 0), (w3, 1)):
        src = w[bass.ds(e, 1)].rearrange("e (c p) i -> p (e c) i", p=P)
        sp.dma_start(w13[:, :, P * k:P * (k + 1)], src[:, :, 0:P]).then_inc(loaded, 16)
        sp.dma_start(w13[:, :, COL_B + 64 * k:COL_B + 64 * k + IB], src[:, :, P:INTER]).then_inc(loaded, 16)
    sp.dma_start(w2_slot[:, 0, :], w2[bass.ds(e, 1), 0:P, :].rearrange("e p d -> (e p) d")).then_inc(loaded, 16)
    sp.dma_start(w2_slot[0:IB, 1, :], w2[bass.ds(e, 1), P:INTER, :].rearrange("e p d -> (e p) d")).then_inc(loaded, 16)


LOADS_PER_EXPERT = 6


def adaln_kernel(nc, x, Wq, bq, Wk, bk, Wv, bv, Wo, bo, gate_w, w1, w2, w3, sw1, sw2, sw3, c_in, wmod,
                 alibi, ones_rows, zero_row, masks, ident_in, tri_in, iota_in, tok_in, slot_init, out):
    ITEMS, BANK_OF = plan()
    ORD, total = {}, {}
    for it in ITEMS:
        ORD[it] = total.get(it[0], 0)
        total[it[0]] = ORD[it] + 1
    VAR = {it: n for n, it in enumerate(i for i in ITEMS if i[0] in ("stat", "ln2s"))}
    READER = {"ln": "A", "qkp": "A", "vp": "D", "nmax": "A", "ctx": "D", "ctxT": "A", "wo": "D",
              "h2T": "A", "gate": "D", "pos": "D", "row": "D", "sg": "D", "sm": "D", "sd": "D"}
    jobs = []
    for it in ITEMS:
        if it[0] == "mod":
            jobs += [("cT", "D"), ("gwT", "D"), ("modT", "D")]
        if it[0] in READER:
            jobs.append((it, READER[it[0]]))
    JOB = {n: j for j, (n, _) in enumerate(jobs)}
    seen, READ = {"A": 0, "D": 0}, []
    for _, r in jobs:
        seen[r] += 1
        READ.append((r, seen[r]))

    def upto(kind, accepts):
        return max(ORD[it] + 1 for it in ITEMS if it[0] == kind and accepts(it))

    def stack_loads(u):
        return NPARTS * (2 + UNITS[u][1]) + 1

    def key_block(u, kt):
        return 2 * UNITS[u][0] + kt // TPB

    def diagonal(u, kt):
        j = kt - TPB * UNITS[u][1]
        return (j * P, True) if j >= 0 else (0, False)

    ctx = ExitStack()
    with ctx:
        def sb(name, shape, dt=F32):
            return ctx.enter_context(nc.sbuf_tensor(name, shape, dt))

        def sem(name):
            return ctx.enter_context(nc.semaphore(name))

        q_parts, k_parts = ([nc.dram_tensor(f"{n}_parts{i}", [NPARTS, NG * HD, HG, BLK], BF16, kind="Internal").ap()
                             for i in range(NB)] for n in "qk")
        h2_rows = nc.dram_tensor("h2_rows", [T + CAP, D], F32, kind="Internal").ap()
        slot_table = nc.dram_tensor("slot_table", [SLOTS, 2], F32, kind="Internal").ap()

        bank = [ctx.enter_context(nc.psum_tensor(f"bank{i}", [P, 512], F32)) for i in range(8)]
        pv_bank = bank[NBANKS]

        ident = sb("ident", [P, P])
        identb = sb("identb", [P, P], BF16)
        mask_qk = sb("mask_qk", [P, 2, P], BF16)
        tri = sb("tri", [P, 2, P], BF16)
        iota_e = sb("iota_e", [P, E])
        tok_id = sb("tok_id", [P, NT])
        neg_half = sb("neg_half", [P, TPB])
        zero_b = sb("zero_b", [P, BLK], BF16)
        wo_sb = sb("wo_sb", [P, DC, D])
        wo_g = sb("wo_g", [P, B, DC, D])
        bqk = sb("bqk", [P, 2, DC])
        bq_s = sb("bq_s", [P, DC])
        bv_row, bo_row = sb("bv_row", [P, D]), sb("bo_row", [P, D])
        gw_in = sb("gw_in", [E, D])
        gwT = sb("gwT", [P, DC, E])
        c_sb, c_exp_sb, c_den, c_rec, c_act = (sb(n, [B, D]) for n in ("c_sb", "c_exp_sb", "c_den", "c_rec", "c_act"))
        cT = sb("cT", [P, DC, B])
        sa, ca1 = sb("sa", [P, DC, B]), sb("ca1", [P, DC, B])
        ga, sb_row, cb1, gb, ga_bo = (sb(n, [P, B, D]) for n in ("ga", "sb_row", "cb1", "gb", "ga_bo"))
        sign2, sign, mag = (sb(n, [P, D]) for n in ("sign2", "sign", "mag"))
        x_sb = sb("x_sb", [P, NT, D])
        stats = sb("stats", [P, TPB, 6])
        mv, mv2 = sb("mv", [P, NT, 2]), sb("mv2", [P, NT, 2])
        var_e, rstd, rstd2 = sb("var_e", [P, NT]), sb("rstd", [P, NT]), sb("rstd2", [P, NT])
        ctx_tok = sb("ctx_tok", [P, TPB, D])
        ctxT = sb("ctxT", [P, 2, 2 * DC * P])
        h2 = sb("h2", [P, TPB, D])
        h2T = sb("h2T", [P, DC, T])
        nlmax, esum, rsum = (sb(n, [P, TPB]) for n in ("nlmax", "esum", "rsum"))
        top = sb("top", [P, TPB, 8])
        topi = sb("topi", [P, TPB, 8], U32)
        topf = sb("topf", [P, TPB, 8])
        onehot = sb("onehot", [P, TPB, TOPK, E])
        onepos = sb("onepos", [P, TPB, TOPK, E])
        member = sb("member", [P, TPB, E], BF16)
        before = sb("before", [P, NT + 1, E], BF16)
        posk, addr, upper = (sb(n, [P, TPB, TOPK]) for n in ("posk", "addr", "upper"))
        slot_ix = sb("slot_ix", [P, NB, TPB, TOPK], U32)
        payload = sb("payload", [P, NB, TPB, TOPK, 2])
        tab = sb("tab", [P, SPT, 2])
        tab_ix = sb("tab_ix", [P, SPT], U32)
        tab_w = sb("tab_w", [P, B, SPT])

        with ExitStack() as early:
            wm = early.enter_context(nc.sbuf_tensor("wm", [P, DC, NMOD * D], F32))
            c_rep = early.enter_context(nc.sbuf_tensor("c_rep", [P, DC * B, P], F32))
        sw1_sb, sw3_sb = sb("sw1_sb", [P, DC, SI]), sb("sw3_sb", [P, DC, SI])
        sw2_sb = sb("sw2_sb", [P, len(SM), D])
        y_init = sb("y_init", [P, 2, 2, D])
        s_act, s_hid = sb("s_act", [P, 2, BLK]), sb("s_hid", [P, len(SM), BLK])
        lg, sc_exp, score = (sb(n, [P, TPB, E]) for n in ("lg", "sc_exp", "score"))

        with ExitStack() as first:
            def sb1(name, shape, dt=F32):
                return first.enter_context(nc.sbuf_tensor(name, shape, dt))

            wq_sb, wk_sb, wv_sb = (sb1(n, [P, DC, D]) for n in ("wq_sb", "wk_sb", "wv_sb"))
            hT = sb1("hT", [P, DC, BLK])
            xhat = sb1("xhat", [P, 2, 2, D])
            v32 = sb1("v32", [P, 2, BLK])
            res = sb1("res", [P, BLK])
            parts = sb1("parts", [P, 2, 3, BLK], BF16)
            q_stack = [sb1(f"q_stack{i}", [P, HG, BLK], BF16) for i in range(STACKS)]
            k_stack = [sb1(f"k_stack{i}", [P, S // BLK, HG, BLK], BF16) for i in range(STACKS)]
            v_aug = [sb1(f"v_aug{i}", [P, TPB, H, VW]) for i in range(VRING)]
            p_t = sb1("p_t", [P, 2, HG, BLK])
            rmax = sb1("rmax", [P, 2, TPB, HG])
            rmax1 = sb1("rmax1", [P, TPB, HG])
            nm = sb1("nm", [P, TPB, 2, HG], BF16)
            nmT = sb1("nmT", [2 * HG, 2, BLK], BF16)
            ctx_f = sb1("ctx_f", [P, BLK])
            ctx_r = sb1("ctx_r", [P, TPB, HG, 1])
        w13_sb = [sb(f"w13_sb{i}", [P, DC * W13]) for i in range(RING)]
        w2_sb = [sb(f"w2_sb{i}", [P, 2, D]) for i in range(RING)]
        idx_st = [sb(f"idx_st{i}", [P, SPE], U32) for i in range(RING)]
        idx_add = [sb(f"idx_add{i}", [P, SPE], U32) for i in range(2)]
        wt_st = [sb(f"wt_st{i}", [P, B, SPE]) for i in range(RING)]
        gate_0 = [sb(f"gate_0{i}", [P, SPE, D]) for i in range(2)]
        gate_w_sb = [sb(f"gate_w_sb{i}", [P, SPE, D]) for i in range(2)]
        xg = [sb(f"xg{i}", [P, SPE, D]) for i in range(RING)]
        xgT = [sb(f"xgT{i}", [P, DC, CAP]) for i in range(2)]
        sigA, hidA = ([sb(f"{n}{i}", [P, CAP]) for i in range(2)] for n in ("sigA", "hidA"))
        sigB, hidB = ([sb(f"{n}{i}", [IB, CAP]) for i in range(2)] for n in ("sigB", "hidB"))
        ob = [sb(f"ob{i}", [P, SPE, D]) for i in range(2)]

        l_x = [sem(f"l_x{i}") for i in range(NB)]
        l_first, l_rest, l_c, l_wm, l_wm_rest, l_wqk, l_wvo, l_ones, l_init, l_sw, l_h2, l_scat, l_tab = (
            sem("l_" + n) for n in ("first", "rest", "c", "wm", "wm_rest", "wqk", "wvo", "ones", "init", "sw", "h2", "scat", "tab"))
        l_parts, l_nm, l_y = ([sem(f"l_{n}{i}") for i in range(2)] for n in ("parts", "nm", "y"))
        l_stack = [sem(f"l_stack{i}") for i in range(STACKS)]
        e_w, e_x = ([sem(f"{n}{i}") for i in range(RING)] for n in ("e_w", "e_x"))
        e_added, pool_at, add_ix = sem("e_added"), sem("pool_at"), sem("add_ix")
        dve_chain, pool_chain = sem("dve_chain"), sem("pool_chain")
        job_full = sem("job_full")
        job_read = {"A": sem("job_read_act"), "D": sem("job_read_dve")}
        (set_up, c_exped, c_acted, wo_scaled, var_set, rstd_set, xhat_set, resid_set, parts_set, max_full,
         max_read, nm_set, score_full, exp_done, pv_done, ctxf_set, x2hat_set, h2_set, nlmax_set, sexp_set,
         member_set, slots_set, route_step, ranks_set, sig_set, y_set, tabix_set, pads_set) = (sem(n) for n in (
            "set_up", "c_exped", "c_acted", "wo_scaled", "var_set", "rstd_set", "xhat_set", "resid_set",
            "parts_set", "max_full", "max_read", "nm_set", "score_full", "exp_done", "pv_done", "ctxf_set",
            "x2hat_set", "h2_set", "nlmax_set", "sexp_set", "member_set", "slots_set", "route_step",
            "ranks_set", "sig_set", "y_set", "tabix_set", "pads_set"))
        e_staged, e_turned, e_xT, e_up, e_sig, e_hid, e_down, e_ob, e_gate0, e_gate = (sem(n) for n in (
            "e_staged", "e_turned", "e_xT", "e_up", "e_sig", "e_hid", "e_down", "e_ob", "e_gate0", "e_gate"))
        N_FIRST, N_REST = 5, 7

        block = ctx.enter_context(nc.Block())

        def wait_read(eng, name):
            r, n = READ[JOB[name]]
            eng.wait_ge(job_read[r], n)

        def wait_full(eng, name):
            eng.wait_ge(job_full, JOB[name] + 1)

        @block.sync
        def _(sp):
            with nc.allow_non_contiguous_dma(reason="biases by feature"):
                row = lambda v: v.rearrange("(a d) -> a d", a=1).to_broadcast([P, D])
                chunks = lambda w: w.rearrange("(c p) n -> p c n", p=P)
                sp.dma_start(c_sb[:, :], c_in).then_inc(l_c, 16)
                first = ((ident[:, :], ident_in[0]), (gw_in[:, :], gate_w), (identb[:, :], masks[2]),
                         (bqk[:, 0, :], bq.rearrange("(c p) -> p c", p=P)),
                         (bqk[:, 1, :], bk.rearrange("(c p) -> p c", p=P)))
                rest = ((bv_row[:, :], row(bv)), (mask_qk[:, 0, :], masks[0]), (mask_qk[:, 1, :], masks[1]),
                        (bo_row[:, :], row(bo)), (tri[:, :, :], tri_in), (iota_e[:, :], iota_in), (tok_id[:, :], tok_in))
                assert (len(first), len(rest)) == (N_FIRST, N_REST)
                sp.dma_start(x_sb[:, 0:TPB, :], x[0:BLK, :].rearrange("(t p) d -> p t d", p=P)).then_inc(l_x[0], 16)
                sp.dma_start(*first[0]).then_inc(l_first, 16)
                sp.dma_start(wm[:, :, 0:2 * D], chunks(wmod)[:, :, 0:2 * D]).then_inc(l_wm, 16)
                for dst, src in first[1:]:
                    sp.dma_start(dst, src).then_inc(l_first, 16)
                for w, src in ((wq_sb, Wq), (wk_sb, Wk)):
                    sp.dma_start(w[:, :, :], chunks(src)).then_inc(l_wqk, 16)
                sp.dma_start(wm[:, :, 2 * D:], chunks(wmod)[:, :, 2 * D:]).then_inc(l_wm_rest, 16)
                for w, src in ((wv_sb, Wv), (wo_sb, Wo)):
                    sp.dma_start(w[:, :, :], chunks(src)).then_inc(l_wvo, 16)
                for dst, src in rest:
                    sp.dma_start(dst, src).then_inc(l_rest, 16)
            for i in range(STACKS):
                sp.dma_start(q_stack[i][ROW_ALIBI:ROW_NMAX, :, :], ones_rows[0:3, 0]).then_inc(l_ones, 16)
                sp.dma_start(k_stack[i][ROW_NMAX:K_EXP, :, :, :], ones_rows[0:2]).then_inc(l_ones, 16)
            for tb in range(1, NB):
                sp.dma_start(x_sb[:, TPB * tb:TPB * (tb + 1), :],
                             x[BLK * tb:BLK * (tb + 1), :].rearrange("(t p) d -> p t d", p=P)).then_inc(l_x[tb], 16)
            sp.dma_start(slot_table, slot_init).then_inc(l_init, 16)
            sp.dma_start(h2_rows[T:T + CAP, :], zero_row.to_broadcast([CAP, D])).then_inc(l_init, 16)
            sp.dma_start(out[T:T + CAP, :], zero_row.to_broadcast([CAP, D])).then_inc(l_init, 16)
            for it in ITEMS:
                kind = it[0]
                if kind == "qkp":
                    _, tb, side, c = it
                    n = ORD[it]
                    sp.wait_ge(parts_set, n + 1)
                    dst = (q_parts, k_parts)[side][tb][:, c * P // HG:(c + 1) * P // HG, :, :]
                    sp.dma_start(dst.rearrange("j a h t -> (a h) j t"), parts[:, n % 2, :, :]).then_inc(l_parts[n % 2], 16)
                if kind == "stk":
                    u = it[1]
                    b, qb, g = UNITS[u]
                    s_, rows = l_stack[u % STACKS], slice(HD * g, HD * (g + 1))
                    for i in range(2):
                        sp.wait_ge(l_parts[i], 16 * 2 * (u // NG + 1))
                    if u >= STACKS:
                        sp.wait_ge(score_full, upto("qk", lambda i: i[1] == u - STACKS))
                    for kp in range(NPARTS):
                        n = NPARTS - kp
                        at = slice(HD * ROW_OF_KPART[kp], HD * (ROW_OF_KPART[kp] + n))
                        sp.dma_start(q_stack[u % STACKS][at, :, :],
                                     q_parts[u // NG][0:n, rows].rearrange("j d h t -> j d (h t)")).then_inc(s_, 16)
                        for half in range(qb + 1):
                            sp.dma_start(k_stack[u % STACKS][at, half, :, :],
                                         k_parts[2 * b + half][kp:kp + 1, rows].rearrange("j d h t -> j d (h t)")
                                         .to_broadcast([n, HD, HG * BLK])).then_inc(s_, 16)
                    sp.dma_start(k_stack[u % STACKS][ROW_ALIBI:ROW_NMAX, 0:qb + 1, :, :],
                                 alibi[:, g, 0:qb + 1]).then_inc(s_, 16)
                if kind == "nmax":
                    u = it[1]
                    wait_read(sp, it)
                    for part in range(2):
                        sp.dma_start(q_stack[u % STACKS][ROW_NMAX + part:ROW_NMAX + part + 1, :, :],
                                     nmT[HG * part:HG * (part + 1), u % 2, :]).then_inc(l_nm[u % 2], 16)
                if kind == "ln2":
                    tb = it[1]
                    sp.wait_ge(h2_set, tb + 1)
                    sp.dma_start(h2_rows[BLK * tb:BLK * (tb + 1), :].rearrange("(t p) d -> p t d", p=P),
                                 h2[:, :, :]).then_inc(l_h2, 16)
                if kind == "free":
                    wait_read(sp, ("ctx", NU - 1))
                    sp.wait_ge(exp_done, total["qk"])
                    for r in range(RING):
                        load_expert(sp, r, w1, w3, w2, w13_sb[r], w2_sb[r], e_w[r])
                if kind == "sw":
                    wait_read(sp, ("row", B - 1, 1))
                    sp.dma_start(sw1_sb[:, :, :], sw1.rearrange("(c p) n -> p c n", p=P)).then_inc(l_sw, 16)
                    sp.dma_start(sw3_sb[:, :, :], sw3.rearrange("(c p) n -> p c n", p=P)).then_inc(l_sw, 16)
                    for m, (r0, rn) in enumerate(SM):
                        sp.dma_start(sw2_sb[0:rn, m, :], sw2[r0:r0 + rn, :]).then_inc(l_sw, 16)
                if kind == "tab":
                    sp.wait_ge(l_scat, 16 * NT * TOPK)
                    sp.dma_start(tab[:, :, :], slot_table.rearrange("(p j) n -> p j n", p=P)).then_inc(l_tab, 16)
                if kind == "sd":
                    _, tb, pr = it
                    n, r0 = ORD[it], BLK * tb + 2 * P * pr
                    sp.wait_ge(y_set, n + 1)
                    sp.dma_start(out[r0:r0 + 2 * P, :].rearrange("(t p) d -> p t d", p=P),
                                 y_init[:, n % 2, :, :]).then_inc(l_y[n % 2], 16)
            with sp.Fori(1, E // RING) as i:
                for r in range(RING):
                    sp.wait_ge(e_down, (i - 1) * RING + r + 1)
                    load_expert(sp, i * RING + r, w1, w3, w2, w13_sb[r], w2_sb[r], e_w[r])
            sp.wait_ge(e_added, 16 * SPE * E)

        @block.tensor
        def _(pe):
            def begin(name):
                k, before = BANK_OF[name]
                if before is not None and before[0] == "max":
                    pe.wait_ge(max_read, ORD[before] + 1)
                elif before is not None and before[0] == "qk":
                    pe.wait_ge(exp_done, ORD[before] + 1)
                elif before is not None:
                    wait_read(pe, before)
                return bank[k]

            pe.wait_ge(set_up, 1)
            pe.wait_ge(l_first, 16 * N_FIRST)
            pe.matmul(pv_bank[:, :], identb[:, :], zero_b[:, :], start=True, stop=True)
            for it in ITEMS:
                kind = it[0]
                if kind == "mod":
                    jb = begin("cT")
                    pe.wait_ge(c_acted, 1)
                    for c in range(DC):
                        ins = pe.transpose(jb[:, B * c:B * (c + 1)], c_act[:, c * P:(c + 1) * P], ident[0:B, 0:B])
                    ins.then_inc(job_full, 1)
                    jb = begin("gwT")
                    for c in range(DC):
                        ins = pe.transpose(jb[:, E * c:E * (c + 1)], gw_in[:, c * P:(c + 1) * P], ident[0:E, 0:E])
                    ins.then_inc(job_full, 1)
                    jb = begin("modT")
                    wait_read(pe, "cT")
                    pe.wait_ge(l_wm, 16)
                    for q in range(2 * DC):
                        for c in range(DC):
                            ins = pe.matmul(jb[:, B * q:B * (q + 1)], wm[:, c, q * P:(q + 1) * P], cT[:, c, :],
                                            start=(c == 0), stop=(c == DC - 1))
                    ins.then_inc(job_full, 1)
                elif kind == "row":
                    _, b, k = it
                    jb = begin(it)
                    pe.wait_ge(l_wm_rest, 16)
                    for c in range(DC):
                        ins = pe.matmul(jb[:, :], c_rep[:, c * B + b, :], wm[:, c, 2 * D * (k + 1):2 * D * (k + 2)],
                                        start=(c == 0), stop=(c == DC - 1))
                    ins.then_inc(job_full, 1)
                elif kind == "ln":
                    _, tb, pr = it
                    jb = begin(it)
                    pe.wait_ge(xhat_set, ORD[it] + 1)
                    for c in range(DC):
                        for i in range(2):
                            ins = pe.transpose(jb[:, (2 * c + i) * P:(2 * c + i + 1) * P],
                                               xhat[:, ORD[it] % 2, i, c * P:(c + 1) * P], ident[:, :])
                    ins.then_inc(job_full, 1)
                elif kind == "qkp":
                    _, tb, side, co = it
                    jb = begin(it)
                    wait_read(pe, ("ln", tb, 1))
                    pe.wait_ge(l_wqk, 32)
                    for c in range(DC):
                        ins = pe.matmul(jb[:, :], (wq_sb, wk_sb)[side][:, c, co * P:(co + 1) * P], hT[:, c, :],
                                        start=(c == 0), stop=(c == DC - 1))
                    ins.then_inc(job_full, 1)
                elif kind == "vp":
                    _, tb, pr = it
                    jb = begin(it)
                    pe.wait_ge(l_wvo, 32)
                    for i in range(2):
                        for c in range(DC):
                            ins = pe.matmul(jb[:, D * i:D * (i + 1)], hT[:, c, (2 * pr + i) * P:(2 * pr + i + 1) * P],
                                            wv_sb[:, c, :], start=(c == 0), stop=(c == DC - 1))
                    ins.then_inc(job_full, 1)
                elif kind == "max":
                    _, u, qt, hl, half = it
                    ring = u % STACKS
                    crossed = half == UNITS[u][1]
                    w = (qt + 1) * P if crossed else BLK
                    if (qt, hl, half) == (0, 0, 0):
                        pe.wait_ge(l_stack[ring], 16 * sum(stack_loads(v) for v in range(ring, u + 1, STACKS)))
                        pe.wait_ge(l_ones, 32 * STACKS)
                        pe.wait_ge(l_rest, 16 * N_REST)
                    mb = begin(it)
                    ins = pe.matmul(mb[:, 0:w], q_stack[ring][0:K_MAX, hl, qt * P:(qt + 1) * P],
                                    k_stack[ring][0:K_MAX, half, hl, 0:w], start=True, stop=not crossed)
                    if crossed:
                        ins = pe.matmul(mb[:, w - P:w], identb[:, :], mask_qk[:, 0, :], start=False, stop=True)
                    ins.then_inc(max_full, 1)
                elif kind == "nmax":
                    jb = begin(it)[:, :].bitcast(BF16)
                    pe.wait_ge(nm_set, it[1] + 1)
                    for qt in range(TPB):
                        ins = pe.transpose(jb[0:2 * HG, qt * P:(qt + 1) * P],
                                           nm[:, qt, :, :].rearrange("p a h -> p (a h)"), identb[:, :])
                    ins.then_inc(job_full, 1)
                elif kind == "qk":
                    _, u, kt, hl = it
                    ring = u % STACKS
                    q0, crossed = diagonal(u, kt)
                    if (kt, hl) == (0, 0):
                        pe.wait_ge(l_nm[u % 2], 32 * (u // 2 + 1))
                    sbk = begin(it)
                    ins = pe.matmul(sbk[:, q0:BLK], k_stack[ring][0:K_EXP, kt // TPB, hl, kt % TPB * P:(kt % TPB + 1) * P],
                                    q_stack[ring][0:K_EXP, hl, q0:BLK], start=True, stop=not crossed)
                    if crossed:
                        ins = pe.matmul(sbk[:, q0:q0 + P], identb[:, :], mask_qk[:, 1, :], start=False, stop=True)
                    ins.then_inc(score_full, 1)
                elif kind == "pv":
                    _, u, kt = it
                    m, kb = ORD[it], key_block(u, kt)
                    q0, _ = diagonal(u, kt)
                    pe.wait_ge(exp_done, HG * (m + 1))
                    if kt == 0:
                        wait_read(pe, ("vp", kb, 1))
                        if u:
                            pe.wait_ge(ctxf_set, u)
                    if kt == TPB:
                        wait_read(pe, ("vp", kb, 1))
                    last = kt == TPB * (UNITS[u][1] + 1) - 1
                    for hl in range(HG):
                        ins = pe.matmul(pv_bank[32 * hl:32 * hl + VW, q0:BLK],
                                        v_aug[kb % VRING][:, kt % TPB, HG * UNITS[u][2] + hl, :],
                                        p_t[:, m % 2, hl, q0:BLK], start=(kt == 0), stop=last)
                    ins.then_inc(pv_done, 1)
                elif kind == "ctx":
                    jb = begin(it)
                    pe.wait_ge(ctxf_set, it[1] + 1)
                    for qt in range(TPB):
                        ins = pe.transpose(jb[:, qt * P:(qt + 1) * P], ctx_f[:, qt * P:(qt + 1) * P], ident[:, :])
                    ins.then_inc(job_full, 1)
                elif kind == "ctxT":
                    _, tb, pr = it
                    jb = begin(it)
                    wait_read(pe, ("ctx", NG * tb + NG - 1))
                    for i in range(2):
                        for c in range(DC):
                            j = DC * i + c
                            ins = pe.transpose(jb[:, j * P:(j + 1) * P], ctx_tok[:, 2 * pr + i, c * P:(c + 1) * P], ident[:, :])
                    ins.then_inc(job_full, 1)
                elif kind == "wo":
                    _, tb, pr = it
                    jb = begin(it)
                    wait_read(pe, ("ctxT", tb, pr))
                    pe.wait_ge(wo_scaled, 1)
                    for i in range(2):
                        for c in range(DC):
                            j = DC * i + c
                            ins = pe.matmul(jb[:, D * i:D * (i + 1)], ctxT[:, pr, j * P:(j + 1) * P],
                                            wo_g[:, tb // 2, c, :], start=(c == 0), stop=(c == DC - 1))
                    ins.then_inc(job_full, 1)
                elif kind == "h2T":
                    _, tb, pr = it
                    jb = begin(it)
                    pe.wait_ge(h2_set, tb + 1)
                    for c in range(DC):
                        for i in range(2):
                            ins = pe.transpose(jb[:, (2 * c + i) * P:(2 * c + i + 1) * P],
                                               h2[:, 2 * pr + i, c * P:(c + 1) * P], ident[:, :])
                    ins.then_inc(job_full, 1)
                elif kind == "gate":
                    tb = it[1]
                    jb = begin(it)
                    wait_read(pe, ("h2T", tb, 1))
                    wait_read(pe, "gwT")
                    for i in range(TPB):
                        t0 = (TPB * tb + i) * P
                        for c in range(DC):
                            ins = pe.matmul(jb[:, E * i:E * (i + 1)], h2T[:, c, t0:t0 + P], gwT[:, c, :],
                                            start=(c == 0), stop=(c == DC - 1))
                    ins.then_inc(job_full, 1)
                elif kind == "pos":
                    tb = it[1]
                    jb = begin(it)
                    pe.wait_ge(member_set, tb + 1)
                    for i in range(TPB):
                        pe.matmul(jb[:, E * i:E * (i + 1)], tri[:, 0, :], member[:, i, :], start=True, stop=False)
                        ins = pe.matmul(jb[:, E * i:E * (i + 1)], tri[:, 1, :], before[:, TPB * tb + i, :],
                                        start=False, stop=True)
                    ins.then_inc(job_full, 1)
                elif kind in ("sg", "sm"):
                    _, tb, m = it
                    r0, rn = SM[m]
                    jb = begin(it)
                    if ORD[it] == 0:
                        pe.wait_ge(l_sw, 16 * (2 + len(SM)))
                    if m == 0:
                        wait_read(pe, ("h2T", tb, 1))
                    for c in range(DC):
                        ins = pe.matmul(jb[0:rn, :], (sw1_sb if kind == "sg" else sw3_sb)[:, c, r0:r0 + rn],
                                        h2T[:, c, BLK * tb:BLK * (tb + 1)], start=(c == 0), stop=(c == DC - 1))
                    ins.then_inc(job_full, 1)
                elif kind == "sd":
                    _, tb, pr = it
                    jb = begin(it)
                    wait_read(pe, ("sm", tb, len(SM) - 1))
                    for i in range(2):
                        for m, (_, rn) in enumerate(SM):
                            ins = pe.matmul(jb[:, D * i:D * (i + 1)],
                                            s_hid[0:rn, m, (2 * pr + i) * P:(2 * pr + i + 1) * P],
                                            sw2_sb[0:rn, m, :], start=(m == 0), stop=(m == len(SM) - 1))
                    ins.then_inc(job_full, 1)

            pe.wait_ge(pads_set, 1)
            pe.wait_ge(y_set, total["sd"])
            pe.wait_ge(max_read, total["max"])
            pe.wait_ge(exp_done, total["qk"])
            pe.wait_ge(ctxf_set, NU)

            def turn(i, r):
                e = i * RING + r
                pe.wait_ge(e_x[r], 32 * i + 32)
                if not (isinstance(e, int) and e < 2):
                    pe.wait_ge(e_xT, e - 1)
                for c in range(DC):
                    for s in range(SPE):
                        ins = pe.transpose(bank[6 + r % 2][:, (SPE * c + s) * P:(SPE * c + s + 1) * P],
                                           xg[r][:, s, c * P:(c + 1) * P], ident[:, :])
                ins.then_inc(e_turned, 1)

            def up(i, r):
                e = i * RING + r
                pe.wait_ge(e_w[r], 16 * LOADS_PER_EXPERT * i + 16 * LOADS_PER_EXPERT)
                pe.wait_ge(e_xT, e + 1)
                if not (isinstance(e, int) and e < 2):
                    pe.wait_ge(e_hid, e - 1)
                a_bank, c_bank = bank[2 * (r % 2)], bank[2 * (r % 2) + 1]
                for k in range(2):
                    for c in range(DC):
                        w0 = c * W13 + k * P
                        pe.matmul(a_bank[:, CAP * k:CAP * (k + 1)], w13_sb[r][:, w0:w0 + P], xgT[r % 2][:, c, :],
                                  start=(c == 0), stop=(c == DC - 1))
                for c in range(DC):
                    w = w13_sb[r][:, c * W13 + COL_B:(c + 1) * W13]
                    ins = pe.matmul(c_bank[0:W13 - COL_B, 0:CAP], w, xgT[r % 2][:, c, :], start=(c == 0), stop=(c == DC - 1))
                ins.then_inc(e_up, 1)

            def down(i, r):
                e = i * RING + r
                pe.wait_ge(e_hid, e + 1)
                if not (isinstance(e, int) and e < 2):
                    pe.wait_ge(e_ob, e - 1)
                for s in range(SPE):
                    o = bank[4 + r % 2][:, D * s:D * (s + 1)]
                    pe.matmul(o, hidA[r % 2][:, s * P:(s + 1) * P], w2_sb[r][:, 0, :], start=True, stop=False)
                    ins = pe.matmul(o, hidB[r % 2][:, s * P:(s + 1) * P], w2_sb[r][0:IB, 1, :], start=False, stop=True)
                ins.then_inc(e_down, 1)

            turn(0, 0)

            def body(i, first=False, last=False):
                for r in range(RING):
                    if not (last and r == RING - 1):
                        turn(i + (r + 1) // RING, (r + 1) % RING)
                    up(i, r)
                    if not (first and r == 0):
                        down(i if r else i - 1, (r - 1) % RING)

            body(0, first=True)
            with pe.Fori(1, E // RING - 1) as i:
                body(i)
            body(E // RING - 1, last=True)
            down(E // RING - 1, RING - 1)

        @block.scalar
        def _(act):
            act.wait_ge(l_c, 16)
            act.activation(c_exp_sb[:, :], c_sb[:, :], ACT.Exp, scale=-1.0).then_inc(c_exped, 1)
            for it in ITEMS:
                kind = it[0]
                if kind == "ln":
                    _, tb, pr = it
                    wait_full(act, it)
                    wait_read(act, "modT")
                    if tb:
                        wait_full(act, ("vp", tb - 1, 1))
                    for c in range(DC):
                        ins = act.activation(hT[:, c, 2 * P * pr:2 * P * (pr + 1)],
                                             bank[BANK_OF[it][0]][:, 2 * P * c:2 * P * (c + 1)], ACT.Identity,
                                             bias=sa[:, c, tb // 2:tb // 2 + 1], scale=ca1[:, c, tb // 2:tb // 2 + 1])
                    ins.then_inc(job_read["A"], 1)
                elif kind == "qkp":
                    _, tb, side, c = it
                    n = ORD[it]
                    wait_full(act, it)
                    if n >= 2:
                        act.wait_ge(parts_set, n - 1)
                        act.wait_ge(l_parts[n % 2], 16 * (n // 2))
                    bias = bq_s[:, c:c + 1] if side == 0 else bqk[:, 1, c:c + 1]
                    for dst in (v32[:, n % 2, :], parts[:, n % 2, 0, :]):
                        ins = act.activation(dst, bank[BANK_OF[it][0]][:, :], ACT.Identity, bias=bias,
                                             scale=Q_SCALE if side == 0 else 1.0)
                    ins.then_inc(job_read["A"], 1)
                elif kind == "nmax":
                    u = it[1]
                    wait_full(act, it)
                    if u >= 2:
                        act.wait_ge(l_nm[u % 2], 32 * (u // 2))
                    act.activation(nmT[:, u % 2, :], bank[BANK_OF[it][0]][:, :].bitcast(BF16)[0:2 * HG, 0:BLK],
                                   ACT.Copy).then_inc(job_read["A"], 1)
                elif kind == "qk":
                    _, u, kt, hl = it
                    m = ORD[("pv", u, kt)]
                    q0, _ = diagonal(u, kt)
                    act.wait_ge(score_full, ORD[it] + 1)
                    if m >= 2 and hl == 0:
                        act.wait_ge(pv_done, m - 1)
                    act.activation(p_t[:, m % 2, hl, q0:BLK], bank[BANK_OF[it][0]][:, q0:BLK],
                                   ACT.Exp).then_inc(exp_done, 1)
                elif kind == "acc":
                    u = it[1]
                    act.wait_ge(pv_done, upto("pv", lambda i: i[1] == u))
                    if u:
                        wait_full(act, ("ctx", u - 1))
                    act.activation(ctx_f[:, :], pv_bank[:, :], ACT.Copy).then_inc(ctxf_set, 1)
                elif kind == "ctxT":
                    _, tb, pr = it
                    wait_full(act, it)
                    if tb:
                        wait_full(act, ("wo", tb - 1, pr))
                    act.activation(ctxT[:, pr, :], bank[BANK_OF[it][0]][:, :], ACT.Copy).then_inc(job_read["A"], 1)
                elif kind == "h2T":
                    _, tb, pr = it
                    t0 = BLK * tb + 2 * P * pr
                    wait_full(act, it)
                    act.activation(h2T[:, :, t0:t0 + 2 * P],
                                   bank[BANK_OF[it][0]][:, :].rearrange("p (c t) -> p c t", c=DC),
                                   ACT.Copy).then_inc(job_read["A"], 1)
                elif kind == "route" and it[2] == 0:
                    act.wait_ge(nlmax_set, it[1] + 1)
                    for i in range(TPB):
                        ins = act.activation(sc_exp[:, i, :], lg[:, i, :], ACT.Exp, bias=nlmax[:, i:i + 1],
                                             accum_out=esum[:, i:i + 1])
                    ins.then_inc(sexp_set, 1)
                elif kind == "sg":
                    _, tb, m = it
                    n, rn = ORD[it], SM[m][1]
                    wait_full(act, it)
                    if n >= 2:
                        wait_read(act, ("sm", *divmod(n - 2, len(SM))))
                    act.activation(s_act[0:rn, n % 2, :], bank[BANK_OF[it][0]][0:rn, :], ACT.Tanh,
                                   scale=0.5).then_inc(sig_set, 1)

            def sigs(i, r):
                e = i * RING + r
                act.wait_ge(e_up, e + 1)
                if not (isinstance(e, int) and e < 2):
                    act.wait_ge(e_hid, e - 1)
                act.activation(sigA[r % 2][:, :], bank[2 * (r % 2)][:, 0:CAP], ACT.Silu)
                act.activation(sigB[r % 2][:, :], bank[2 * (r % 2) + 1][0:IB, 0:CAP], ACT.Silu).then_inc(e_sig, 1)

            def gates(i, r):
                e = i * RING + r
                act.wait_ge(e_staged, e + 1)
                if not (isinstance(e, int) and e < 2):
                    act.wait_ge(e_gate, e - 1)
                for s in range(SPE):
                    ins = act.activation(gate_0[r % 2][:, s, :], gb[:, 0, :], ACT.Copy, scale=wt_st[r][:, 0, s:s + 1])
                ins.then_inc(e_gate0, 1)

            def body(i):
                for r in range(RING):
                    gates(i, r)
                    sigs(i, r)

            body(0)
            with act.Fori(1, E // RING) as i:
                body(i)

        @block.vector
        def _(dve):
            chain = [0]

            def link(ins):
                chain[0] += 1
                ins.then_inc(dve_chain, 1)
                dve.wait_ge(dve_chain, chain[0])

            def split(it):
                n = ORD[it]
                wait_read(dve, it)
                v, pt = v32[:, n % 2, :], parts[:, n % 2, :, :]
                if n:
                    dve.wait_ge(parts_set, n)
                link(dve.tensor_tensor(res[:, :], v, pt[:, 0, :], ALU.subtract))
                link(dve.tensor_copy(pt[:, 1, :], res[:, :]))
                dve.tensor_tensor(pt[:, 2, :], res[:, :], pt[:, 1, :], ALU.subtract).then_inc(parts_set, 1)

            def gate_of(dst, src):
                link(dve.tensor_scalar(sign2[:, :], src, 0.0, 2.0, ALU.is_ge, ALU.mult))
                link(dve.tensor_scalar(sign[:, :], sign2[:, :], -1.0, None, ALU.add))
                link(dve.tensor_tensor(mag[:, :], src, sign[:, :], ALU.mult))
                return dve.scalar_tensor_tensor(out=dst, in0=mag[:, :], scalar=MIN_GATE, in1=sign[:, :],
                                                op0=ALU.max, op1=ALU.mult)

            def row_stats(tiles, into, n):
                if n:
                    dve.wait_ge(var_set, n)
                for i in range(TPB):
                    ins = dve.bn_stats(stats[:, i, :], x_sb[:, tiles + i, :])
                link(ins)
                for i in range(TPB):
                    ins = dve.bn_aggr(into[:, tiles + i, :], stats[:, i, :])
                ins.then_inc(var_set, 1)

            def stage(i, r):
                e = i * RING + r
                if not (isinstance(e, int) and e < RING):
                    dve.wait_ge(e_turned, e - RING + 1)
                    dve.wait_ge(e_gate, e - RING + 1)
                dve.tensor_copy(wt_st[r][:, :, :], tab_w[:, :, bass.ds(SPE * e, SPE)])
                dve.tensor_copy(idx_st[r][:, :], tab_ix[:, bass.ds(SPE * e, SPE)]).then_inc(e_staged, 1)

            dve.wait_ge(c_exped, 1)
            link(dve.tensor_scalar(c_den[:, :], c_exp_sb[:, :], 1.0, None, ALU.add))
            link(dve.reciprocal(c_rec[:, :], c_den[:, :]))
            dve.tensor_tensor(c_act[:, :], c_sb[:, :], c_rec[:, :], ALU.mult).then_inc(c_acted, 1)
            for it in ITEMS:
                kind = it[0]
                if kind == "stat":
                    dve.wait_ge(l_x[it[1]], 16)
                    row_stats(TPB * it[1], mv, VAR[it])
                elif kind == "mod":
                    dve.wait_ge(l_first, 16 * N_FIRST)
                    dve.tensor_scalar(bq_s[:, :], bqk[:, 0, :], Q_SCALE, None, ALU.mult)
                    wait_full(dve, "cT")
                    jb = bank[BANK_OF["cT"][0]]
                    dve.tensor_copy(c_rep[:, :, :], jb[:, 0:DC * B].rearrange("p (k a) -> p k a", a=1)
                                    .to_broadcast([P, DC * B, P]))
                    dve.tensor_copy(cT[:, :, :], jb[:, 0:DC * B].rearrange("p (c b) -> p c b", c=DC)).then_inc(job_read["D"], 1)
                    wait_full(dve, "gwT")
                    dve.tensor_copy(gwT[:, :, :], bank[BANK_OF["gwT"][0]][:, 0:DC * E].rearrange("p (c e) -> p c e", c=DC))\
                       .then_inc(job_read["D"], 1)
                    wait_full(dve, "modT")
                    jb = bank[BANK_OF["modT"][0]][:, 0:2 * DC * B].rearrange("p (k c b) -> p k c b", k=2, c=DC)
                    dve.tensor_copy(sa[:, :, :], jb[:, 0])
                    dve.tensor_scalar(ca1[:, :, :], jb[:, 1], 1.0, None, ALU.add).then_inc(job_read["D"], 1)
                elif kind == "row":
                    _, b, k = it
                    wait_full(dve, it)
                    jb = bank[BANK_OF[it][0]]
                    if k == 0:
                        dve.tensor_copy(sb_row[:, b, :], jb[:, D:2 * D])
                        gate_of(ga[:, b, :], jb[:, 0:D]).then_inc(job_read["D"], 1)
                    else:
                        dve.tensor_scalar(cb1[:, b, :], jb[:, 0:D], 1.0, None, ALU.add)
                        gate_of(gb[:, b, :], jb[:, D:2 * D]).then_inc(job_read["D"], 1)
                elif kind == "ln":
                    _, tb, pr = it
                    n = ORD[it]
                    dve.wait_ge(rstd_set, VAR[("stat", tb)] + 1)
                    if n >= 2:
                        wait_full(dve, ("ln", tb - 1, pr))
                    for i in range(2):
                        t = TPB * tb + 2 * pr + i
                        ins = dve.tensor_scalar(xhat[:, n % 2, i, :], x_sb[:, t, :], mv[:, t, 0:1], rstd[:, t:t + 1],
                                                ALU.subtract, ALU.mult)
                    ins.then_inc(xhat_set, 1)
                elif kind == "qkp":
                    split(it)
                elif kind == "vp":
                    _, tb, pr = it
                    wait_full(dve, it)
                    if pr == 0:
                        if tb == 0:
                            dve.wait_ge(set_up, 1)
                            dve.wait_ge(l_rest, 16 * N_REST)
                        if tb >= VRING:
                            dve.wait_ge(pv_done, upto("pv", lambda i: key_block(i[1], i[2]) == tb - VRING))
                    for i in range(2):
                        ins = dve.tensor_tensor(v_aug[tb % VRING][:, 2 * pr + i, :, 0:HD],
                                                bank[BANK_OF[it][0]][:, D * i:D * (i + 1)].rearrange("p (h d) -> p h d", h=H),
                                                bv_row[:, :].rearrange("p (h d) -> p h d", h=H), ALU.add)
                    ins.then_inc(job_read["D"], 1)
                elif kind == "max":
                    _, u, qt, hl, half = it
                    w = (qt + 1) * P if half == UNITS[u][1] else BLK
                    dve.wait_ge(max_full, ORD[it] + 1)
                    dve.reduce_max(rmax[:, half, qt, hl:hl + 1], bank[BANK_OF[it][0]][:, 0:w], AX.X).then_inc(max_read, 1)
                elif kind == "neg":
                    u = it[1]
                    dve.wait_ge(max_read, upto("max", lambda i: i[1] == u))
                    if u:
                        wait_full(dve, ("nmax", u - 1))
                    m = rmax[:, 0]
                    if UNITS[u][1]:
                        m = rmax1[:, :, :]
                        link(dve.tensor_tensor(m, rmax[:, 0], rmax[:, 1], ALU.max))
                    link(dve.tensor_scalar(nm[:, :, 0, :], m, -1.0, None, ALU.mult))
                    dve.scalar_tensor_tensor(out=nm[:, :, 1, :], in0=m, scalar=-1.0, in1=nm[:, :, 0, :],
                                             op0=ALU.mult, op1=ALU.subtract).then_inc(nm_set, 1)
                elif kind == "ctx":
                    u = it[1]
                    g = UNITS[u][2]
                    wait_full(dve, it)
                    if g == 0 and u:
                        wait_full(dve, ("ctxT", u // NG - 1, 1))
                    jb = bank[BANK_OF[it][0]][:, :].rearrange("p (t h d) -> p t h d", t=TPB, h=HG)
                    link(dve.reciprocal(ctx_r[:, :, :, :], jb[:, :, :, HD:HD + 1]))
                    dve.tensor_tensor(ctx_tok[:, :, HG * HD * g:HG * HD * (g + 1)].rearrange("p t (h d) -> p t h d", h=HG),
                                      jb[:, :, :, 0:HD], ctx_r[:, :, :, :].to_broadcast([P, TPB, HG, HD]),
                                      ALU.mult).then_inc(job_read["D"], 1)
                elif kind == "wo":
                    _, tb, pr = it
                    wait_full(dve, it)
                    dve.wait_ge(resid_set, tb + 1)
                    xs = x_sb[:, TPB * tb + 2 * pr:TPB * tb + 2 * pr + 2, :]
                    dve.tensor_tensor(xs, bank[BANK_OF[it][0]][:, :].rearrange("p (t d) -> p t d", t=2), xs,
                                      ALU.add).then_inc(job_read["D"], 1)
                elif kind == "ln2s":
                    wait_read(dve, ("wo", it[1], 1))
                    row_stats(TPB * it[1], mv2, VAR[it])
                elif kind == "ln2":
                    tb = it[1]
                    dve.wait_ge(rstd_set, VAR[("ln2s", tb)] + 1)
                    if tb:
                        dve.wait_ge(l_h2, 16 * tb)
                        wait_full(dve, ("h2T", tb - 1, 1))
                    for i in range(TPB):
                        t = TPB * tb + i
                        ins = dve.tensor_scalar(h2[:, i, :], x_sb[:, t, :], mv2[:, t, 0:1], rstd2[:, t:t + 1],
                                                ALU.subtract, ALU.mult)
                    ins.then_inc(x2hat_set, 1)
                    if tb == NB - 1:
                        h2b = lambda v: v[:, tb // 2:tb // 2 + 1, :].to_broadcast([P, TPB, D])
                        dve.wait_ge(x2hat_set, tb + 1)
                        link(dve.tensor_tensor(h2[:, :, :], h2[:, :, :], h2b(cb1), ALU.mult))
                        dve.tensor_tensor(h2[:, :, :], h2[:, :, :], h2b(sb_row), ALU.add).then_inc(h2_set, 1)
                elif kind == "gate":
                    wait_full(dve, it)
                    jb = bank[BANK_OF[it][0]][:, 0:TPB * E].rearrange("p (t e) -> p t e", t=TPB)
                    dve.tensor_copy(lg[:, :, :], jb).then_inc(job_read["D"], 1)
                    wait_read(dve, it)
                    dve.tensor_reduce(nlmax[:, :], lg[:, :, :], AX.X, ALU.max, negate=True).then_inc(nlmax_set, 1)
                elif kind == "route":
                    _, tb, n = it
                    if n:
                        dve.wait_ge(route_step, 5 * tb + n)
                    if n == 0:
                        dve.wait_ge(sexp_set, tb + 1)
                        if tb:
                            dve.wait_ge(slots_set, tb)
                        link(dve.reciprocal(rsum[:, :], esum[:, :]))
                        for i in range(TPB):
                            ins = dve.tensor_scalar(score[:, i, :], sc_exp[:, i, :], rsum[:, i:i + 1], None, ALU.mult)
                    elif n == 1:
                        for i in range(TPB):
                            ins = dve.max(top[:, i, :], score[:, i, :])
                    elif n == 2:
                        for i in range(TPB):
                            ins = dve.max_index(topi[:, i, :], top[:, i, :], score[:, i, :])
                    elif n == 3:
                        dve_copy = dve.tensor_copy(topf[:, :, :], topi[:, :, :])
                        link(dve_copy)
                        for i in range(TPB):
                            ins = dve.tensor_tensor(onehot[:, i, :, :],
                                                    iota_e[:, :].rearrange("p (a e) -> p a e", a=1).to_broadcast([P, TOPK, E]),
                                                    topf[:, i, 0:TOPK].rearrange("p (k a) -> p k a", a=1)
                                                    .to_broadcast([P, TOPK, E]), ALU.is_equal)
                    else:
                        if tb:
                            wait_full(dve, ("pos", tb - 1))
                        with nc.allow_low_precision(reason="counts up to one are exact"):
                            ins = dve.tensor_reduce(member[:, :, :], onehot[:, :, :, :].rearrange("p t k e -> p t e k"),
                                                    AX.X, ALU.add)
                    ins.then_inc(route_step, 1)
                elif kind == "pos":
                    tb = it[1]
                    wait_full(dve, it)
                    jb = bank[BANK_OF[it][0]]
                    for i in range(TPB):
                        ins = dve.tensor_tensor(onepos[:, i, :, :], onehot[:, i, :, :],
                                                jb[:, E * i:E * (i + 1)].rearrange("p (a e) -> p a e", a=1)
                                                .to_broadcast([P, TOPK, E]), ALU.mult)
                    ins.then_inc(job_read["D"], 1)
                    wait_read(dve, it)
                    dve.tensor_reduce(posk[:, :, :], onepos[:, :, :, :], AX.X, ALU.add).then_inc(ranks_set, 1)
                elif kind == "sg":
                    _, tb, m = it
                    n, rn = ORD[it], SM[m][1]
                    dve.wait_ge(sig_set, n + 1)
                    dve.scalar_tensor_tensor(out=s_act[0:rn, n % 2, :], in0=s_act[0:rn, n % 2, :], scalar=1.0,
                                             in1=bank[BANK_OF[it][0]][0:rn, :], op0=ALU.add, op1=ALU.mult)\
                       .then_inc(job_read["D"], 1)
                elif kind == "sm":
                    _, tb, m = it
                    n, rn = ORD[it], SM[m][1]
                    wait_full(dve, it)
                    wait_read(dve, ("sg", tb, m))
                    if m == 0 and tb:
                        wait_full(dve, ("sd", tb - 1, 1))
                    dve.tensor_tensor(s_hid[0:rn, m, :], s_act[0:rn, n % 2, :], bank[BANK_OF[it][0]][0:rn, :],
                                      ALU.mult).then_inc(job_read["D"], 1)
                elif kind == "tab":
                    dve.wait_ge(l_tab, 16)
                    link(dve.tensor_scalar(tab_w[:, 1, :], tab[:, :, 0], float(S), None, ALU.is_ge))
                    link(dve.tensor_tensor(tab_w[:, 1, :], tab_w[:, 1, :], tab[:, :, 1], ALU.mult))
                    dve.tensor_tensor(tab_w[:, 0, :], tab[:, :, 1], tab_w[:, 1, :], ALU.subtract)
                    dve.tensor_copy(tab_ix[:, :], tab[:, :, 0]).then_inc(tabix_set, 1)
                    dve.wait_ge(tabix_set, 1)
                    for r in range(RING):
                        stage(0, r)
                elif kind == "sd":
                    _, tb, pr = it
                    n = ORD[it]
                    wait_full(dve, it)
                    if n >= 2:
                        dve.wait_ge(l_y[n % 2], 16 * (n // 2))
                    wait_read(dve, ("wo", tb, 1))
                    if n:
                        dve.wait_ge(y_set, n)
                    for i in range(2):
                        ins = dve.scalar_tensor_tensor(out=y_init[:, n % 2, i, :], in0=bank[BANK_OF[it][0]][:, D * i:D * (i + 1)],
                                                       scalar=0.5, in1=gb[:, tb // 2, :], op0=ALU.mult, op1=ALU.mult)
                    ins.then_inc(job_read["D"], 1)
                    wait_read(dve, it)
                    t = TPB * tb + 2 * pr
                    dve.tensor_tensor(y_init[:, n % 2, :, :], y_init[:, n % 2, :, :], x_sb[:, t:t + 2, :],
                                      ALU.add).then_inc(y_set, 1)

            def keep_xT(i, r):
                e = i * RING + r
                dve.wait_ge(e_turned, e + 1)
                if not (isinstance(e, int) and e < 2):
                    dve.wait_ge(e_up, e - 1)
                dve.tensor_copy(xgT[r % 2][:, :, :], bank[6 + r % 2][:, :].rearrange("p (c t) -> p c t", c=DC))\
                   .then_inc(e_xT, 1)

            def hids(i, r):
                e = i * RING + r
                dve.wait_ge(e_sig, e + 1)
                if not (isinstance(e, int) and e < 2):
                    dve.wait_ge(e_down, e - 1)
                dve.tensor_tensor(hidA[r % 2][:, :], sigA[r % 2][:, :], bank[2 * (r % 2)][:, CAP:2 * CAP], ALU.mult)
                dve.tensor_tensor(hidB[r % 2][:, :], sigB[r % 2][:, :], bank[2 * (r % 2) + 1][64:64 + IB, 0:CAP],
                                  ALU.mult).then_inc(e_hid, 1)

            def gates(i, r):
                e = i * RING + r
                dve.wait_ge(e_gate0, e + 1)
                if not (isinstance(e, int) and e < 2):
                    dve.wait_ge(e_ob, e - 1)
                for s in range(SPE):
                    ins = dve.scalar_tensor_tensor(out=gate_w_sb[r % 2][:, s, :], in0=gb[:, 1, :], scalar=wt_st[r][:, 1, s:s + 1],
                                                   in1=gate_0[r % 2][:, s, :], op0=ALU.mult, op1=ALU.add)
                ins.then_inc(e_gate, 1)

            def weigh(i, r):
                e = i * RING + r
                dve.wait_ge(e_down, e + 1)
                dve.wait_ge(e_gate, e + 1)
                if not (isinstance(e, int) and e < 2):
                    dve.wait_ge(e_added, 16 * SPE * (e - 1))
                dve.tensor_copy(idx_add[r % 2][:, :], tab_ix[:, bass.ds(SPE * e, SPE)]).then_inc(add_ix, 1)
                dve.tensor_tensor(ob[r % 2][:, :, :], bank[4 + r % 2][:, :].rearrange("p (s d) -> p s d", s=SPE),
                                  gate_w_sb[r % 2][:, :, :], ALU.mult).then_inc(e_ob, 1)

            keep_xT(0, 0)

            def body(i, first=False, last=False):
                for r in range(RING):
                    if not (last and r == RING - 1):
                        keep_xT(i + (r + 1) // RING, (r + 1) % RING)
                    gates(i, r)
                    hids(i, r)
                    if not last:
                        stage(i + 1, r)
                    if not (first and r == 0):
                        weigh(i if r else i - 1, (r - 1) % RING)

            body(0, first=True)
            with dve.Fori(1, E // RING - 1) as i:
                body(i)
            body(E // RING - 1, last=True)
            weigh(E // RING - 1, RING - 1)

        @block.gpsimd
        def _(pool):
            chain = [0]

            def link(ins):
                chain[0] += 1
                ins.then_inc(pool_chain, 1)
                pool.wait_ge(pool_chain, chain[0])

            link(pool.memset(neg_half[:, :], -0.5))
            pool.memset(before[:, 0, :], 0.0)
            for v in v_aug:
                pool.memset(v[:, :, :, HD:VW], 1.0)
            pool.memset(zero_b[:, :], 0.0).then_inc(set_up, 1)
            for it in ITEMS:
                kind = it[0]
                if kind in ("stat", "ln2s"):
                    into, mvx = (rstd, mv) if kind == "stat" else (rstd2, mv2)
                    t = slice(TPB * it[1], TPB * (it[1] + 1))
                    pool.wait_ge(var_set, VAR[it] + 1)
                    link(pool.tensor_scalar(var_e[:, t], mvx[:, t, 1], 1.0, EPS, ALU.mult, ALU.add))
                    pool.tensor_tensor(into[:, t], var_e[:, t], neg_half[:, :], ALU.pow).then_inc(rstd_set, 1)
                elif kind == "ln2" and it[1] < NB - 1:
                    tb = it[1]
                    pool.wait_ge(x2hat_set, tb + 1)
                    h2b = lambda v: v[:, tb // 2:tb // 2 + 1, :].to_broadcast([P, TPB, D])
                    link(pool.tensor_tensor(h2[:, :, :], h2[:, :, :], h2b(cb1), ALU.mult))
                    pool.tensor_tensor(h2[:, :, :], h2[:, :, :], h2b(sb_row), ALU.add).then_inc(h2_set, 1)
                elif kind == "wog":
                    wait_read(pool, ("row", B - 1, 1))
                    pool.wait_ge(l_wvo, 32)
                    pool.wait_ge(l_rest, 16 * N_REST)
                    for b in range(B):
                        for c in range(DC):
                            pool.tensor_tensor(wo_g[:, b, c, :], wo_sb[:, c, :], ga[:, b, :], ALU.mult)
                        ins = pool.tensor_tensor(ga_bo[:, b, :], bo_row[:, :], ga[:, b, :], ALU.mult)
                    ins.then_inc(wo_scaled, 1)
                    pool.wait_ge(wo_scaled, 1)
                    pool.wait_ge(xhat_set, 2)
                    for i in range(TPB):
                        ins = pool.tensor_tensor(x_sb[:, i, :], x_sb[:, i, :], ga_bo[:, 0, :], ALU.add)
                    ins.then_inc(resid_set, 1)
                elif kind == "resid" and it[1]:
                    tb = it[1]
                    pool.wait_ge(xhat_set, 2 * (tb + 1))
                    for i in range(TPB):
                        t = TPB * tb + i
                        ins = pool.tensor_tensor(x_sb[:, t, :], x_sb[:, t, :], ga_bo[:, tb // 2, :], ALU.add)
                    ins.then_inc(resid_set, 1)
                elif kind == "rank":
                    tb = it[1]
                    pool.wait_ge(route_step, 5 * (tb + 1))
                    for i in range(TPB):
                        t = TPB * tb + i
                        ins = pool.tensor_tensor(before[:, t + 1, :], before[:, t, :], member[:, i, :], ALU.add)
                        if i < TPB - 1:
                            link(ins)
                    ins.then_inc(member_set, 1)
                elif kind == "pos":
                    tb = it[1]
                    pool.wait_ge(ranks_set, tb + 1)
                    pool.wait_ge(member_set, tb + 1)
                    link(pool.tensor_scalar(upper[:, :, :], posk[:, :, :], float(P), float(1 - P * SPT), ALU.is_ge, ALU.mult))
                    link(pool.tensor_scalar(addr[:, :, :], posk[:, :, :], float(SPT), None, ALU.mult))
                    link(pool.tensor_tensor(addr[:, :, :], addr[:, :, :], upper[:, :, :], ALU.add))
                    link(pool.tensor_scalar(upper[:, :, :], posk[:, :, :], float(CAP), float(2 * SLOTS), ALU.is_ge, ALU.mult))
                    link(pool.tensor_tensor(addr[:, :, :], addr[:, :, :], upper[:, :, :], ALU.add))
                    link(pool.tensor_scalar(upper[:, :, :], topf[:, :, 0:TOPK], float(SPE), None, ALU.mult))
                    link(pool.tensor_tensor(addr[:, :, :], upper[:, :, :], addr[:, :, :], ALU.add))
                    pool.tensor_copy(slot_ix[:, tb, :, :], addr[:, :, :])
                    pool.tensor_copy(payload[:, tb, :, :, 1], top[:, :, 0:TOPK])
                    pool.tensor_copy(payload[:, tb, :, :, 0],
                                     tok_id[:, TPB * tb:TPB * (tb + 1)].rearrange("p (t a) -> p t a", a=1)
                                     .to_broadcast([P, TPB, TOPK])).then_inc(slots_set, 1)
                    pool.wait_ge(slots_set, tb + 1)
                    pool.wait_ge(l_init, 48)
                    for i in range(TPB):
                        for k in range(TOPK):
                            pool.indirect_dma_start(
                                slot_table, bass.IndirectOffsetOnAxis(ap=slot_ix[:, tb, i, k:k + 1], axis=0),
                                payload[:, tb, i, k, :], None, bounds_check=SLOTS - 1, oob_is_err=False).then_inc(l_scat, 16)
                elif kind == "free":
                    wait_read(pool, ("ctx", NU - 1))
                    pool.wait_ge(exp_done, total["qk"])
                    for r in range(RING):
                        ins = pool.memset(w13_sb[r][:, 0:DC * W13].rearrange("p (c n) -> p c n", c=DC)[:, :, COL_B + IB:COL_B + 64], 0.0)
                    ins.then_inc(pads_set, 1)
            pool.wait_ge(tabix_set, 1)
            pool.wait_ge(l_h2, 16 * NB)

            def gather(i, r):
                e = i * RING + r
                pool.wait_ge(e_staged, e + 1)
                if not (isinstance(e, int) and e < RING):
                    pool.wait_ge(e_turned, e - RING + 1)
                pool.sem_inc(pool_at, 1)
                for s in range(SPE):
                    pool.indirect_dma_start(xg[r][:, s, :], None, h2_rows,
                                            bass.IndirectOffsetOnAxis(ap=idx_st[r][:, s:s + 1], axis=0)).then_inc(e_x[r], 16)

            def add(i, r):
                e = i * RING + r
                pool.wait_ge(e_ob, e + 1)
                if isinstance(e, int) and e < 1:
                    for k in range(2):
                        pool.wait_ge(l_y[k], 16 * total["sd"] // 2)
                else:
                    pool.wait_ge(e_added, 16 * SPE * e)
                pool.wait_ge(add_ix, e + 1)
                pool.sem_inc(pool_at, 1)
                for s in range(SPE):
                    pool.indirect_dma_start(out, bass.IndirectOffsetOnAxis(ap=idx_add[r % 2][:, s:s + 1], axis=0),
                                            ob[r % 2][:, s, :], None, compute_op=ALU.add).then_inc(e_added, 16)

            AHEAD = 3
            for r in range(AHEAD):
                gather(0, r)

            def body(i, first=False, last=False):
                for r in range(RING):
                    if not (last and r >= RING - AHEAD):
                        gather(i + (r + AHEAD) // RING, (r + AHEAD) % RING)
                    if not (first and r == 0):
                        add(i if r else i - 1, (r - 1) % RING)

            body(0, first=True)
            with pool.Fori(1, E // RING - 1) as i:
                body(i)
            body(E // RING - 1, last=True)
            add(E // RING - 1, RING - 1)


def constants():
    bf = np.dtype("bfloat16")
    slope = np.float32(2.0 ** (-8.0 / H)) ** np.arange(1, H + 1, dtype=np.float32)
    bias = slope[:, None] * np.arange(1 - S, 1, dtype=np.float32)[None, :]
    alibi = []
    for _ in range(3):
        alibi.append(bias.astype(bf))
        bias = bias - alibi[-1].astype(np.float32)
    q, k = np.arange(P)[:, None], np.arange(P)[None, :]
    masks = np.stack([np.where(k > q, NEG, 0.0), np.where(q > k, NEG, 0.0), (q == k) * 1.0]).astype(bf)
    tri = np.stack([(q < k) * 1.0, np.ones((P, P))], axis=1).astype(bf)
    slot = np.zeros((P, E, SPE, 2), np.float32)
    slot[..., 0] = T + np.arange(SPE)[None, None, :] * P + np.arange(P)[:, None, None]
    return {
        "alibi": np.stack(alibi).reshape(3, NG, HG, S // BLK, BLK).transpose(0, 1, 3, 2, 4),
        "ones_rows": np.ones((3, S // BLK, HG, BLK), bf), "zero_row": np.zeros((1, D), np.float32),
        "masks": masks, "ident": np.eye(P, dtype=np.float32)[None], "tri": tri,
        "iota": np.tile(np.arange(E, dtype=np.float32), (P, 1)),
        "tok": (np.arange(P)[:, None] + P * np.arange(NT)[None, :]).astype(np.float32),
        "slot_init": slot.reshape(SLOTS, 2),
    }


_INS = ["L0_attn_x", "L0_attn_Wq", "L0_attn_bq", "L0_attn_Wk", "L0_attn_bk", "L0_attn_Wv", "L0_attn_bv", "L0_attn_Wo",
        "L0_attn_bo", "L0_ffn_gate_w", "L0_ffn_w1", "L0_ffn_w2", "L0_ffn_w3", "L0_ffn_sw1", "L0_ffn_sw2", "L0_ffn_sw3",
        "L0_c", "L0_wmod"]


def kernel(**inputs):
    import numpy as _np
    import concourse.bacc as _bacc
    from concourse import mybir as _mybir
    from concourse.bass_utils import run_bass_kernel_spmd as _run

    nc = _bacc.Bacc("TRN2", target_bir_lowering=False, num_devices=1)
    arrays, args = {}, []
    data = {n: _np.asarray(inputs[n]) for n in _INS}
    data["L0_attn_x"] = data["L0_attn_x"].reshape(T, D)
    for n in ("Wq", "Wk", "bq", "bk"):
        a = data["L0_attn_" + n]
        data["L0_attn_" + n] = _np.swapaxes(a.reshape(a.shape[:-1] + (NG, HG, HD)), -1, -2).reshape(a.shape)
    for name, a in {**data, **constants()}.items():
        a = _np.ascontiguousarray(a)
        arrays[f"in_{name}"] = a
        args.append(nc.dram_tensor(f"in_{name}", a.shape, _mybir.dt.from_np(a.dtype), kind="ExternalInput").ap())
    args.append(nc.dram_tensor("out_0", (T + CAP, D), _mybir.dt.float32, kind="ExternalOutput").ap())
    adaln_kernel(nc, *args)
    r = _run(nc, [arrays], core_ids=[0])
    return r.results[0]["out_0"][0:T].reshape(B, S, D)
```
